# Optimizing a Trainium2 kernel written in Bass

```python
import numpy as np
import jax
import jax.numpy as jnp

def _softmax(x, axis=-1):
    return jax.nn.softmax(x, axis=axis)

def _gelu(x):
    return jax.nn.gelu(x, approximate=True)

def _silu(x):
    return jax.nn.silu(x)

def _sigmoid(x):
    return jax.nn.sigmoid(x)

def _layernorm(x, axis=-1, eps=1e-05):
    m = jnp.mean(x, axis=axis, keepdims=True)
    v = jnp.var(x, axis=axis, keepdims=True)
    return (x - m) / jnp.sqrt(v + eps)

def _scatter_add(tgt, idx, src, axis=0):
    return tgt.at[idx].add(src)

def _segment_sum(src, seg, n):
    return jax.ops.segment_sum(src, seg, n)
kernel_name = 'mk_adj_ffn_d2_adj_r2_d76bcb'

def setup_inputs(seed: int=0):
    np.random.seed(seed)
    _w = jnp.asarray

    def _rec_inputs():
        import jax
        import jax.numpy as jnp
        _gk = jax.random.key(seed)
        x = -8.776e-05 + 1 * jax.random.normal(jax.random.fold_in(_gk, 1), (4096, 128), jnp.float32)
        _w = (1.0 + jnp.arange(4096, dtype=jnp.float32)) ** (-0.5)
        _w = _w / _w.mean()
        _pij = jnp.clip(0.000976562 * _w[:, None] * _w[None, :], 0.0, 1.0)
        _a = jax.random.uniform(jax.random.fold_in(_gk, 2), (4096, 4096)) < _pij
        _a = jnp.logical_or(_a, jnp.eye(4096, dtype=bool))
        _af = _a.astype(jnp.float32)
        _af = _af * jax.random.uniform(jax.random.fold_in(_gk, 3), (4096, 4096), jnp.float32, 0.05, 1)
        adj = _af
        return (x, adj)
    x, adj = _rec_inputs()

    def _L0_gnn_setup():
        import jax, jax.numpy as jnp
        import numpy as np
        N = 10000
        D = 128
        F = 128
        K = F // 8
        key = jax.random.key(seed)
        k1, k2, k3, k4, k5 = jax.random.split(key, 5)
        h = jax.random.normal(k1, (N, D), dtype=jnp.float32)
        adj = jax.random.uniform(k2, (N, N), dtype=jnp.float32)
        W1 = jax.random.normal(k3, (D, K), dtype=jnp.float32) * 0.05
        W2 = jax.random.normal(k4, (K, D, F), dtype=jnp.float32) * 0.05
        b = jax.random.normal(k5, (K, F), dtype=jnp.float32) * 0.05
        return {'h': h, 'adj': adj, 'W1': W1, 'W2': W2, 'b': b}
    _L0_gnn_all = _L0_gnn_setup()
    _L0_gnn_in = {k: v for k, v in _L0_gnn_all.items() if k in ('W1', 'W2', 'b')}
    del _L0_gnn_all

    def _L0_ffn_setup():
        import jax, jax.numpy as jnp
        import numpy as np
        H, P, G, NS, K = (8, 64, 64, 64, 3)
        D_INNER = H * P
        CONV_DIM = D_INNER + 2 * NS
        D_IN_PROJ = 2 * D_INNER + 2 * NS + 2 * H

        def _hydra(u, in_w, conv_w, conv_b, dt_bias, A_log, Dp, fcD_w, norm_w, out_w):
            Bt, L, _ = u.shape
            zxbcdt = u @ in_w.T
            z = zxbcdt[..., :D_INNER]
            xBC = zxbcdt[..., D_INNER:D_INNER + CONV_DIM]
            dt = zxbcdt[..., -2 * H:]
            dt = jnp.concatenate([dt[..., :H], jnp.flip(dt[..., H:], axis=1)], axis=0)
            dt = jax.nn.softplus(dt + dt_bias)
            xp = jnp.pad(xBC, ((0, 0), (K - 1, 0), (0, 0)))
            xBC = sum((xp[:, k:k + L, :] * conv_w[:, k] for k in range(K))) + conv_b
            xBC = jax.nn.silu(xBC)
            x = xBC[..., :D_INNER]
            Bm = xBC[..., D_INNER:D_INNER + NS]
            Cm = xBC[..., D_INNER + NS:]
            x_og = x
            x2 = jnp.concatenate([x, jnp.flip(x, 1)], 0).reshape(2 * Bt, L, H, P)
            B2 = jnp.concatenate([Bm, jnp.flip(Bm, 1)], 0)
            C2 = jnp.concatenate([Cm, jnp.flip(Cm, 1)], 0)
            dA = jnp.exp(dt * -jnp.exp(A_log))
            dBx = jnp.einsum('blh,bln,blhp->blhpn', dt, B2, x2)

            def step(h, inp):
                dA_t, dBx_t, C_t = inp
                h = h * dA_t[:, :, None, None] + dBx_t
                return (h, jnp.einsum('bhpn,bn->bhp', h, C_t))
            h0 = jnp.zeros((2 * Bt, H, P, NS), u.dtype)
            _, ys = jax.lax.scan(step, h0, (dA.transpose(1, 0, 2), dBx.transpose(1, 0, 2, 3, 4), C2.transpose(1, 0, 2)))
            y = ys.transpose(1, 0, 2, 3).reshape(2 * Bt, L, D_INNER)
            y_fw, y_bw = (y[:Bt], jnp.flip(y[Bt:], 1))
            y = jnp.pad(y_fw[:, :-1], ((0, 0), (1, 0), (0, 0))) + jnp.pad(y_bw[:, 1:], ((0, 0), (0, 1), (0, 0)))
            y = y + x_og * jnp.repeat(x_og @ fcD_w.T + Dp, P, axis=-1)
            yg = y * jax.nn.silu(z)
            yg = yg * jax.lax.rsqrt(jnp.mean(jnp.square(yg), -1, keepdims=True) + 1e-05) * norm_w
            return yg @ out_w.T
        key = jax.random.key(seed)
        ks = jax.random.split(key, 10)
        dim, Bsz, N = (128, 4, 4096)
        s = 0.02
        return {'x': jax.random.normal(ks[0], (Bsz, N, dim), jnp.float32), 'W_fx': jax.random.normal(ks[1], (D_INNER, dim), jnp.float32) * s, 'b_fx': jnp.zeros((D_INNER,), jnp.float32), 'W_x': jax.random.normal(ks[2], (D_INNER, dim), jnp.float32) * s, 'b_x': jnp.zeros((D_INNER,), jnp.float32), 'W_slice': jax.random.normal(ks[3], (G, P), jnp.float32) * s, 'b_slice': jnp.zeros((G,), jnp.float32), 'temperature': jnp.full((1, H, 1, 1), 0.5, jnp.float32), 'hy_in_w': jax.random.normal(ks[4], (D_IN_PROJ, D_INNER), jnp.float32) * s, 'hy_conv_w': jax.random.normal(ks[5], (CONV_DIM, K), jnp.float32) * s, 'hy_conv_b': jnp.zeros((CONV_DIM,), jnp.float32), 'hy_dt_bias': jnp.log(jnp.expm1(jnp.full((H,), 0.01, jnp.float32))), 'hy_A_log': jnp.log(jnp.linspace(1.0, 16.0, H)).astype(jnp.float32), 'hy_D': jnp.ones((H,), jnp.float32), 'hy_fcD_w': jax.random.normal(ks[6], (H, D_INNER), jnp.float32) * s, 'hy_norm_w': jnp.ones((D_INNER,), jnp.float32), 'hy_out_w': jax.random.normal(ks[7], (D_INNER, D_INNER), jnp.float32) * s, 'out_w': jax.random.normal(ks[8], (dim, D_INNER), jnp.float32) * s, 'out_b': jnp.zeros((dim,), jnp.float32)}
    _L0_ffn_all = _L0_ffn_setup()
    _L0_ffn_in = {k: v for k, v in _L0_ffn_all.items() if k in ('W_fx', 'b_fx', 'W_x', 'b_x', 'W_slice', 'b_slice', 'temperature', 'hy_in_w', 'hy_conv_w', 'hy_conv_b', 'hy_dt_bias', 'hy_A_log', 'hy_D', 'hy_fcD_w', 'hy_norm_w', 'hy_out_w', 'out_w', 'out_b')}
    del _L0_ffn_all

    def _L1_gnn_setup():
        import jax, jax.numpy as jnp
        import numpy as np
        N = 4096
        D = 128
        L = 3

        def _cxin_conv(x, a, eps, W, b):
            ax = a @ x
            h = ax + (1.0 + eps[0]) * ax
            for i in range(L):
                h = jax.nn.relu(h @ W[i].T + b[i])
            return h
        key = jax.random.key(seed)
        ks = jax.random.split(key, 8)
        s = 1.0 / np.sqrt(D)
        return {'x1': jax.random.normal(ks[0], (N, D), jnp.float32), 'x2': jax.random.normal(ks[1], (N, D), jnp.float32), 'G1': jax.random.uniform(ks[2], (N, N), jnp.float32), 'G2': jax.random.uniform(ks[3], (N, N), jnp.float32), 'eps1': jnp.zeros((1,), jnp.float32), 'eps2': jnp.zeros((1,), jnp.float32), 'W1': jax.random.normal(ks[4], (L, D, D), jnp.float32) * s, 'b1': jnp.zeros((L, D), jnp.float32), 'W2': jax.random.normal(ks[5], (L, D, D), jnp.float32) * s, 'b2': jnp.zeros((L, D), jnp.float32), 'Wm': jax.random.normal(ks[6], (D, 2 * D), jnp.float32) * (1.0 / np.sqrt(2 * D)), 'bm': jnp.zeros((D,), jnp.float32)}
    _L1_gnn_all = _L1_gnn_setup()
    _L1_gnn_in = {k: v for k, v in _L1_gnn_all.items() if k in ('x2', 'eps1', 'eps2', 'W1', 'b1', 'W2', 'b2', 'Wm', 'bm')}
    del _L1_gnn_all

    def _L1_ffn_setup():
        import jax, jax.numpy as jnp
        import numpy as np
        TOP_K = 2
        LN_EPS = 1e-05
        key = jax.random.key(seed)
        ks = jax.random.split(key, 8)
        B, S, D, E, H = (16, 512, 128, 8, 512)
        x = jax.random.normal(ks[0], (B, S, D), dtype=jnp.float32)
        Wr = jax.random.normal(ks[1], (D, E), dtype=jnp.float32) * 0.1
        br = jnp.zeros((E,), dtype=jnp.float32)
        ln_g = jnp.ones((E, D), dtype=jnp.float32)
        ln_b = jnp.zeros((E, D), dtype=jnp.float32)
        W1 = jax.random.normal(ks[2], (E, D, H), dtype=jnp.float32) * (1.0 / np.sqrt(D))
        b1 = jnp.zeros((E, H), dtype=jnp.float32)
        W2 = jax.random.normal(ks[3], (E, H, D), dtype=jnp.float32) * (1.0 / np.sqrt(H))
        b2 = jnp.zeros((E, D), dtype=jnp.float32)
        return {'x': x, 'Wr': Wr, 'br': br, 'ln_g': ln_g, 'ln_b': ln_b, 'W1': W1, 'b1': b1, 'W2': W2, 'b2': b2}
    _L1_ffn_all = _L1_ffn_setup()
    _L1_ffn_in = {k: v for k, v in _L1_ffn_all.items() if k in ('Wr', 'br', 'ln_g', 'ln_b', 'W1', 'b1', 'W2', 'b2')}
    del _L1_ffn_all
    return {'x': x, 'adj': adj, 'L0_gnn_W1': _L0_gnn_in['W1'], 'L0_gnn_W2': _L0_gnn_in['W2'], 'L0_gnn_b': _L0_gnn_in['b'], 'L0_ffn_W_fx': _L0_ffn_in['W_fx'], 'L0_ffn_b_fx': _L0_ffn_in['b_fx'], 'L0_ffn_W_x': _L0_ffn_in['W_x'], 'L0_ffn_b_x': _L0_ffn_in['b_x'], 'L0_ffn_W_slice': _L0_ffn_in['W_slice'], 'L0_ffn_b_slice': _L0_ffn_in['b_slice'], 'L0_ffn_temperature': _L0_ffn_in['temperature'], 'L0_ffn_hy_in_w': _L0_ffn_in['hy_in_w'], 'L0_ffn_hy_conv_w': _L0_ffn_in['hy_conv_w'], 'L0_ffn_hy_conv_b': _L0_ffn_in['hy_conv_b'], 'L0_ffn_hy_dt_bias': _L0_ffn_in['hy_dt_bias'], 'L0_ffn_hy_A_log': _L0_ffn_in['hy_A_log'], 'L0_ffn_hy_D': _L0_ffn_in['hy_D'], 'L0_ffn_hy_fcD_w': _L0_ffn_in['hy_fcD_w'], 'L0_ffn_hy_norm_w': _L0_ffn_in['hy_norm_w'], 'L0_ffn_hy_out_w': _L0_ffn_in['hy_out_w'], 'L0_ffn_out_w': _L0_ffn_in['out_w'], 'L0_ffn_out_b': _L0_ffn_in['out_b'], 'L1_gnn_x2': _L1_gnn_in['x2'], 'L1_gnn_eps1': _L1_gnn_in['eps1'], 'L1_gnn_eps2': _L1_gnn_in['eps2'], 'L1_gnn_W1': _L1_gnn_in['W1'], 'L1_gnn_b1': _L1_gnn_in['b1'], 'L1_gnn_W2': _L1_gnn_in['W2'], 'L1_gnn_b2': _L1_gnn_in['b2'], 'L1_gnn_Wm': _L1_gnn_in['Wm'], 'L1_gnn_bm': _L1_gnn_in['bm'], 'L1_ffn_Wr': _L1_ffn_in['Wr'], 'L1_ffn_br': _L1_ffn_in['br'], 'L1_ffn_ln_g': _L1_ffn_in['ln_g'], 'L1_ffn_ln_b': _L1_ffn_in['ln_b'], 'L1_ffn_W1': _L1_ffn_in['W1'], 'L1_ffn_b1': _L1_ffn_in['b1'], 'L1_ffn_W2': _L1_ffn_in['W2'], 'L1_ffn_b2': _L1_ffn_in['b2']}

def reference(x, adj, L0_gnn_W1, L0_gnn_W2, L0_gnn_b, L0_ffn_W_fx, L0_ffn_b_fx, L0_ffn_W_x, L0_ffn_b_x, L0_ffn_W_slice, L0_ffn_b_slice, L0_ffn_temperature, L0_ffn_hy_in_w, L0_ffn_hy_conv_w, L0_ffn_hy_conv_b, L0_ffn_hy_dt_bias, L0_ffn_hy_A_log, L0_ffn_hy_D, L0_ffn_hy_fcD_w, L0_ffn_hy_norm_w, L0_ffn_hy_out_w, L0_ffn_out_w, L0_ffn_out_b, L1_gnn_x2, L1_gnn_eps1, L1_gnn_eps2, L1_gnn_W1, L1_gnn_b1, L1_gnn_W2, L1_gnn_b2, L1_gnn_Wm, L1_gnn_bm, L1_ffn_Wr, L1_ffn_br, L1_ffn_ln_g, L1_ffn_ln_b, L1_ffn_W1, L1_ffn_b1, L1_ffn_W2, L1_ffn_b2):
    import jax
    import jax.numpy as jnp

    def _L0_gnn_ref(h, adj, W1, W2, b):
        import jax, jax.numpy as jnp
        import numpy as np
        N = 10000
        D = 128
        F = 128
        K = F // 8
        node = h @ W1
        hw = jnp.einsum('nc,kcf->nkf', h, W2)
        x = jnp.einsum('nk,nkf->nf', node, hw)
        x = adj @ x
        x = x + node @ b
        return jax.nn.relu(x)

    def _L0_ffn_ref(x, W_fx, b_fx, W_x, b_x, W_slice, b_slice, temperature, hy_in_w, hy_conv_w, hy_conv_b, hy_dt_bias, hy_A_log, hy_D, hy_fcD_w, hy_norm_w, hy_out_w, out_w, out_b):
        import jax, jax.numpy as jnp
        import numpy as np
        H, P, G, NS, K = (8, 64, 64, 64, 3)
        D_INNER = H * P
        CONV_DIM = D_INNER + 2 * NS
        D_IN_PROJ = 2 * D_INNER + 2 * NS + 2 * H

        def _hydra(u, in_w, conv_w, conv_b, dt_bias, A_log, Dp, fcD_w, norm_w, out_w):
            Bt, L, _ = u.shape
            zxbcdt = u @ in_w.T
            z = zxbcdt[..., :D_INNER]
            xBC = zxbcdt[..., D_INNER:D_INNER + CONV_DIM]
            dt = zxbcdt[..., -2 * H:]
            dt = jnp.concatenate([dt[..., :H], jnp.flip(dt[..., H:], axis=1)], axis=0)
            dt = jax.nn.softplus(dt + dt_bias)
            xp = jnp.pad(xBC, ((0, 0), (K - 1, 0), (0, 0)))
            xBC = sum((xp[:, k:k + L, :] * conv_w[:, k] for k in range(K))) + conv_b
            xBC = jax.nn.silu(xBC)
            x = xBC[..., :D_INNER]
            Bm = xBC[..., D_INNER:D_INNER + NS]
            Cm = xBC[..., D_INNER + NS:]
            x_og = x
            x2 = jnp.concatenate([x, jnp.flip(x, 1)], 0).reshape(2 * Bt, L, H, P)
            B2 = jnp.concatenate([Bm, jnp.flip(Bm, 1)], 0)
            C2 = jnp.concatenate([Cm, jnp.flip(Cm, 1)], 0)
            dA = jnp.exp(dt * -jnp.exp(A_log))
            dBx = jnp.einsum('blh,bln,blhp->blhpn', dt, B2, x2)

            def step(h, inp):
                dA_t, dBx_t, C_t = inp
                h = h * dA_t[:, :, None, None] + dBx_t
                return (h, jnp.einsum('bhpn,bn->bhp', h, C_t))
            h0 = jnp.zeros((2 * Bt, H, P, NS), u.dtype)
            _, ys = jax.lax.scan(step, h0, (dA.transpose(1, 0, 2), dBx.transpose(1, 0, 2, 3, 4), C2.transpose(1, 0, 2)))
            y = ys.transpose(1, 0, 2, 3).reshape(2 * Bt, L, D_INNER)
            y_fw, y_bw = (y[:Bt], jnp.flip(y[Bt:], 1))
            y = jnp.pad(y_fw[:, :-1], ((0, 0), (1, 0), (0, 0))) + jnp.pad(y_bw[:, 1:], ((0, 0), (0, 1), (0, 0)))
            y = y + x_og * jnp.repeat(x_og @ fcD_w.T + Dp, P, axis=-1)
            yg = y * jax.nn.silu(z)
            yg = yg * jax.lax.rsqrt(jnp.mean(jnp.square(yg), -1, keepdims=True) + 1e-05) * norm_w
            return yg @ out_w.T
        B, N, _ = x.shape
        fx = (x @ W_fx.T + b_fx).reshape(B, N, H, P).transpose(0, 2, 1, 3)
        xm = (x @ W_x.T + b_x).reshape(B, N, H, P).transpose(0, 2, 1, 3)
        temp = jnp.maximum(temperature, 1e-06)
        sw = jax.nn.softmax((xm @ W_slice.T + b_slice) / temp, axis=-1)
        snorm = sw.sum(2)
        st = jnp.einsum('bhnc,bhng->bhgc', fx, sw) / (snorm + 1e-05)[..., None]
        st = st.transpose(0, 2, 1, 3).reshape(B, G, D_INNER)
        ot = _hydra(st, hy_in_w, hy_conv_w, hy_conv_b, hy_dt_bias, hy_A_log, hy_D, hy_fcD_w, hy_norm_w, hy_out_w)
        ot = ot.reshape(B, G, H, P).transpose(0, 2, 1, 3)
        out = jnp.einsum('bhgc,bhng->bhnc', ot, sw).transpose(0, 2, 1, 3).reshape(B, N, D_INNER)
        return out @ out_w.T + out_b

    def _L1_gnn_ref(x1, x2, G1, G2, eps1, eps2, W1, b1, W2, b2, Wm, bm):
        import jax, jax.numpy as jnp
        import numpy as np
        N = 4096
        D = 128
        L = 3

        def _cxin_conv(x, a, eps, W, b):
            ax = a @ x
            h = ax + (1.0 + eps[0]) * ax
            for i in range(L):
                h = jax.nn.relu(h @ W[i].T + b[i])
            return h
        out1 = _cxin_conv(x1, G1, eps1, W1, b1)
        out2 = _cxin_conv(x2, G2, eps2, W2, b2)
        merged = jnp.concatenate((out1, out2), axis=1)
        return merged @ Wm.T + bm

    def _L1_ffn_ref(x, Wr, br, ln_g, ln_b, W1, b1, W2, b2):
        import jax, jax.numpy as jnp
        import numpy as np
        TOP_K = 2
        LN_EPS = 1e-05
        B, S, D = x.shape
        N = B * S
        xt = x.reshape(N, D)
        logits = xt @ Wr + br
        probs = jax.nn.softmax(logits, axis=-1)
        top_p, top_idx = jax.lax.top_k(probs, TOP_K)
        weights = top_p / top_p.sum(axis=-1, keepdims=True)
        mu = xt.mean(axis=-1, keepdims=True)
        var = ((xt - mu) ** 2).mean(axis=-1, keepdims=True)
        xn = (xt - mu) * jax.lax.rsqrt(var + LN_EPS)
        xe = xn[None, :, :] * ln_g[:, None, :] + ln_b[:, None, :]
        h = jax.nn.gelu(jnp.einsum('end,edh->enh', xe, W1) + b1[:, None, :], approximate=False)
        y = jnp.einsum('enh,ehd->end', h, W2) + b2[:, None, :]
        y_tok = jnp.transpose(y, (1, 0, 2))
        sel = jnp.take_along_axis(y_tok, top_idx[:, :, None], axis=1)
        out = (weights[:, :, None] * sel).sum(axis=1)
        return out.reshape(B, S, D)
    x = x + _L0_gnn_ref(_layernorm(x, axis=-1), adj, L0_gnn_W1, L0_gnn_W2, L0_gnn_b)
    x = x + _L0_ffn_ref(_layernorm(x, axis=-1)[None], L0_ffn_W_fx, L0_ffn_b_fx, L0_ffn_W_x, L0_ffn_b_x, L0_ffn_W_slice, L0_ffn_b_slice, L0_ffn_temperature, L0_ffn_hy_in_w, L0_ffn_hy_conv_w, L0_ffn_hy_conv_b, L0_ffn_hy_dt_bias, L0_ffn_hy_A_log, L0_ffn_hy_D, L0_ffn_hy_fcD_w, L0_ffn_hy_norm_w, L0_ffn_hy_out_w, L0_ffn_out_w, L0_ffn_out_b)[0]
    x = x + _L1_gnn_ref(_layernorm(x, axis=-1), L1_gnn_x2, adj, adj, L1_gnn_eps1, L1_gnn_eps2, L1_gnn_W1, L1_gnn_b1, L1_gnn_W2, L1_gnn_b2, L1_gnn_Wm, L1_gnn_bm)
    x = x + _L1_ffn_ref(_layernorm(x, axis=-1)[None], L1_ffn_Wr, L1_ffn_br, L1_ffn_ln_g, L1_ffn_ln_b, L1_ffn_W1, L1_ffn_b1, L1_ffn_W2, L1_ffn_b2)[0]
    return x

_drawn_inputs = setup_inputs


def setup_inputs(seed=0):
    import zlib

    import numpy as np

    out = dict(_drawn_inputs(seed))
    spreads = {'L0_ffn_b_fx': (0.0, 0.1),
     'L0_ffn_b_x': (0.0, 0.8),
     'L0_ffn_b_slice': (0.0, 0.8),
     'L0_ffn_temperature': (0.5, 0.6),
     'L0_ffn_hy_conv_b': (0.0, 0.1),
     'L0_ffn_hy_dt_bias': (-4.600166320800781, 0.6),
     'L0_ffn_hy_D': (1.0, 0.6),
     'L0_ffn_hy_norm_w': (1.0, 0.6),
     'L0_ffn_out_b': (0.0, 0.1),
     'L1_gnn_b1': (0.0, 0.1),
     'L1_gnn_b2': (0.0, 0.1),
     'L1_gnn_bm': (0.0, 0.1),
     'L1_ffn_br': (0.0, 0.1),
     'L1_ffn_ln_g': (1.0, 0.2),
     'L1_ffn_ln_b': (0.0, 0.315),
     'L1_ffn_b1': (0.0, 0.306),
     'L1_ffn_b2': (0.0, 0.1)}
    factors = {'L0_ffn_W_x': 8.0,
     'L0_ffn_W_slice': 8.0,
     'L0_ffn_hy_conv_w': 8.0,
     'L0_ffn_hy_A_log': 64.0,
     'L0_ffn_hy_fcD_w': 26.508}
    for name, (base, spread) in spreads.items():
        noise = np.random.default_rng([zlib.crc32(name.encode()), seed]).standard_normal(out[name].shape)
        drawn = base * np.exp(spread * noise) if base else spread * noise
        out[name] = jnp.asarray(drawn.astype(out[name].dtype))
    for name, factor in factors.items():
        out[name] = (out[name] * factor).astype(out[name].dtype)
    return out
```

```python
import concourse.bass as bass
from concourse import mybir
from contextlib import ExitStack

F32 = mybir.dt.float32
F32R = mybir.dt.float32r
ALU = mybir.AluOpType
ACT = mybir.ActivationFunctionType
AX = mybir.AxisListType.X

P = 128
N = 4096
D = 128
BW = 512
NB = N // BW
NT = N // P
TB = BW // P
UJ = 2
NU = NT // UJ
UW = UJ * BW
RING = 4
LEAD = 3
KG = 16
HEADS, HP, G = 8, 64, 64
HG = HEADS * G
HB = HG // P
DI = HEADS * HP
NIN = 2 * DI + 2 * 64 + 2 * HEADS
E = 8
HID = 512
HC = HID // P
STEPS = E * HC
VBANKS = ((3, 4), (1, 7))
TW = D + 1
EPS = 1e-5
CW = P + 8 * 64 + 64 + P + 64


def build_network(nc, A, out_t, scratch_xn, scratch_w):
    ctx = ExitStack()
    with ctx:
        sems = {}

        def sem(name):
            if name not in sems:
                sems[name] = ctx.enter_context(nc.semaphore(name))
            return sems[name]

        T = {}

        def overlay(nbytes, *groups):
            for group in groups:
                with ExitStack() as st:
                    for name, shape, dt in group:
                        T[name] = st.enter_context(nc.sbuf_tensor("t_" + name, shape, dt))
            ctx.enter_context(nc.sbuf_tensor(f"region_{groups[0][0][0]}", [P, nbytes // 4], F32))

        overlay(65536,
                [("x_n", [P, NT, D], F32), ("w2h", [P, KG * D + KG], F32R), ("w2l", [P, KG * D + KG], F32R),
                 ("prod", [P, 2, 8, D], F32), ("acc", [P, 2, 2, D], F32), ("x0f", [P, TB, D], F32), ("h_n", [P, TB, D], F32), ("nmr", [P, TB], F32),
                 ("hth", [P, 2, BW], F32R), ("htl", [P, 2, BW], F32R), ("node", [P, 2, TB, KG], F32),
                 ("w1t", [KG, P], F32), ("gb", [KG, P], F32), ("wbf", [P, P], F32),
                 ("wbh", [P, P], F32R), ("wbl", [P, P], F32R)],
                [("sw_t", [P, HB, N], F32)],
                [("m1h", [P, E, HID], F32R), ("m1l", [P, E, HID], F32R),
                 ("m2h", [P, E, HC, D], F32R), ("m2l", [P, E, HC, D], F32R)])
        overlay(32768,
                [("x0h", [P, NT, D], F32R), ("x0l", [P, NT, D], F32R)],
                [("x2raw", [P, NT, D], F32), ("hsc", [P, 4096], F32)],
                [("xnh", [P, NT, D], F32R), ("xnl", [P, NT, D], F32R)],
                [("mxh", [P, N], F32R), ("mxl", [P, N], F32R)])
        overlay(32768,
                [("term_t", [P, N], F32), ("lg", [P, 4, HG], F32), ("xn_n", [P, TB, TW], F32),
                 ("xn_t", [P, BW], F32)],
                [("x2h", [P, NT, D], F32R), ("x2l", [P, NT, D], F32R)],
                [("wb", [P, 2, E, BW], F32)])
        overlay(49152,
                [("raw", [P, RING, UW], F32), ("ah", [P, RING, UW], F32R), ("al", [P, RING, UW], F32R)],
                [("w2raw", [P, KG * D + KG], F32), ("wx", [P, HB, D], F32), ("wslt", [P, G], F32),
                 ("bxc", [P, HB], F32), ("bxb", [P, HB, P], F32), ("bsl", [P, G], F32),
                 ("tempb", [P, HEADS], F32)],
                [("hin", [P, 4, NIN], F32), ("hout", [P, 4, DI], F32), ("wfxt", [P, DI], F32),
                 ("outwt", [P, 4, D], F32), ("fcdt", [P, 4, HEADS], F32), ("convw", [P, 6, 4], F32),
                 ("normw", [P, 4], F32), ("bfx", [1, DI], F32), ("hvec", [P, 3, HEADS], F32),
                 ("hcst", [P, CW - P], F32), ("slices_t", [P, DI], F32), ("st_t", [P, 4, P], F32)],
                [("gel", [P, 4, BW], F32), ("geh", [P, 4, BW], F32R), ("gelo", [P, 4, BW], F32R),
                 ("xnr", [P, BW], F32), ("wy", [P, 2, BW], F32), ("wtr", [E, 2, BW], F32),
                 ("total", [P, BW], F32)])
        overlay(16384, [("res", [P, N], F32)])
        overlay(12544,
                [("wc", [P, HG], F32), ("cb", [P, HG], F32), ("sums", [P, HB, TW], F32),
                 ("pre", [P, BW], F32)],
                [("g1", [P, BW], F32), ("g2", [P, BW], F32), ("mlp", [P, 8, D], F32),
                 ("m1raw", [P, HID], F32), ("m2raw", [P, HID], F32)])
        for name, shape in [("ident", [P, P]), ("stat", [P, TB, 6]), ("mv", [P, TB, 2]), ("ve", [P, TB]),
                            ("lnv", [P, TB]), ("r0", [P, TB]), ("r1", [P, TB]), ("r2", [P, TB]),
                            ("rs", [P, TB]), ("itemp", [P, HEADS]), ("smx", [P, 4, HEADS]),
                            ("sden", [P, 4, HEADS]), ("pause", [P, 1])]:
            T[name] = ctx.enter_context(nc.sbuf_tensor("t_" + name, shape, F32))
        overlay(1792,
                [("outb", [P, 1], F32), ("bmc", [P, 1], F32), ("gbias", [P, 6], F32), ("epsb", [P, 2], F32),
                 ("lngb", [P, 2, E], F32), ("b1c", [P, STEPS], F32), ("wr", [P, E], F32),
                 ("brb", [P, E], F32), ("low", [P, 64], F32), ("b2", [E, D], F32),
                 ("r3", [P, TB], F32), ("r4", [P, TB], F32), ("r5", [P, TB], F32), ("r6", [P, TB], F32),
                 ("r7", [P, TB], F32), ("r8", [P, TB], F32), ("rt", [P, TB, E], F32), ("rq", [P, TB], F32), ("rkg", [P, TB, E], F32), ("rke", [P, TB, E], F32)])
        (x_n, w2h, w2l, prod, acc, x0f, h_n, nmr, hth, htl, node, w1t, gb, wbf, wbh, wbl, sw_t, m1h, m1l, m2h, m2l,
         x0h, x0l, x2raw, hsc, xnh, xnl, mxh, mxl, term_t, lg, xn_n, xn_t, x2h, x2l, wb, raw, ah, al,
         w2raw, wx, wslt, bxc, bxb, bsl, tempb, hin, hout, wfxt, outwt, fcdt, convw, normw, bfx, hvec,
         hcst, slices_t, st_t, gel, geh, gelo, xnr, wy, wtr, total, res, wc, cb, sums, pre, g1, g2, mlp,
         m1raw, m2raw, ident, stat, mv, ve, lnv, r0, r1, r2, rs, itemp, smx, sden, pause, outb, bmc, gbias, epsb,
         lngb, b1c, wr, brb, low, b2, r3, r4, r5, r6, r7, r8, rt, rq, rkg, rke) = T.values()
        ps = ctx.enter_context(nc.psum_tensor("ps", [P, 8, 512], F32))

        at = [0]

        def hs(n):
            at[0] += n
            return hsc[:, at[0] - n:at[0]]

        hden, hrden, hrr = hs(4), hs(4), hs(4)
        tn = hs(512).rearrange("p (b d) -> p b d", b=4)
        rrow = hs(512)
        xp = hs(6 * 66).rearrange("p (b t) -> p b t", b=6)
        xc = hs(384).rearrange("p (b t) -> p b t", b=6)
        xe = hs(384).rearrange("p (b t) -> p b t", b=6)
        xtd = hs(512).rearrange("p (b t) -> p b t", b=4)
        bt = hs(128)
        ct = hs(64)
        dtu, dtn, dtl, dtv, dta, hea = hs(8), hs(8), hs(8), hs(8), hs(8), hs(8)
        fcs = hs(8)
        hss, hms, hln, hr0, hr1, hr2, hrs = (hs(1) for _ in range(7))
        decay = slices_t[:].rearrange("p (h t) -> p h t", h=HEADS)
        scan = tn.rearrange("p b d -> p (b d)").rearrange("p (h t) -> p h t", h=HEADS)
        mix = hs(512).rearrange("p (h t) -> p h t", h=HEADS)
        assert at[0] <= 4096
        hfree = hin[:].rearrange("p a b -> p (a b)")
        xdt = hfree[:, 0:512].rearrange("p (h c) -> p h c", h=HEADS)
        xo = hfree[:, 512:1024]
        zs = hfree[:, 1024:1536]
        yy = hfree[:, 1536:2048]
        ze = hfree[:, 2048:2560]
        ygt = hfree[:, 2560:2816].rearrange("p (b t) -> p b t", b=4)
        ott = hfree[:, 2816:3072].rearrange("p (b t) -> p b t", b=4)
        msl = pre
        rperm = hcst[:, 0:512]
        perm0 = hcst[:, 512:576]
        sameside = hcst[:, 576:576 + P]

        MIXER = ["den", "rden", "norm", "slices_ps", "slices", "st_ps", "st", "in_ps", "pad", "tap0", "tap1", "tap2",
                 "exp", "plus", "recip", "silu", "x_ps", "dt_neg", "dt_exp", "dt_plus", "dt_ln", "dt", "dt_a", "dt_a_min",
                 "keep", "spread", "keep_ps", "scan", "skip", "xdt", "y_ps", "y", "z_exp", "z_plus", "z_recip", "z_silu",
                 "gated_raw", "square", "ms", "ms_ln", "ms_guess", "ms_n1", "ms_n2", "ms_root", "gated", "gated_ps",
                 "ygt", "ot_ps", "ott", "msl_ps", "msl"]

        def mixer_after(eng, step):
            eng.wait_ge(sem("mixer"), MIXER.index(step) + 1)

        def mixer_done(ins):
            ins.then_inc(sem("mixer"), 1)

        block = ctx.enter_context(nc.Block())

        def lo_sem(u):
            return sem("rest_pool") if u % 4 == 3 else sem("rest_dve")

        def lo_val(blk, u):
            return 4 * blk + u // 4 + 1 if u % 4 == 3 else 12 * blk + 3 * (u // 4) + u % 4 + 1

        def before(blk, u, n):
            return (blk, u - n) if u >= n else (None if isinstance(blk, int) and blk == 0 else (blk - 1, u - n + NU))

        def after(blk, u, n):
            return (blk, u + n) if u + n < NU else (blk + 1, u + n - NU)

        def split_act(act, blk, u):
            s = u % RING
            act.wait_ge(sem(f"raw_in{s}"), 16 * (4 * blk + u // 4 + 1))
            prev = before(blk, u, RING)
            if prev:
                act.wait_ge(sem("unit_used"), NU * prev[0] + prev[1] + 1)
            nc.scalar.activation(ah[:, s, :], raw[:, s, :], ACT.Copy).then_inc(sem("rounded"), 1)

        def split_rest(eng, which, blk, u):
            if (u % 4 == 3) != (which is nc.gpsimd):
                return
            s = u % RING
            eng.wait_ge(sem("rounded"), NU * blk + u + 1)
            which.tensor_tensor(al[:, s, :], raw[:, s, :], ah[:, s, :].bitcast(F32), ALU.subtract).then_inc(lo_sem(u), 1)

        def load_unit(sp, blk, ib, u):
            s = u % RING
            prev = before(blk, u, RING)
            if prev:
                sp.wait_ge(lo_sem(prev[1]), lo_val(*prev))
            sp.dma_start(raw[:, s, :], A["adjt"][ib, u]).then_inc(sem(f"raw_in{s}"), 16)

        def mm3(o, wh, wl, mh, ml, start, stop):
            nc.tensor.matmul(o, wh, mh, start=start, stop=False)
            nc.tensor.matmul(o, wh, ml, start=False, stop=False)
            return nc.tensor.matmul(o, wl, mh, start=False, stop=stop)

        def transposes(src, bank, name):
            for q in range(TB):
                last = nc.tensor.transpose(ps[:, bank, q * P:(q + 1) * P], src[:, q * P:(q + 1) * P], ident[:])
            last.then_inc(sem(name), 1)

        def own(ins, tag):
            return ins.then_inc(sem(tag + "_own"), 1)

        def own_step(dve, k, tag, per, n):
            dve.wait_ge(sem(tag + "_own"), per * k + n)

        def ln_stats(dve, k, src, tag, per=5):
            for q in range(TB):
                last = nc.vector.bn_stats(stat[:, q, :], src(q))
            own(last, tag)
            own_step(dve, k, tag, per, 1)
            nc.vector.memset(pause[:], 0.0)
            for q in range(TB):
                last = nc.vector.bn_aggr(mv[:, q, :], stat[:, q, :])
            own(last, tag)
            own_step(dve, k, tag, per, 2)
            nc.vector.tensor_scalar(ve[:], mv[:, :, 1], EPS, None, ALU.add).then_inc(sem(tag + "_ve"), 1)

        def ln_guess(act, k, tag, v, first):
            act.wait_ge(sem(tag + "_ve"), k + 1)
            nc.scalar.activation(lnv[:], v, ACT.Ln).then_inc(sem(tag + "_ln"), 1)
            act.wait_ge(sem(tag + "_ln"), k + 1)
            nc.scalar.activation(first, lnv[:], ACT.Exp, scale=-0.5).then_inc(sem(tag + "_guess"), 1)

        def ln_newton(dve, k, tag, v, first, t1, t2, root, own_tag=None, per=5, n=3):
            o = own_tag or tag
            dve.wait_ge(sem(tag + "_guess"), k + 1)
            own(nc.vector.scalar_tensor_tensor(t1, first, -0.5, first, ALU.mult, ALU.mult), o)
            own_step(dve, k, o, per, n)
            own(nc.vector.tensor_tensor(t2, t1, v, ALU.mult), o)
            own_step(dve, k, o, per, n + 1)
            own(nc.vector.scalar_tensor_tensor(root, t2, 1.5, first, ALU.add, ALU.mult), o)
            own_step(dve, k, o, per, n + 2)

        def ln_apply(src, dst, root, name):
            for q in range(TB):
                last = nc.vector.tensor_scalar(dst(q), src(q), mv[:, q, 0:1], root[:, q:q + 1], ALU.subtract, ALU.mult)
            last.then_inc(sem(name), 1)

        @block.sync
        def _(sp):
            def load(dst, src, name):
                sp.dma_start(dst, src).then_inc(sem(name), 16)

            nodes = A["x"].rearrange("(t p) d -> p t d", p=P)
            load(x_n[:, 0:TB], nodes[:, 0:TB], "x_in0")
            load(ident[:], A["cst"][:, 0:P], "ident_in")
            load(w2raw[:], A["w2"], "w2_in")
            load(w1t[:], A["w1t"], "prep_in")
            load(gb[:], A["gb"], "prep_in")
            load(wx[:], A["wx"].rearrange("(b p) d -> p b d", p=P), "prep_in")
            load(wslt[:], A["wslt"], "prep_in")
            load(bxc[:], A["bx"], "prep_in")
            load(bsl[:], A["bslice"].partition_broadcast(P), "prep_in")
            load(tempb[:], A["temp"].partition_broadcast(P), "prep_in")
            load(x_n[:, TB:], nodes[:, TB:], "x_in")
            load(res[:], A["xt"], "xt_in")
            small = [(outb[:], A["outb"].rearrange("(p o) -> p o", o=1)), (bmc[:], A["bm"].rearrange("(p o) -> p o", o=1)),
                     (gbias[:, 0:3], A["gb1"]), (gbias[:, 3:6], A["gb2"]),
                     (epsb[:, 0:1], A["eps1"].partition_broadcast(P)), (epsb[:, 1:2], A["eps2"].partition_broadcast(P)),
                     (lngb[:, 0, :], A["lng"]), (lngb[:, 1, :], A["lnb"]),
                     (b1c[:], A["b1"]), (wr[:], A["wr"]), (brb[:], A["br"].partition_broadcast(P)),
                     (low[:], A["cst"][:, CW - 64:CW]), (b2[:], A["b2"])]
            for dst, src in small:
                load(dst, src, "small_in")
            sp.wait_ge(sem("prep_done"), 1)
            sp.wait_ge(sem("w2_split"), 1)
            for u in range(NU):
                load_unit(sp, 0, 0, u)
            with sp.Fori(1, NB) as ib:
                for u in range(NU):
                    load_unit(sp, ib, ib, u)
            sp.wait_ge(sem("unit_used"), NU * NB)
            for dst, src in [(wfxt[:], A["wfxt"]), (bfx[:], A["bfx"].rearrange("(o n) -> o n", o=1)),
                             (hin[:], A["hin"].rearrange("(b p) n -> p b n", p=P)),
                             (convw[:], A["convw"]), (hcst[:], A["cst"][:, P:CW]),
                             (hvec[:, 0, :], A["dtb"].partition_broadcast(P)),
                             (hvec[:, 1, :], A["alog"].partition_broadcast(P)),
                             (hvec[:, 2, :], A["hd"].partition_broadcast(P)),
                             (fcdt[:], A["fcdt"].rearrange("(b p) h -> p b h", p=P)),
                             (hout[:], A["hout"].rearrange("(b p) n -> p b n", p=P)),
                             (outwt[:], A["outwt"].rearrange("(b p) d -> p b d", p=P)),
                             (normw[:], A["normw"]),
                             (x2raw[:], A["x2"].rearrange("(t p) d -> p t d", p=P))]:
                load(dst, src, "mixer_in")
            mixer_after(sp, "msl")

            def second(blk, ib, begin=0):
                for u in range(begin, NU):
                    load_unit(sp, blk, ib, u)
                    if u == 5:
                        if not isinstance(ib, int) or ib > 0:
                            sp.wait_ge(sem("m1_rest"), ib)
                            sp.wait_ge(sem("m2_rest"), ib)
                            sp.wait_ge(sem("b1_used"), ib)
                        load(m1raw[:], A["m1"][ib], "m_in")
                        load(m2raw[:], A["m2"][ib], "m_in")

            for u in range(RING):
                load_unit(sp, NB, 0, u)
            sp.wait_ge(sem("out_ps"), NB)
            load(mlp[:], A["mlpw"], "mlp_in")
            second(NB, 0, RING)
            with sp.Fori(1, NB) as ib:
                second(ib + NB, ib)

            def load_block(b):
                if not isinstance(b, int) or b > 0:
                    sp.wait_ge(sem("wtr_in"), 16 * b)
                    sp.wait_ge(sem("wb_in"), 16 * b)
                    sp.wait_ge(sem("mx_rest"), b)
                sp.wait_ge(sem("xn_stored"), 16 * (b + 1))
                sp.wait_ge(sem("w_stored"), 16 * (b + 1))
                if not isinstance(b, int) or b > 1:
                    sp.wait_ge(sem("weighted"), E * (b - 1))
                    sp.wait_ge(sem("bias2_ps"), b - 1)
                load(xnr[:], scratch_xn[:, bass.ts(b, BW)], "xnr_in")
                load(wtr[:, b % 2, :], scratch_w[:, bass.ts(b, BW)], "wtr_in")
                load(wb[:, b % 2, :, :], scratch_w[:, bass.ts(b, BW)].partition_broadcast(P), "wb_in")

            def store_block(b):
                sp.wait_ge(sem("added"), (E - 1) * (b + 1))
                sp.dma_start(out_t[:, bass.ts(b, BW)], total[:]).then_inc(sem("out_done"), 16)

            sp.wait_ge(sem("unit_used"), 2 * NU * NB)
            load_block(0)
            load_block(1)
            store_block(0)
            with sp.Fori(2, NB) as b:
                load_block(b)
                store_block(b - 1)
            store_block(NB - 1)
            sp.wait_ge(sem("out_done"), 16 * NB)

        @block.tensor
        def _(pe):
            def fold():
                pe.wait_ge(sem("acc_ok"), TB)
                pe.wait_ge(sem("bias_cols"), 1)
                for h in range(HEADS):
                    o, b = HP * (h % 2), h // 2
                    nc.tensor.matmul(ps[:, VBANKS[0][h % 2], b * G:(b + 1) * G], wx[o:o + HP, b, :], wslt[o:o + HP, :],
                                     start=True, stop=True)
                for h in range(HEADS):
                    o, b = HP * (h % 2), h // 2
                    last = nc.tensor.matmul(ps[:, VBANKS[1][h % 2], b * G:(b + 1) * G], bxb[o:o + HP, b, :],
                                            wslt[o:o + HP, :], start=True, stop=True)
                last.then_inc(sem("fold_ps"), 1)

            def h_transposes(b):
                pe.wait_ge(sem("la_xn"), b + 1)
                transposes(h_n[:].rearrange("p a d -> p (a d)"), 0, "h_ps")

            def h_products(b, par, has_next):
                pe.wait_ge(sem("ht_rest"), b + 1)
                if not isinstance(b, int) or b > 0:
                    pe.wait_ge(sem("term_ok"), b)
                for q in range(TB):
                    hh, hl = hth[:, par, q * P:(q + 1) * P], htl[:, par, q * P:(q + 1) * P]
                    c = KG * D
                    last = mm3(ps[:, 0, q * KG:(q + 1) * KG], hh, hl, w2h[:, c:c + KG], w2l[:, c:c + KG], True, True)
                last.then_inc(sem("node_ps"), 1)
                mm3(ps[:, 2, :], wbh[:], wbl[:], hth[:, par, :], htl[:, par, :], True, True).then_inc(sem("term_ps"), 1)
                for q in range(TB):
                    hh, hl = hth[:, par, q * P:(q + 1) * P], htl[:, par, q * P:(q + 1) * P]
                    if not isinstance(b, int) or b > 0 or q > 1:
                        pe.wait_ge(sem("acc_ok"), TB * b + q - 1)
                    for kc in (0, 1):
                        last = mm3(ps[:, VBANKS[q % 2][kc], :], hh, hl, w2h[:, kc * 512:(kc + 1) * 512],
                                   w2l[:, kc * 512:(kc + 1) * 512], True, True)
                    last.then_inc(sem("hw_dve"), 1)
                    if not isinstance(b, int) or b > 0 or q > 0:
                        pe.wait_ge(sem("prod_ok"), TB * b + q)
                    for kc in (2, 3):
                        last = mm3(ps[:, 3 + kc, :], hh, hl, w2h[:, kc * 512:(kc + 1) * 512],
                                   w2l[:, kc * 512:(kc + 1) * 512], True, True)
                    last.then_inc(sem("hw_act"), 1)
                    if q == 2 and has_next:
                        h_transposes(b + 1)

            pe.wait_ge(sem("ident_in"), 16)
            h_transposes(0)
            pe.wait_ge(sem("prep_in"), 16 * 7)
            nc.tensor.matmul(ps[:, 5, 0:P], w1t[:], gb[:], start=True, stop=True).then_inc(sem("wb_ps"), 1)
            pe.wait_ge(sem("w2_split"), 1)
            pe.wait_ge(sem("wb_rest"), 1)
            h_products(0, 0, True)
            fold()
            pe.wait_ge(sem("prep_done"), 1)
            with pe.Fori(0, NB // 2 - 1) as i:
                h_products(2 * i + 1, 1, True)
                h_products(2 * i + 2, 0, True)
            h_products(NB - 1, 1, False)

            def post1(slot, b):
                if slot == 0:
                    pe.wait_ge(sem("x1_ok"), b + 1)
                    for q in range(TB):
                        last = nc.tensor.transpose(ps[:, 2, q * P:(q + 1) * P], xn_t[:, q * P:(q + 1) * P], ident[:])
                    last.then_inc(sem("x1n_ps"), 1)
                if slot == 3:
                    pe.wait_ge(sem("lb_xn"), b + 1)
                    for q in range(TB):
                        last = nc.tensor.transpose(ps[:, 2, q * P:(q + 1) * P], xn_n[:, q, 0:D], ident[:])
                    last.then_inc(sem("xnt_ps"), 1)
                if 4 <= slot < 8:
                    q = slot - 4
                    if q == 0:
                        pe.wait_ge(sem("xnt_ok"), b + 1)
                    if q >= 2:
                        pe.wait_ge(sem("lg_ok"), TB * b + q - 1)
                    nc.tensor.matmul(ps[:, 3 + q % 2, :], xn_t[:, q * P:(q + 1) * P], wc[:], start=True, stop=True)\
                        .then_inc(sem("lg_ps"), 1)
                if 11 <= slot < 15:
                    q = slot - 11
                    pe.wait_ge(sem("sw_ok"), TB * b + q + 1)
                    if q >= 1:
                        pe.wait_ge(sem("swt_ok"), TB * b + q)
                    for hb in range(HB):
                        last = nc.tensor.transpose(ps[:, 5, hb * P:(hb + 1) * P], lg[:, q, hb * P:(hb + 1) * P], ident[:])
                    last.then_inc(sem("swt_ps"), 1)
                    for hb in range(HB):
                        o = (hb % 2) * TW
                        last = nc.tensor.matmul(ps[:, 6 + hb // 2, o:o + TW], lg[:, q, hb * P:(hb + 1) * P], xn_n[:, q, :],
                                                start=(q == 0 and hb % 2 == 0), stop=(q == TB - 1), skip_group_check=True)
                    last.then_inc(sem("sums_ps"), 1)

            def pass1(ib, first):
                for u in range(NU):
                    s = u % RING
                    pe.wait_ge(lo_sem(u), lo_val(ib, u))
                    for j in range(UJ):
                        jt = u * UJ + j
                        last = mm3(ps[:, ib % 2, :], x0h[:, jt, :], x0l[:, jt, :], ah[:, s, j * BW:(j + 1) * BW],
                                   al[:, s, j * BW:(j + 1) * BW], jt == 0, jt == NT - 1)
                    last.then_inc(sem("unit_used"), 1)
                    if not first:
                        post1(u, ib - 1)

            pe.wait_ge(sem("x0_rest"), NT)
            pass1(0, True)
            with pe.Fori(1, NB) as ib:
                pass1(ib, False)
            for slot in range(NU):
                post1(slot, NB - 1)

            pe.wait_ge(sem("mixer_in"), 16 * 13)
            mixer_after(pe, "norm")
            for hb in range(HB):
                nc.tensor.transpose(ps[:, 2, hb * P:(hb + 1) * P], tn[:, hb, :], ident[:])
            for hb in range(HB):
                last = nc.tensor.matmul(ps[0:1, 3, hb * P:(hb + 1) * P], hrr[:, hb:hb + 1], ident[:], start=True, stop=True)
            mixer_done(last)
            mixer_after(pe, "slices")
            for h in range(HEADS):
                o = HP * (h % 2)
                dst = ps[o:o + HP, 0, (h // 2) * G:(h // 2 + 1) * G]
                nc.tensor.matmul(dst, wfxt[:, h * HP:(h + 1) * HP], slices_t[:, h * G:(h + 1) * G], start=True, stop=False)
                last = nc.tensor.matmul(dst, bfx[0:1, h * HP:(h + 1) * HP], rrow[0:1, h * G:(h + 1) * G],
                                        start=False, stop=True)
            mixer_done(last)
            mixer_after(pe, "st")
            for m in range(6):
                w, c = (P, DI + m * P) if m < 4 else (64, 2 * DI + (m - 4) * 64)
                for kb in range(4):
                    nc.tensor.matmul(ps[0:w, 2, m * 64:(m + 1) * 64], hin[:, kb, c:c + w], st_t[:, kb, 0:64],
                                     start=(kb == 0), stop=(kb == 3))
            for kb in range(4):
                nc.tensor.matmul(ps[:, 3, 0:16], st_t[:, kb, :], hin[:, kb, NIN - 16:NIN], start=(kb == 0), stop=(kb == 3))
            for kb in range(4):
                last = nc.tensor.matmul(ps[0:64, 4, :], st_t[:, kb, 0:64], hin[:, kb, 0:DI], start=(kb == 0), stop=(kb == 3))
            mixer_done(last)
            mixer_after(pe, "silu")
            for mb in range(4):
                nc.tensor.transpose(ps[:, 2, mb * P:(mb + 1) * P], xtd[:, mb, :], ident[:])
            nc.tensor.matmul(ps[:, 7, 0:64], bt[0:64, :], ct[0:64, :], start=True, stop=True)
            for mb in range(4):
                last = nc.tensor.matmul(ps[0:64, 0, 0:HEADS], xtd[:, mb, 0:64], fcdt[:, mb, :], start=(mb == 0), stop=(mb == 3))
            mixer_done(last)
            mixer_after(pe, "spread")
            mixer_done(nc.tensor.matmul(ps[:, 5, :], sameside, decay.rearrange("p h t -> p (h t)"), start=True, stop=True))
            mixer_after(pe, "xdt")
            for h in range(HEADS):
                last = nc.tensor.matmul(ps[0:64, 6, h * HP:(h + 1) * HP], mix[:, h, :], xdt[:, h, :], start=True, stop=True)
            mixer_done(last)
            mixer_after(pe, "gated")
            for b in range(4):
                last = nc.tensor.transpose(ps[:, 2, b * 64:(b + 1) * 64], yy[0:64, b * P:(b + 1) * P], ident[0:64, 0:64])
            mixer_done(last)
            mixer_after(pe, "ygt")
            for ob in range(4):
                for b in range(4):
                    last = nc.tensor.matmul(ps[:, 7, ob * 64:(ob + 1) * 64], hout[:, b, ob * P:(ob + 1) * P], ygt[:, b, :],
                                            start=(b == 0), stop=(b == 3))
            mixer_done(last)
            mixer_after(pe, "ott")
            for h in range(HEADS):
                o = HP * (h % 2)
                last = nc.tensor.matmul(ps[o:o + G, 3, (h // 2) * D:(h // 2 + 1) * D], ott[o:o + HP, h // 2, :],
                                        outwt[o:o + HP, h // 2, :], start=True, stop=True)
            mixer_done(last)
            mixer_after(pe, "msl")

            def deslice(b):
                if not isinstance(b, int) or b >= 2:
                    pe.wait_ge(sem("x2_ok"), b - 1)
                for hb in range(HB):
                    last = nc.tensor.matmul(ps[:, b % 2, :], msl[:, hb * D:(hb + 1) * D], sw_t[:, hb, bass.ts(b, BW)],
                                            start=(hb == 0), stop=(hb == HB - 1))
                last.then_inc(sem("out_ps"), 1)

            def x2_transposes(b):
                pe.wait_ge(sem("x2_ok"), b + 1)
                if not isinstance(b, int) or b > 0:
                    pe.wait_ge(sem("lc_xn"), b)
                for q in range(TB):
                    last = nc.tensor.transpose(ps[:, 2, q * P:(q + 1) * P], g1[:, q * P:(q + 1) * P], ident[:])
                last.then_inc(sem("x2n_ps"), 1)

            deslice(0)
            x2_transposes(0)
            deslice(1)
            with pe.Fori(1, NB - 1) as b:
                x2_transposes(b)
                deslice(b + 1)
            x2_transposes(NB - 1)

            def post2(slot, b):
                if 1 <= slot <= 3:
                    layer = slot - 1
                    pe.wait_ge(sem("g_ok"), 2 * (3 * b + layer) + 2)
                    nc.tensor.matmul(ps[:, 4, :], mlp[:, layer, :], g1[:], start=True, stop=True).then_inc(sem("mlp_ps"), 1)
                    nc.tensor.matmul(ps[:, 5, :], mlp[:, 3 + layer, :], g2[:], start=True, stop=True).then_inc(sem("mlp_ps"), 1)
                if slot == 4:
                    pe.wait_ge(sem("g_out"), 2 * b + 2)
                    pe.wait_ge(sem("b1_used"), b + 1)
                    nc.tensor.matmul(ps[:, 6, :], mlp[:, 6, :], g1[:], start=True, stop=False)
                    nc.tensor.matmul(ps[:, 6, :], mlp[:, 7, :], g2[:], start=False, stop=True).then_inc(sem("merge_ps"), 1)
                if slot == 5:
                    pe.wait_ge(sem("x3_ok"), b + 1)
                    for q in range(TB):
                        last = nc.tensor.transpose(ps[:, 7, q * P:(q + 1) * P], g2[:, q * P:(q + 1) * P], ident[:])
                    last.then_inc(sem("x3n_ps"), 1)
                if slot == 9:
                    pe.wait_ge(sem("ld_xn"), b + 1)
                    for q in range(TB):
                        last = nc.tensor.transpose(ps[:, 7, q * P:(q + 1) * P], g1[:, q * P:(q + 1) * P], ident[:])
                    last.then_inc(sem("x3t_ps"), 1)
                if slot == 11:
                    pe.wait_ge(sem("x3t_ok"), b + 1)
                    pe.wait_ge(sem("b1_used"), min(b + 2, NB) if isinstance(b, int) else b + 2)
                    for q in range(TB):
                        last = nc.tensor.matmul(ps[:, 6, q * E:(q + 1) * E], g2[:, q * P:(q + 1) * P], wr[:], start=True, stop=True)
                    last.then_inc(sem("router_ps"), 1)
                if slot == 14:
                    pe.wait_ge(sem("w_ok"), b + 1)
                    for q in range(TB):
                        last = nc.tensor.transpose(ps[0:E, 7, q * P:(q + 1) * P], rt[:, q, :], ident[:])
                    last.then_inc(sem("wt_ps"), 1)

            def expert_bias(e):
                pe.wait_ge(sem("m_in"), 32 * (e + 1))
                for hc in range(HC):
                    last = nc.tensor.matmul(ps[:, 6, 64 + hc:65 + hc], m1raw[:, hc * P:(hc + 1) * P],
                                            lngb[:, 1, bass.ts(e, 1)], start=True, stop=True)
                last.then_inc(sem("b1_ps"), 1)

            def pass2(blk, ib, first):
                for u in range(NU):
                    s = u % RING
                    pe.wait_ge(lo_sem(u), lo_val(blk, u))
                    for j in range(UJ):
                        jt = u * UJ + j
                        mh, ml = ah[:, s, j * BW:(j + 1) * BW], al[:, s, j * BW:(j + 1) * BW]
                        mm3(ps[:, ib % 2, :], x2h[:, jt, :], x2l[:, jt, :], mh, ml, jt == 0, jt == NT - 1)
                        last = mm3(ps[:, 2 + ib % 2, :], xnh[:, jt, :], xnl[:, jt, :], mh, ml, jt == 0, jt == NT - 1)
                    last.then_inc(sem("unit_used"), 1)
                    if not first:
                        post2(u, ib - 1)
                    if u == 7:
                        expert_bias(ib)

            pe.wait_ge(sem("mlp_in"), 16)
            pe.wait_ge(sem("xn_rest"), NB)
            pe.wait_ge(sem("x2_rest"), 1)
            pass2(NB, 0, True)
            with pe.Fori(1, NB) as ib:
                pass2(ib + NB, ib, False)
            for slot in range(NU):
                post2(slot, NB - 1)

            def up(b, k):
                e, hc = divmod(k, HC)
                if k >= 4 or not isinstance(b, int) or b > 0:
                    pe.wait_ge(sem("gelu_ok"), STEPS * b + k - 3)
                if k == 0:
                    pe.wait_ge(sem("mx_rest"), b + 1)
                cols = bass.ts(b, BW)
                w = slice(hc * P, (hc + 1) * P)
                mm3(ps[:, k % 4, :], m1h[:, e, w], m1l[:, e, w], mxh[:, cols], mxl[:, cols], True, True)\
                    .then_inc(sem("up_ps"), 1)

            def down(b, k):
                e, hc = divmod(k, HC)
                pe.wait_ge(sem("gelu_rest"), STEPS * b + k + 1)
                if hc == 0 and (not isinstance(b, int) or b > 0 or e >= 2):
                    pe.wait_ge(sem("weighted"), E * b + e - 1)
                mm3(ps[:, 4 + e % 2, :], m2h[:, e, hc, :], m2l[:, e, hc, :], geh[:, k % 4, :], gelo[:, k % 4, :],
                    hc == 0, hc == HC - 1).then_inc(sem("down_used"), 1)

            def experts(b, last_block):
                for k in range(STEPS):
                    if k + 3 < STEPS:
                        up(b, k + 3)
                    elif not last_block:
                        up(b + 1, k + 3 - STEPS)
                    if k == 1:
                        pe.wait_ge(sem("wtr_in"), 16 * (b + 1))
                        if not isinstance(b, int) or b > 0:
                            pe.wait_ge(sem("weighted"), E * (b - 1) + 1)
                        nc.tensor.matmul(ps[:, 6, :], b2[:], wtr[:, b % 2, :], start=True, stop=True).then_inc(sem("bias2_ps"), 1)
                    down(b, k)

            pe.wait_ge(sem("m1_rest"), E)
            pe.wait_ge(sem("m2_rest"), E)
            pe.wait_ge(sem("wt_ok"), NB)
            for k in range(3):
                up(0, k)
            experts(0, False)
            with pe.Fori(1, NB - 1) as b:
                experts(b, False)
            experts(NB - 1, True)

        @block.scalar
        def _(act):
            nc.scalar.preload_act_table_set("natural_log_exp_and_others")
            ln_guess(act, 0, "la", ve[:], r0[:])
            act.wait_ge(sem("la_shift"), 1)
            for q in range(TB):
                last = nc.scalar.activation(h_n[:, q, :], x_n[:, q, :], ACT.Identity, bias=nmr[:, q:q + 1], scale=rs[:, q:q + 1])
            last.then_inc(sem("la_xn"), 1)
            act.wait_ge(sem("w2_in"), 16)
            nc.scalar.activation(w2h[:], w2raw[:], ACT.Copy).then_inc(sem("w2_round"), 1)
            act.wait_ge(sem("wb_ok"), 1)
            nc.scalar.activation(wbh[:], wbf[:], ACT.Copy).then_inc(sem("wb_round"), 1)

            def h_norm(b):
                act.wait_ge(sem("la_shift"), b + 1)
                if not isinstance(b, int) or b > 0:
                    act.wait_ge(sem("h_ps"), b)
                for q in range(TB):
                    last = nc.scalar.activation(h_n[:, q, :], x_n[:, TB * b + q, :], ACT.Identity, bias=nmr[:, q:q + 1],
                                                scale=rs[:, q:q + 1])
                last.then_inc(sem("la_xn"), 1)

            def h_round(b, par):
                act.wait_ge(sem("h_ps"), b + 1)
                nc.scalar.activation(hth[:, par, :], ps[:, 0, :], ACT.Copy).then_inc(sem("ht_round"), 1)

            def x0_round(t, s):
                act.wait_ge(sem("x0_full"), t + 1)
                nc.scalar.activation(x0h[:, t, :], x0f[:, s, :], ACT.Copy).then_inc(sem("x0_round"), 1)

            def basis(b, par, has_next):
                act.wait_ge(sem("node_ok"), b + 1)
                for q in range(TB):
                    act.wait_ge(sem("hw_act"), TB * b + q + 1)
                    if not isinstance(b, int) or b > 0 or q >= 2:
                        act.wait_ge(sem("x0_full"), TB * b + q - 1)
                    for i in range(8):
                        k = 8 + i
                        last = nc.scalar.activation(prod[:, q % 2, i, :], ps[:, 5 + i // 4, (i % 4) * D:(i % 4 + 1) * D],
                                                    ACT.Copy, scale=node[:, par, q, k:k + 1])
                    last.then_inc(sem("prod_ok"), 1)
                    if not isinstance(b, int) or b > 0 or q >= 2:
                        x0_round(TB * b + q - 2, (q - 2) % TB)
                    if q == 0:
                        if has_next:
                            ln_guess(act, b + 1, "la", ve[:], r0[:])
                        act.wait_ge(sem("term_ps"), b + 1)
                        nc.scalar.activation(term_t[:, bass.ts(b, BW)], ps[:, 2, :], ACT.Copy).then_inc(sem("term_ok"), 1)
                    if q == 1 and has_next:
                        h_norm(b + 1)
                    if q == 2 and has_next:
                        h_round(b + 1, 1 - par)

            h_round(0, 0)
            basis(0, 0, True)
            with act.Fori(0, NB // 2 - 1) as i:
                basis(2 * i + 1, 1, True)
                basis(2 * i + 2, 0, True)
            basis(NB - 1, 1, False)
            x0_round(NT - 2, 2)
            x0_round(NT - 1, 3)

            def post1(slot, b):
                if slot == 1:
                    act.wait_ge(sem("x1_ok"), b + 1)
                    nc.scalar.activation(res[:, bass.ts(b, BW)], xn_t[:], ACT.Copy).then_inc(sem("res1_ok"), 1)
                if slot == 1:
                    ln_guess(act, b, "lb", ve[:], r0[:])
                if slot == 4:
                    act.wait_ge(sem("xnt_ps"), b + 1)
                    act.wait_ge(sem("res1_ok"), b + 1)
                    nc.scalar.activation(xn_t[:], ps[:, 2, :], ACT.Copy).then_inc(sem("xnt_ok"), 1)
                if 7 <= slot < 11:
                    q = slot - 7
                    act.wait_ge(sem("lg_sub"), TB * b + q + 1)
                    nc.scalar.activation(lg[:, q, :], lg[:, q, :], ACT.Exp).then_inc(sem("lg_exp"), 1)
                if 12 <= slot < 16:
                    q = slot - 12
                    act.wait_ge(sem("swt_ps"), TB * b + q + 1)
                    nc.scalar.activation(sw_t[:, :, bass.ts(b * TB + q, P)],
                                         ps[:, 5, :].rearrange("p (h n) -> p h n", h=HB), ACT.Copy).then_inc(sem("swt_ok"), 1)

            def pass1(ib, first, last):
                for u in range(NU):
                    nxt = after(ib, u, LEAD)
                    if u + LEAD < NU or not last:
                        split_act(act, *nxt)
                    if not first:
                        post1(u, ib - 1)

            for u in range(LEAD):
                split_act(act, 0, u)
            pass1(0, True, False)
            with act.Fori(1, NB - 1) as ib:
                pass1(ib, False, False)
            pass1(NB - 1, False, True)
            for slot in range(NU):
                post1(slot, NB - 1)

            act.wait_ge(sem("alog_min"), 1)
            nc.scalar.activation(hea, hvec[:, 1, :], ACT.Exp).then_inc(sem("alog_exp"), 1)
            mixer_after(act, "tap2")
            nc.scalar.activation(xe[:, 0:4, :], xc[:, 0:4, :], ACT.Exp, scale=-1.0)
            mixer_done(nc.scalar.activation(xe[0:64, 4:6, :], xc[0:64, 4:6, :], ACT.Exp, scale=-1.0))
            mixer_after(act, "dt_neg")
            mixer_done(nc.scalar.activation(dtn, dtn, ACT.Exp, scale=-1.0))
            mixer_after(act, "dt_plus")
            mixer_done(nc.scalar.activation(dtl, dtn, ACT.Ln))
            mixer_after(act, "dt_a_min")
            mixer_done(nc.scalar.activation(dta, dta, ACT.Exp, scale=-1.0))
            mixer_after(act, "y")
            mixer_done(nc.scalar.activation(ze[0:64, :], ps[0:64, 4, :], ACT.Exp, scale=-1.0))
            mixer_after(act, "gated_raw")
            mixer_done(nc.scalar.activation(ze[0:64, :], yy[0:64, :], ACT.Square, accum_out=hss[0:64, :]))
            mixer_after(act, "ms")
            mixer_done(nc.scalar.activation(hln[0:64, :], hms[0:64, :], ACT.Ln))
            mixer_after(act, "ms_ln")
            mixer_done(nc.scalar.activation(hr0[0:64, :], hln[0:64, :], ACT.Exp, scale=-0.5))
            act.wait_ge(sem("sums_ok"), NB)
            nc.scalar.activation(x2h[:], x2raw[:], ACT.Copy).then_inc(sem("x2_round"), 1)

            def norm2(b):
                ln_guess(act, b, "lc", ve[:], r0[:])
                act.wait_ge(sem("lc_xn"), b + 1)
                nc.scalar.activation(xnh[:, bass.ts(b, TB), :], g2[:].rearrange("p (t d) -> p t d", t=TB), ACT.Copy)\
                    .then_inc(sem("xn_round"), 1)

            act.wait_ge(sem("x2_rest"), 1)
            norm2(0)
            with act.Fori(1, NB) as b:
                norm2(b)

            def post2(slot, b):
                if slot == 0:
                    act.wait_ge(sem("unit_used"), NU * NB + NU * (b + 1))
                    if not isinstance(b, int) or b > 0:
                        act.wait_ge(sem("xn_stored"), 16 * b)
                        act.wait_ge(sem("w_stored"), 16 * b)
                    nc.scalar.activation(g1[:], ps[:, 2 + b % 2, :], ACT.Copy, scale=epsb[:, 0:1]).then_inc(sem("g_ok"), 1)
                    nc.scalar.activation(g2[:], ps[:, b % 2, :], ACT.Copy, scale=epsb[:, 1:2]).then_inc(sem("g_ok"), 1)
                if 1 <= slot <= 3:
                    i = slot - 1
                    name = "g_out" if i == 2 else "g_ok"
                    act.wait_ge(sem("mlp_ps"), 6 * b + 2 * i + 1)
                    nc.scalar.activation(g1[:], ps[:, 4, :], ACT.Relu, bias=gbias[:, i:i + 1]).then_inc(sem(name), 1)
                    act.wait_ge(sem("mlp_ps"), 6 * b + 2 * i + 2)
                    nc.scalar.activation(g2[:], ps[:, 5, :], ACT.Relu, bias=gbias[:, 3 + i:4 + i]).then_inc(sem(name), 1)
                if slot == 6:
                    ln_guess(act, b, "ld", ve[:], r0[:])
                if slot == 7:
                    ln_guess(act, b, "le", r4[:], r5[:])
                if slot == 10:
                    act.wait_ge(sem("x3t_ps"), b + 1)
                    act.wait_ge(sem("res3_ok"), b + 1)
                    nc.scalar.activation(g2[:], ps[:, 7, :], ACT.Copy).then_inc(sem("x3t_ok"), 1)
                    act.wait_ge(sem("x3t_ok"), b + 1)
                    act.dma_start(scratch_xn[:, bass.ts(b, BW)], g2[:]).then_inc(sem("xn_stored"), 16)
                if slot == 12:
                    act.wait_ge(sem("router_sub"), b + 1)
                    nc.scalar.activation(rt[:], rt[:], ACT.Exp).then_inc(sem("router_exp"), 1)
                if slot == 15:
                    act.wait_ge(sem("wt_ok"), b + 1)
                    act.dma_start(scratch_w[:, bass.ts(b, BW)], g1[0:E, :]).then_inc(sem("w_stored"), 16)

            def pass2(blk, ib, first, last):
                for u in range(NU):
                    nxt = after(blk, u, LEAD)
                    if u + LEAD < NU or not last:
                        split_act(act, *nxt)
                    if not first:
                        post2(u, ib - 1)
                    if u == 8:
                        act.wait_ge(sem("m_in"), 32 * (ib + 1))
                        nc.scalar.activation(m2h[:, ib, :, :], m2raw[:].rearrange("p (c d) -> p c d", c=HC), ACT.Copy)\
                            .then_inc(sem("m2_round"), 1)

            act.wait_ge(sem("out_ps"), NB)
            act.wait_ge(sem("small_in"), 16 * 13)
            act.wait_ge(sem("eps_ok"), 1)
            for u in range(LEAD):
                split_act(act, NB, u)
            pass2(NB, 0, True, False)
            with act.Fori(1, NB - 1) as ib:
                pass2(ib + NB, ib, False, False)
            pass2(2 * NB - 1, NB - 1, False, True)
            for slot in range(NU):
                post2(slot, NB - 1)

            def mx_round(b):
                act.wait_ge(sem("xnr_in"), 16 * (b + 1))
                nc.scalar.activation(mxh[:, bass.ts(b, BW)], xnr[:], ACT.Copy).then_inc(sem("mx_round"), 1)

            def gelu(b, k):
                act.wait_ge(sem("up_ps"), STEPS * b + k + 1)
                if k >= 4 or not isinstance(b, int) or b > 0:
                    act.wait_ge(sem("gelu_rest"), STEPS * b + k - 3)
                nc.scalar.activation(gel[:, k % 4, :], ps[:, k % 4, :], ACT.Gelu, bias=b1c[:, k:k + 1]).then_inc(sem("gelu_ok"), 1)

            def experts(b, last_block):
                for k in range(STEPS):
                    if k + 2 < STEPS:
                        gelu(b, k + 2)
                    elif not last_block:
                        gelu(b + 1, k + 2 - STEPS)
                    if k == 16 and not last_block:
                        mx_round(b + 1)

            act.wait_ge(sem("unit_used"), 2 * NU * NB)
            act.wait_ge(sem("b1_used"), E)
            mx_round(0)
            gelu(0, 0)
            gelu(0, 1)
            experts(0, False)
            with act.Fori(1, NB - 1) as b:
                experts(b, False)
            experts(NB - 1, True)

        @block.vector
        def _(dve):
            nc.vector.memset(sums[:], 0.0).then_inc(sem("sums_ok0"), 1)
            nc.vector.memset(xn_n[:, :, D:TW], 1.0).then_inc(sem("ones_ok"), 1)

            def la_norm(b, part):
                if part == 0:
                    ln_stats(dve, b, lambda q: x_n[:, b * TB + q, :], "la")
                else:
                    ln_newton(dve, b, "la", ve[:], r0[:], r1[:], r2[:], rs[:])
                    nc.vector.scalar_tensor_tensor(nmr[:], mv[:, :, 0], -1.0, rs[:], ALU.mult, ALU.mult).then_inc(sem("la_shift"), 1)

            dve.wait_ge(sem("x_in0"), 16)
            la_norm(0, 0)
            la_norm(0, 1)
            dve.wait_ge(sem("w2_round"), 1)
            nc.vector.tensor_tensor(w2l[:], w2raw[:], w2h[:].bitcast(F32), ALU.subtract).then_inc(sem("w2_split"), 1)
            dve.wait_ge(sem("wb_ps"), 1)
            nc.vector.tensor_copy(wbf[:], ps[:, 5, 0:P]).then_inc(sem("wb_ok"), 1)
            dve.wait_ge(sem("wb_round"), 1)
            nc.vector.tensor_tensor(wbl[:], wbf[:], wbh[:].bitcast(F32), ALU.subtract).then_inc(sem("wb_rest"), 1)

            def heads(ap):
                return ap.rearrange("p (h g) -> p h g", h=HEADS)

            def fold():
                dve.wait_ge(sem("fold_ps"), 1)
                for r in range(2):
                    def every2(ap):
                        return ap.rearrange("p (i r g) -> p i r g", r=2, g=G)[:, :, r, :]

                    def bank(pair):
                        return ps[:, pair[r], 0:4 * G].rearrange("p (i g) -> p i g", g=G)

                    nc.vector.tensor_tensor(every2(wc[:]), bank(VBANKS[0]), itemp[:, r::2].unsqueeze(2).to_broadcast([P, 4, G]), ALU.mult)
                    nc.vector.tensor_tensor(every2(cb[:]), bank(VBANKS[1]), bsl[:].unsqueeze(1).to_broadcast([P, 4, G]),
                                            ALU.add).then_inc(sem("cb_sum"), 1)
                dve.wait_ge(sem("cb_sum"), 2)
                nc.vector.tensor_tensor(heads(cb[:]), heads(cb[:]), itemp[:].unsqueeze(2).to_broadcast([P, HEADS, G]), ALU.mult)\
                    .then_inc(sem("prep_done"), 1)

            def h_rest(b, par):
                dve.wait_ge(sem("ht_round"), b + 1)
                nc.vector.tensor_tensor(htl[:, par, :], ps[:, 0, :], hth[:, par, :].bitcast(F32), ALU.subtract)\
                    .then_inc(sem("ht_rest"), 1)

            def x0_full(t, s):
                dve.wait_ge(sem("acc_sum"), t + 1)
                dve.wait_ge(sem("tree3"), t + 1)
                if not isinstance(t, int) or t > 3:
                    dve.wait_ge(sem("x0_rest"), t - 3)
                nc.vector.tensor_tensor(x0f[:, s, :], acc[:, s % 2, 0, :], prod[:, s % 2, 0, :], ALU.add).then_inc(sem("x0_full"), 1)

            def x0_rest(t, s):
                dve.wait_ge(sem("x0_round"), t + 1)
                nc.vector.tensor_tensor(x0l[:, t, :], x0f[:, s, :], x0h[:, t, :].bitcast(F32), ALU.subtract).then_inc(sem("x0_rest"), 1)

            def basis(b, par, has_next):
                dve.wait_ge(sem("node_ps"), b + 1)
                nc.vector.tensor_copy(node[:, par].rearrange("p q k -> p (q k)"), ps[:, 0, 0:TB * KG]).then_inc(sem("node_ok"), 1)
                dve.wait_ge(sem("node_ok"), b + 1)
                for q in range(TB):
                    t = TB * b + q
                    if q == 3 and has_next:
                        h_rest(b + 1, 1 - par)
                    if not isinstance(b, int) or b > 0 or q > 1:
                        dve.wait_ge(sem("x0_full"), t - 1)
                    dve.wait_ge(sem("hw_dve"), t + 1)
                    for i in range(4):
                        for c in range(2):
                            k, src, a = 4 * c + i, ps[:, VBANKS[q % 2][c], i * D:(i + 1) * D], acc[:, q % 2, c, :]
                            if i == 0:
                                ins = nc.vector.tensor_scalar(a, src, node[:, par, q, k:k + 1], None, ALU.mult)
                            else:
                                dve.wait_ge(sem(f"chain{c}"), 3 * t + i)
                                ins = nc.vector.scalar_tensor_tensor(a, src, node[:, par, q, k:k + 1], a, ALU.mult, ALU.add)
                            if i < 3:
                                ins.then_inc(sem(f"chain{c}"), 1)
                    ins.then_inc(sem("acc_ok"), 1)
                    if not isinstance(b, int) or b > 0 or q > 2:
                        x0_rest(t - 3, (q - 3) % TB)
                    if not isinstance(b, int) or b > 0 or q > 0:
                        x0_full(t - 1, (q - 1) % TB)
                    if q == 0 and has_next:
                        la_norm(b + 1, 0)
                    if q == 1 and has_next:
                        la_norm(b + 1, 1)

            h_rest(0, 0)
            dve.wait_ge(sem("prep_in"), 16 * 7)
            nc.vector.tensor_copy(bxb[:], bxc[:].unsqueeze(2).to_broadcast([P, HB, P])).then_inc(sem("bias_cols"), 1)
            nc.vector.tensor_scalar(itemp[:], tempb[:], 1e-6, None, ALU.max).then_inc(sem("temp_max"), 1)
            dve.wait_ge(sem("temp_max"), 1)
            nc.vector.reciprocal(itemp[:], itemp[:]).then_inc(sem("itemp"), 1)
            dve.wait_ge(sem("itemp"), 1)
            dve.wait_ge(sem("x_in"), 16)
            basis(0, 0, True)
            fold()
            with dve.Fori(0, NB // 2 - 1) as i:
                basis(2 * i + 1, 1, True)
                basis(2 * i + 2, 0, True)
            basis(NB - 1, 1, False)
            x0_full(NT - 1, 3)
            for t in range(NT - 3, NT):
                x0_rest(t, t % TB)

            def hg(ap):
                return ap.rearrange("p (h g) -> p h g", h=HEADS)

            def post1(slot, b):
                if slot == 0:
                    dve.wait_ge(sem("unit_used"), NU * (b + 1))
                    nc.vector.tensor_tensor(pre[:], ps[:, b % 2, :], term_t[:, bass.ts(b, BW)], ALU.add).then_inc(sem("pre_ok"), 1)
                    dve.wait_ge(sem("pre_ok"), b + 1)
                    nc.vector.scalar_tensor_tensor(xn_t[:], pre[:], 0.0, res[:, bass.ts(b, BW)], ALU.max, ALU.add)\
                        .then_inc(sem("x1_ok"), 1)
                if slot == 1:
                    dve.wait_ge(sem("x1n_ps"), b + 1)
                    ln_stats(dve, b, lambda q: ps[:, 2, q * P:(q + 1) * P], "lb")
                if slot == 2:
                    ln_newton(dve, b, "lb", ve[:], r0[:], r1[:], r2[:], rs[:])
                    ln_apply(lambda q: ps[:, 2, q * P:(q + 1) * P], lambda q: xn_n[:, q, 0:D], rs, "lb_xn")
                if 5 <= slot < 9:
                    q = slot - 5
                    dve.wait_ge(sem("lg_ps"), TB * b + q + 1)
                    nc.vector.tensor_tensor(lg[:, q, :], ps[:, 3 + q % 2, :], cb[:], ALU.add).then_inc(sem("lg_ok"), 1)
                    dve.wait_ge(sem("lg_ok"), TB * b + q + 1)
                    nc.vector.tensor_reduce(smx[:, q, :], hg(lg[:, q, :]), AX, ALU.max).then_inc(sem("lg_max"), 1)
                if 8 <= slot < 12:
                    q = slot - 8
                    dve.wait_ge(sem("lg_exp"), TB * b + q + 1)
                    nc.vector.tensor_reduce(sden[:, q, :], hg(lg[:, q, :]), AX, ALU.add).then_inc(sem("lg_sum"), 1)
                    dve.wait_ge(sem("lg_sum"), TB * b + q + 1)
                    nc.vector.reciprocal(sden[:, q, :], sden[:, q, :]).then_inc(sem("lg_rec"), 1)
                if slot == 15:
                    dve.wait_ge(sem("sums_ps"), TB * (b + 1))
                    for c in range(2):
                        part = sums[:, 2 * c:2 * c + 2, :].rearrange("p a d -> p (a d)")
                        last = nc.vector.tensor_tensor(part, ps[:, 6 + c, 0:2 * TW], part, ALU.add)
                    last.then_inc(sem("sums_ok"), 1)

            def pass1(ib, first, last):
                for u in range(NU):
                    nxt = after(ib, u, LEAD)
                    if u in (0, 2) and not first:
                        post1(u, ib - 1)
                    if u + LEAD < NU or not last:
                        split_rest(dve, nc.vector, *nxt)
                    if u not in (0, 2) and not first:
                        post1(u, ib - 1)

            dve.wait_ge(sem("xt_in"), 16)
            for u in range(LEAD):
                split_rest(dve, nc.vector, 0, u)
            pass1(0, True, False)
            with dve.Fori(1, NB - 1) as ib:
                pass1(ib, False, False)
            pass1(NB - 1, False, True)
            for slot in range(NU):
                post1(slot, NB - 1)

            dve.wait_ge(sem("sums_ok"), NB)
            dve.wait_ge(sem("unit_used"), NU * NB)
            mixer_done(nc.vector.tensor_scalar(hden, sums[:, :, D], EPS, None, ALU.add))
            mixer_after(dve, "den")
            mixer_done(nc.vector.reciprocal(hrden, hden))
            mixer_after(dve, "rden")
            for hb in range(HB):
                nc.vector.tensor_scalar(tn[:, hb, :], sums[:, hb, 0:D], hrden[:, hb:hb + 1], None, ALU.mult)
            mixer_done(nc.vector.tensor_tensor(hrr, sums[:, :, D], hrden, ALU.mult))
            dve.wait_ge(sem("mixer_in"), 16 * 13)
            nc.vector.tensor_scalar(hvec[:, 1, :], hvec[:, 1, :], 88.0, None, ALU.min).then_inc(sem("alog_min"), 1)
            mixer_after(dve, "slices_ps")
            nc.vector.tensor_copy(slices_t[:], ps[:, 2, :])
            mixer_done(nc.vector.tensor_copy(rrow[0:1, :], ps[0:1, 3, :]))
            mixer_after(dve, "st_ps")
            mixer_done(nc.vector.tensor_copy(st_t[:].rearrange("p b (r g) -> p b r g", r=2),
                                             ps[:, 0, 0:256].rearrange("p (b g) -> p b g", b=4).unsqueeze(2)
                                             .to_broadcast([P, 4, 2, G])))
            mixer_after(dve, "in_ps")
            nc.vector.memset(xp[:, :, 0:2], 0.0)
            nc.vector.tensor_copy(xp[:, 0:4, 2:66], ps[:, 2, 0:256].rearrange("p (b g) -> p b g", b=4))
            nc.vector.tensor_copy(xp[0:64, 4:6, 2:66], ps[0:64, 2, 256:384].rearrange("p (b g) -> p b g", b=2))
            nc.vector.tensor_tensor(dtu[0:64, :], ps[0:64, 3, 0:8], hvec[0:64, 0, :], ALU.add)
            mixer_done(nc.vector.tensor_tensor(dtu[64:P, :], ps[64:P, 3, 8:16], hvec[64:P, 0, :], ALU.add))
            for tap, before_step in ((2, "pad"), (1, "tap0"), (0, "tap1")):
                mixer_after(dve, before_step)
                for m in range(6):
                    w = P if m < 4 else 64
                    src, o = xp[0:w, m, tap:tap + 64], xc[0:w, m, :]
                    if tap == 2:
                        last = nc.vector.tensor_scalar(o, src, convw[0:w, m, 2:3], convw[0:w, m, 3:4], ALU.mult, ALU.add)
                    else:
                        last = nc.vector.scalar_tensor_tensor(o, src, convw[0:w, m, tap:tap + 1], o, ALU.mult, ALU.add)
                mixer_done(last)
            mixer_after(dve, "exp")
            nc.vector.tensor_scalar(xe[:, 0:4, :], xe[:, 0:4, :], 1.0, None, ALU.add)
            mixer_done(nc.vector.tensor_scalar(xe[0:64, 4:6, :], xe[0:64, 4:6, :], 1.0, None, ALU.add))
            mixer_after(dve, "plus")
            nc.vector.reciprocal(xe[:, 0:4, :], xe[:, 0:4, :])
            mixer_done(nc.vector.reciprocal(xe[0:64, 4:6, :], xe[0:64, 4:6, :]))
            mixer_after(dve, "recip")
            for r in range(2):
                nc.vector.tensor_tensor(xtd[:, :, r * 64:(r + 1) * 64], xc[:, 0:4, :], xe[:, 0:4, :], ALU.mult)
                nc.vector.tensor_tensor(bt[0:64, r * 64:(r + 1) * 64], xc[0:64, 4, :], xe[0:64, 4, :], ALU.mult)
            mixer_done(nc.vector.tensor_tensor(ct[0:64, :], xc[0:64, 5, :], xe[0:64, 5, :], ALU.mult))
            mixer_after(dve, "x_ps")
            mixer_done(nc.vector.scalar_tensor_tensor(dtn, dtu, -1.0, dtu, ALU.mult, ALU.max))
            mixer_after(dve, "dt_exp")
            mixer_done(nc.vector.tensor_scalar(dtn, dtn, 1.0, None, ALU.add))
            mixer_after(dve, "dt_ln")
            mixer_done(nc.vector.scalar_tensor_tensor(dtv, dtu, 0.0, dtl, ALU.max, ALU.add))
            mixer_after(dve, "dt")
            dve.wait_ge(sem("alog_exp"), 1)
            mixer_done(nc.vector.tensor_tensor(dta, hea, dtv, ALU.mult))
            mixer_after(dve, "dt_a")
            mixer_done(nc.vector.tensor_scalar(dta, dta, 200.0, None, ALU.min))
            mixer_after(dve, "keep")
            nc.vector.memset(mix, 0.0)
            mixer_done(nc.vector.tensor_tensor(decay, perm0.unsqueeze(1).to_broadcast([P, HEADS, 64]),
                                               dta.unsqueeze(2).to_broadcast([P, HEADS, 64]), ALU.mult))
            mixer_after(dve, "keep_ps")
            mixer_done(nc.vector.tensor_tensor_scan(scan.rearrange("p h t -> p (h t)"), ps[:, 5, :], rperm, 0.0,
                                                    ALU.mult, ALU.add))
            mixer_after(dve, "scan")
            nc.vector.tensor_tensor(mix[0:64, :, 1:64], scan[0:64, :, 0:63],
                                    ps[0:64, 7, 0:63].unsqueeze(1).to_broadcast([64, HEADS, 63]), ALU.mult)
            nc.vector.tensor_tensor(mix[64:P, :, 0:63], scan[64:P, :, 62::-1],
                                    ps[64:P, 7, 1:64].unsqueeze(1).to_broadcast([64, HEADS, 63]), ALU.mult)
            mixer_done(nc.vector.tensor_tensor(fcs[0:64, :], ps[0:64, 0, 0:8], hvec[0:64, 2, :], ALU.add))
            mixer_after(dve, "skip")
            nc.vector.tensor_tensor(xdt, heads(ps[:, 2, :]), dtv.unsqueeze(2).to_broadcast([P, HEADS, HP]), ALU.mult)
            mixer_done(nc.vector.tensor_tensor(heads(xo[0:64, :]), heads(ps[0:64, 2, :]),
                                               fcs[0:64, :].unsqueeze(2).to_broadcast([64, HEADS, HP]), ALU.mult))
            mixer_after(dve, "y_ps")
            mixer_done(nc.vector.tensor_tensor(yy[0:64, :], ps[0:64, 6, :], xo[0:64, :], ALU.add))
            mixer_after(dve, "z_exp")
            mixer_done(nc.vector.tensor_scalar(ze[0:64, :], ze[0:64, :], 1.0, None, ALU.add))
            mixer_after(dve, "z_plus")
            mixer_done(nc.vector.reciprocal(zs[0:64, :], ze[0:64, :]))
            mixer_after(dve, "z_recip")
            mixer_done(nc.vector.tensor_tensor(zs[0:64, :], ps[0:64, 4, :], zs[0:64, :], ALU.mult))
            mixer_after(dve, "z_silu")
            mixer_done(nc.vector.tensor_tensor(yy[0:64, :], yy[0:64, :], zs[0:64, :], ALU.mult))
            mixer_after(dve, "square")
            mixer_done(nc.vector.tensor_scalar(hms[0:64, :], hss[0:64, :], 1.0 / DI, EPS, ALU.mult, ALU.add))
            mixer_after(dve, "ms_guess")
            mixer_done(nc.vector.scalar_tensor_tensor(hr1[0:64, :], hr0[0:64, :], -0.5, hr0[0:64, :], ALU.mult, ALU.mult))
            mixer_after(dve, "ms_n1")
            mixer_done(nc.vector.tensor_tensor(hr2[0:64, :], hr1[0:64, :], hms[0:64, :], ALU.mult))
            mixer_after(dve, "ms_n2")
            mixer_done(nc.vector.scalar_tensor_tensor(hrs[0:64, :], hr2[0:64, :], 1.5, hr0[0:64, :], ALU.add, ALU.mult))
            mixer_after(dve, "ms_root")
            mixer_done(nc.vector.tensor_scalar(yy[0:64, :], yy[0:64, :], hrs[0:64, :], None, ALU.mult))
            mixer_after(dve, "gated_ps")
            for b in range(4):
                last = nc.vector.tensor_scalar(ygt[:, b, :], ps[:, 2, b * 64:(b + 1) * 64], normw[:, b:b + 1], None, ALU.mult)
            mixer_done(last)
            mixer_after(dve, "ot_ps")
            mixer_done(nc.vector.tensor_copy(ott.rearrange("p b t -> p (b t)"), ps[:, 7, 0:256]))
            mixer_after(dve, "msl_ps")
            mixer_done(nc.vector.tensor_copy(msl[:], ps[:, 3, :]))
            dve.wait_ge(sem("small_in"), 16 * 13)
            nc.vector.tensor_scalar(epsb[:], epsb[:], 2.0, None, ALU.add).then_inc(sem("eps_ok"), 1)

            def x2_block(b):
                dve.wait_ge(sem("out_ps"), b + 1)
                if not isinstance(b, int) or b > 0:
                    dve.wait_ge(sem("x2n_ps"), b)
                    dve.wait_ge(sem("res2_ok"), b)
                nc.vector.scalar_tensor_tensor(g1[:], ps[:, b % 2, :], outb[:], res[:, bass.ts(b, BW)], ALU.add, ALU.add)\
                    .then_inc(sem("x2_ok"), 1)

            def x2_norm(b):
                dve.wait_ge(sem("x2n_ps"), b + 1)
                ln_stats(dve, b, lambda q: ps[:, 2, q * P:(q + 1) * P], "lc")
                ln_newton(dve, b, "lc", ve[:], r0[:], r1[:], r2[:], rs[:])
                ln_apply(lambda q: ps[:, 2, q * P:(q + 1) * P], lambda q: g2[:, q * P:(q + 1) * P], rs, "lc_xn")
                dve.wait_ge(sem("xn_round"), b + 1)
                nc.vector.tensor_tensor(xnl[:, bass.ts(b, TB), :], g2[:].rearrange("p (t d) -> p t d", t=TB),
                                        xnh[:, bass.ts(b, TB), :].bitcast(F32), ALU.subtract).then_inc(sem("xn_rest"), 1)

            dve.wait_ge(sem("res1_ok"), NB)
            x2_block(0)
            x2_norm(0)
            with dve.Fori(1, NB) as b:
                x2_block(b)
                x2_norm(b)

            def e4(ap):
                return ap.rearrange("p q e -> p (q e)")

            def post2(slot, b):
                if slot == 5:
                    dve.wait_ge(sem("merge_ps"), b + 1)
                    nc.vector.scalar_tensor_tensor(g2[:], ps[:, 6, :], bmc[:], res[:, bass.ts(b, BW)], ALU.add, ALU.add)\
                        .then_inc(sem("x3_ok"), 1)
                if slot == 6:
                    dve.wait_ge(sem("x3n_ps"), b + 1)
                    ln_stats(dve, b, lambda q: ps[:, 7, q * P:(q + 1) * P], "ld", 12)
                if slot == 7:
                    ln_newton(dve, b, "ld", ve[:], r0[:], r1[:], r2[:], rs[:], per=12)
                    nc.vector.tensor_tensor(r3[:], rs[:], rs[:], ALU.mult).then_inc(sem("ld_own"), 1)
                    own_step(dve, b, "ld", 12, 6)
                    nc.vector.tensor_tensor(r3[:], r3[:], mv[:, :, 1], ALU.mult).then_inc(sem("ld_own"), 1)
                    own_step(dve, b, "ld", 12, 7)
                    nc.vector.tensor_scalar(r4[:], r3[:], EPS, None, ALU.add).then_inc(sem("le_ve"), 1)
                if slot == 8:
                    ln_newton(dve, b, "le", r4[:], r5[:], r6[:], r7[:], r8[:], "ld", 12, 8)
                    nc.vector.tensor_tensor(r6[:], rs[:], r8[:], ALU.mult).then_inc(sem("ld_own"), 1)
                    nc.vector.tensor_tensor(r7[:], r4[:], r8[:], ALU.mult).then_inc(sem("ld_own"), 1)
                    own_step(dve, b, "ld", 12, 12)
                    ln_apply(lambda q: ps[:, 7, q * P:(q + 1) * P], lambda q: g1[:, q * P:(q + 1) * P], r6, "ld_xn")
                if slot == 12:
                    dve.wait_ge(sem("router_ps"), b + 1)
                    pr = ps[:, 6, 0:TB * E].rearrange("p (q e) -> p q e", q=TB)
                    nc.vector.tensor_tensor(rt[:], pr, r7[:].unsqueeze(2).to_broadcast([P, TB, E]), ALU.mult).then_inc(sem("router_own"), 1)
                    own_step(dve, b, "router", 12, 1)
                    nc.vector.tensor_tensor(rt[:], rt[:], brb[:].unsqueeze(1).to_broadcast([P, TB, E]), ALU.add).then_inc(sem("router_own"), 1)
                    own_step(dve, b, "router", 12, 2)
                    nc.vector.tensor_reduce(rq[:], rt[:], AX, ALU.max).then_inc(sem("router_own"), 1)
                    own_step(dve, b, "router", 12, 3)
                    nc.vector.tensor_tensor(rt[:], rt[:], rq[:].unsqueeze(2).to_broadcast([P, TB, E]), ALU.subtract)\
                        .then_inc(sem("router_sub"), 1)
                if slot == 13:
                    dve.wait_ge(sem("router_exp"), b + 1)
                    dve.wait_ge(sem("x3t_ok"), b + 1)
                    other = rt[:].unsqueeze(2).to_broadcast([P, TB, E, E])
                    own = rt[:].unsqueeze(3).to_broadcast([P, TB, E, E])
                    gt = ps[:, 7, 0:256].rearrange("p (q e f) -> p q e f", q=TB, e=E)
                    eq = ps[:, 7, 256:512].rearrange("p (q e f) -> p q e f", q=TB, e=E)
                    lowb = low[:].rearrange("p (e f) -> p e f", e=E).unsqueeze(1).to_broadcast([P, TB, E, E])
                    nc.vector.tensor_tensor(gt, other, own, ALU.is_gt).then_inc(sem("router_own"), 1)
                    nc.vector.tensor_tensor(eq, other, own, ALU.is_equal).then_inc(sem("router_own"), 1)
                    own_step(dve, b, "router", 12, 4)
                    nc.vector.tensor_reduce(rkg[:], gt, AX, ALU.add).then_inc(sem("router_own"), 1)
                    own_step(dve, b, "router", 12, 5)
                    nc.vector.tensor_tensor(eq, eq, lowb, ALU.mult).then_inc(sem("router_own"), 1)
                    own_step(dve, b, "router", 12, 7)
                    nc.vector.tensor_reduce(rke[:], eq, AX, ALU.add).then_inc(sem("router_own"), 1)
                    own_step(dve, b, "router", 12, 8)
                    own_step(dve, b, "router", 12, 6)
                    nc.vector.tensor_tensor(rkg[:], rkg[:], rke[:], ALU.add).then_inc(sem("router_own"), 1)
                    own_step(dve, b, "router", 12, 9)
                    nc.vector.scalar_tensor_tensor(e4(rt[:]), e4(rkg[:]), 2.0, e4(rt[:]), ALU.is_lt, ALU.mult).then_inc(sem("router_own"), 1)
                    own_step(dve, b, "router", 12, 10)
                    nc.vector.tensor_reduce(rq[:], rt[:], AX, ALU.add).then_inc(sem("router_own"), 1)
                    own_step(dve, b, "router", 12, 11)
                    nc.vector.reciprocal(rq[:], rq[:]).then_inc(sem("router_own"), 1)
                    own_step(dve, b, "router", 12, 12)
                    nc.vector.tensor_tensor(rt[:], rt[:], rq[:].unsqueeze(2).to_broadcast([P, TB, E]), ALU.mult).then_inc(sem("w_ok"), 1)
                if slot == 15:
                    dve.wait_ge(sem("wt_ps"), b + 1)
                    nc.vector.tensor_copy(g1[0:E, :], ps[0:E, 7, :]).then_inc(sem("wt_ok"), 1)

            def expert_weights(e):
                dve.wait_ge(sem("m_in"), 32 * (e + 1))
                g = lngb[:, 0, bass.ts(e, 1)]
                nc.vector.tensor_scalar(m1h[:, e, :], m1raw[:], g, None, ALU.mult).then_inc(sem("m1_round"), 1)
                dve.wait_ge(sem("m1_round"), e + 1)
                nc.vector.scalar_tensor_tensor(m1l[:, e, :], m1raw[:], g, m1h[:, e, :].bitcast(F32), ALU.mult, ALU.subtract)\
                    .then_inc(sem("m1_rest"), 1)
                dve.wait_ge(sem("m2_round"), e + 1)
                nc.vector.tensor_tensor(m2l[:, e, :, :], m2raw[:].rearrange("p (c d) -> p c d", c=HC),
                                        m2h[:, e, :, :].bitcast(F32), ALU.subtract).then_inc(sem("m2_rest"), 1)
                dve.wait_ge(sem("b1_ps"), e + 1)
                nc.vector.tensor_tensor(b1c[:, bass.ts(e, HC)], ps[:, 6, 64:64 + HC], b1c[:, bass.ts(e, HC)], ALU.add)\
                    .then_inc(sem("b1_used"), 1)

            def pass2(blk, ib, first, last):
                for u in range(NU):
                    nxt = after(blk, u, LEAD)
                    early = u in (5, 7, 8)
                    if early and not first:
                        post2(u, ib - 1)
                    if u + LEAD < NU or not last:
                        split_rest(dve, nc.vector, *nxt)
                    if not early and not first:
                        post2(u, ib - 1)
                    if u == 10:
                        expert_weights(ib)

            dve.wait_ge(sem("res2_ok"), NB)
            for u in range(LEAD):
                split_rest(dve, nc.vector, NB, u)
            pass2(NB, 0, True, False)
            with dve.Fori(1, NB - 1) as ib:
                pass2(ib + NB, ib, False, False)
            pass2(2 * NB - 1, NB - 1, False, True)
            for slot in range(NU):
                post2(slot, NB - 1)

            def split(b, k):
                dve.wait_ge(sem("gelu_ok"), STEPS * b + k + 1)
                if k >= 4 or not isinstance(b, int) or b > 0:
                    dve.wait_ge(sem("down_used"), STEPS * b + k - 3)
                nc.vector.tensor_copy(geh[:, k % 4, :], gel[:, k % 4, :]).then_inc(sem("gelu_round"), 1)
                dve.wait_ge(sem("gelu_round"), STEPS * b + k + 1)
                nc.vector.tensor_tensor(gelo[:, k % 4, :], gel[:, k % 4, :], geh[:, k % 4, :].bitcast(F32), ALU.subtract)\
                    .then_inc(sem("gelu_rest"), 1)

            def weigh(b, e):
                dve.wait_ge(sem("down_used"), STEPS * b + HC * (e + 1))
                if e == 0:
                    dve.wait_ge(sem("wb_in"), 16 * (b + 1))
                if e >= 2:
                    dve.wait_ge(sem("added"), (E - 1) * b + max(1, e - 2))
                elif not isinstance(b, int) or b > 0:
                    dve.wait_ge(sem("added"), (E - 1) * b)
                ins = nc.vector.tensor_tensor(wy[:, e % 2, :], ps[:, 4 + e % 2, :], wb[:, b % 2, e, :], ALU.mult)
                if e == 0:
                    ins.then_inc(sem("first_own"), 1)
                    dve.wait_ge(sem("first_own"), 2 * b + 1)
                    dve.wait_ge(sem("bias2_ps"), b + 1)
                    nc.vector.tensor_tensor(wy[:, 0, :], ps[:, 6, :], wy[:, 0, :], ALU.add).then_inc(sem("first_own"), 1)
                    dve.wait_ge(sem("first_own"), 2 * b + 2)
                    ins = nc.vector.tensor_tensor(wy[:, 0, :], res[:, bass.ts(b, BW)], wy[:, 0, :], ALU.add)
                ins.then_inc(sem("weighted"), 1)

            def mx_rest(b):
                dve.wait_ge(sem("mx_round"), b + 1)
                nc.vector.tensor_tensor(mxl[:, bass.ts(b, BW)], xnr[:], mxh[:, bass.ts(b, BW)].bitcast(F32), ALU.subtract)\
                    .then_inc(sem("mx_rest"), 1)

            def experts(b, last_block):
                for k in range(STEPS):
                    if k + 2 < STEPS:
                        split(b, k + 2)
                    elif not last_block:
                        split(b + 1, k + 2 - STEPS)
                    if k % HC == HC - 1:
                        weigh(b, k // HC)
                    if k == 17 and not last_block:
                        mx_rest(b + 1)

            dve.wait_ge(sem("res3_ok"), NB)
            mx_rest(0)
            split(0, 0)
            split(0, 1)
            experts(0, False)
            with dve.Fori(1, NB - 1) as b:
                experts(b, False)
            experts(NB - 1, True)

        @block.gpsimd
        def _(pool):
            def tree(b):
                for q in range(TB):
                    t, s = TB * b + q, q % 2
                    pool.wait_ge(sem("prod_ok"), t + 1)
                    nc.gpsimd.tensor_tensor(prod[:, s, 0:4, :], prod[:, s, 0:4, :], prod[:, s, 4:8, :], ALU.add).then_inc(sem("tree1"), 1)
                    pool.wait_ge(sem("tree1"), t + 1)
                    nc.gpsimd.tensor_tensor(prod[:, s, 0:2, :], prod[:, s, 0:2, :], prod[:, s, 2:4, :], ALU.add).then_inc(sem("tree2"), 1)
                    pool.wait_ge(sem("acc_ok"), t + 1)
                    nc.gpsimd.tensor_tensor(acc[:, s, 0, :], acc[:, s, 0, :], acc[:, s, 1, :], ALU.add).then_inc(sem("acc_sum"), 1)
                    pool.wait_ge(sem("tree2"), t + 1)
                    nc.gpsimd.tensor_tensor(prod[:, s, 0, :], prod[:, s, 0, :], prod[:, s, 1, :], ALU.add).then_inc(sem("tree3"), 1)

            with pool.Fori(0, NB) as b:
                tree(b)

            def post1(slot, b):
                if 6 <= slot < 10:
                    q = slot - 6
                    pool.wait_ge(sem("lg_max"), TB * b + q + 1)
                    nc.gpsimd.tensor_tensor(hg(lg[:, q, :]), hg(lg[:, q, :]), smx[:, q, :].unsqueeze(2).to_broadcast([P, HEADS, G]),
                                            ALU.subtract).then_inc(sem("lg_sub"), 1)
                if 9 <= slot < 13:
                    q = slot - 9
                    pool.wait_ge(sem("lg_rec"), TB * b + q + 1)
                    nc.gpsimd.tensor_tensor(hg(lg[:, q, :]), hg(lg[:, q, :]), sden[:, q, :].unsqueeze(2).to_broadcast([P, HEADS, G]),
                                            ALU.mult).then_inc(sem("sw_ok"), 1)

            def hg(ap):
                return ap.rearrange("p (h g) -> p h g", h=HEADS)

            def pass1(ib, first, last):
                for u in range(NU):
                    nxt = after(ib, u, LEAD)
                    if u + LEAD < NU or not last:
                        split_rest(pool, nc.gpsimd, *nxt)
                    if not first:
                        post1(u, ib - 1)

            pass1(0, True, False)
            with pool.Fori(1, NB - 1) as ib:
                pass1(ib, False, False)
            pass1(NB - 1, False, True)
            for slot in range(NU):
                post1(slot, NB - 1)

            pool.wait_ge(sem("x2_round"), 1)
            nc.gpsimd.tensor_tensor(x2l[:], x2raw[:], x2h[:].bitcast(F32), ALU.subtract).then_inc(sem("x2_rest"), 1)

            def norm2(b):
                pool.wait_ge(sem("x2_ok"), b + 1)
                nc.gpsimd.tensor_copy(res[:, bass.ts(b, BW)], g1[:]).then_inc(sem("res2_ok"), 1)

            norm2(0)
            with pool.Fori(1, NB) as b:
                norm2(b)

            def post2(slot, b):
                if slot == 6:
                    pool.wait_ge(sem("x3_ok"), b + 1)
                    nc.gpsimd.tensor_copy(res[:, bass.ts(b, BW)], g2[:]).then_inc(sem("res3_ok"), 1)

            def pass2(blk, ib, first, last):
                for u in range(NU):
                    nxt = after(blk, u, LEAD)
                    if u + LEAD < NU or not last:
                        split_rest(pool, nc.gpsimd, *nxt)
                    if not first:
                        post2(u, ib - 1)

            pass2(NB, 0, True, False)
            with pool.Fori(1, NB - 1) as ib:
                pass2(ib + NB, ib, False, False)
            pass2(2 * NB - 1, NB - 1, False, True)
            for slot in range(NU):
                post2(slot, NB - 1)

            def add(b):
                for e in range(1, E):
                    pool.wait_ge(sem("weighted"), E * b + e + 1)
                    if e > 1:
                        pool.wait_ge(sem("added"), (E - 1) * b + e - 1)
                    elif not isinstance(b, int) or b > 0:
                        pool.wait_ge(sem("out_done"), 16 * b)
                    nc.gpsimd.tensor_tensor(total[:], wy[:, 0, :] if e == 1 else total[:], wy[:, e % 2, :], ALU.add)\
                        .then_inc(sem("added"), 1)

            add(0)
            with pool.Fori(1, NB) as b:
                add(b)


def kernel(**inputs):
    import numpy as np
    import concourse.bacc as bacc
    from concourse.bass_utils import run_bass_kernel_spmd

    v = {k: np.asarray(a) for k, a in inputs.items()}
    same = lambda a: np.ascontiguousarray(a)
    f = "L0_ffn_"
    conv = np.zeros((P, 6, 4), np.float32)
    for m in range(6):
        w, c = (P, m * P) if m < 4 else (64, DI + (m - 4) * 64)
        conv[:w, m, 0:3] = v[f + "hy_conv_w"][c:c + w]
        conv[:w, m, 3] = v[f + "hy_conv_b"][c:c + w]
    r = np.arange(P)
    step = np.where(r < 64, r, P - 1 - r)
    own = (step[:, None] == np.arange(64)[None, :]).astype(np.float32)
    first_off = own.copy()
    first_off[:, 0] = 0
    side = (r[:, None] // 64 == r[None, :] // 64).astype(np.float32)
    low = np.tile(np.tril(np.ones((E, E), np.float32), -1).reshape(1, 64), (P, 1))
    cst = np.concatenate([np.eye(P, dtype=np.float32), np.tile(own, (1, HEADS)), first_off, side, low], 1)
    arrays = {
        "x": same(v["x"]), "xt": same(v["x"].T),
        "adjt": same(v["adj"].reshape(NB, BW, NU, UJ, P).transpose(0, 2, 4, 3, 1)).reshape(NB, NU, P, UW),
        "cst": cst,
        "w2": same(np.concatenate([v["L0_gnn_W2"].transpose(1, 0, 2).reshape(D, KG * D), v["L0_gnn_W1"]], 1)),
        "w1t": same(v["L0_gnn_W1"].T), "gb": same(v["L0_gnn_b"]),
        "wx": same(v[f + "W_x"]), "wslt": same(np.concatenate([v[f + "W_slice"].T] * 2, 0)), "bx": same(v[f + "b_x"].reshape(HB, P).T),
        "bslice": same(v[f + "b_slice"]), "temp": same(v[f + "temperature"].reshape(HEADS)),
        "outb": same(v[f + "out_b"]), "bm": same(v["L1_gnn_bm"]), "gb1": same(v["L1_gnn_b1"].T), "gb2": same(v["L1_gnn_b2"].T),
        "eps1": same(v["L1_gnn_eps1"]), "eps2": same(v["L1_gnn_eps2"]),
        "lng": same(v["L1_ffn_ln_g"].T), "lnb": same(v["L1_ffn_ln_b"].T),
        "b1": same(v["L1_ffn_b1"].reshape(STEPS, P).T), "wr": same(v["L1_ffn_Wr"]), "br": same(v["L1_ffn_br"]),
        "b2": same(v["L1_ffn_b2"]),
        "wfxt": same(v[f + "W_fx"].T), "bfx": same(v[f + "b_fx"]), "hin": same(v[f + "hy_in_w"].T), "convw": conv,
        "dtb": same(v[f + "hy_dt_bias"]), "alog": same(v[f + "hy_A_log"]), "hd": same(v[f + "hy_D"]),
        "fcdt": same(v[f + "hy_fcD_w"].T), "hout": same(v[f + "hy_out_w"].T), "outwt": same(v[f + "out_w"].T),
        "normw": same(v[f + "hy_norm_w"].reshape(4, P).T), "x2": same(v["L1_gnn_x2"]),
        "mlpw": same(np.concatenate([v["L1_gnn_W1"].transpose(2, 0, 1), v["L1_gnn_W2"].transpose(2, 0, 1),
                                     v["L1_gnn_Wm"].reshape(D, 2, D).transpose(2, 1, 0)], 1)),
        "m1": same(v["L1_ffn_W1"]),
        "m2": same(v["L1_ffn_W2"].reshape(E, HC, P, D).transpose(0, 2, 1, 3)).reshape(E, P, HC * D),
    }
    nc = bacc.Bacc("TRN2", target_bir_lowering=False, num_devices=1)
    ins = {k: nc.dram_tensor("in_" + k, a.shape, F32, kind="ExternalInput").ap() for k, a in arrays.items()}
    out_t = nc.dram_tensor("out_t", (D, N), F32, kind="ExternalOutput").ap()
    scratch_xn = nc.dram_tensor("scratch_xn", (D, N), F32).ap()
    scratch_w = nc.dram_tensor("scratch_w", (E, N), F32).ap()
    build_network(nc, ins, out_t, scratch_xn, scratch_w)
    result = run_bass_kernel_spmd(nc, [{"in_" + k: a for k, a in arrays.items()}], core_ids=[0])
    return np.ascontiguousarray(result.results[0]["out_t"].T)
```

```python
import concourse.bass as bass
from concourse import mybir
from contextlib import ExitStack

F32 = mybir.dt.float32
F32R = mybir.dt.float32r
I32 = mybir.dt.int32
ALU = mybir.AluOpType
ACT = mybir.ActivationFunctionType
AX = mybir.AxisListType.X

P = 128
N = 4096
D = 128
BW = 512
NB = N // BW
NT = N // P
TB = BW // P
UJ = 2
NU = NT // UJ
UW = UJ * BW
RING = 4
LEAD = 3
KG = 16
HEADS, HP, G = 8, 64, 64
HG = HEADS * G
HB = HG // P
DI = HEADS * HP
NIN = 2 * DI + 2 * 64 + 2 * HEADS
E = 8
HID = 512
HC = HID // P
STEPS = E * HC
VBANKS = ((3, 4), (1, 7))
PE_TAIL = {0: "layer 0, first", 1: "layer 0, second", 2: "layer 1, first", 3: "layer 1, second", 4: "layer 2, first",
           5: "layer 2, second", 7: "merge", 9: "turn", 19: "turn back", 21: "route", 28: "turn weights"}
ACT_TAIL = {1: "layer 0, first", 2: "layer 0, second", 3: "layer 1, first", 4: "layer 1, second", 5: "layer 2, first",
            6: "layer 2, second", 20: "keep normed", 23: "exponentials", 30: "store weights"}
DVE_TAIL = {8: "merge", 10: "statistics", 12: "root", 14: "second variance", 15: "second root", 17: "norm", 22: "route",
            25: "choose", 29: "keep weights"}
TW = D + 1
EPS = 1e-5
CW = P + 8 * 64 + 64 + P + 64


def build_network(nc, A, out_t, scratch_xn, scratch_w):
    ctx = ExitStack()
    with ctx:
        sems = {}

        def sem(name):
            if name not in sems:
                sems[name] = ctx.enter_context(nc.semaphore(name))
            return sems[name]

        T = {}

        def overlay(nbytes, *groups):
            for group in groups:
                with ExitStack() as st:
                    for name, shape, dt in group:
                        T[name] = st.enter_context(nc.sbuf_tensor("t_" + name, shape, dt))
            ctx.enter_context(nc.sbuf_tensor(f"region_{groups[0][0][0]}", [P, nbytes // 4], F32))

        overlay(65536,
                [("x_n", [P, NT, D], F32), ("w2h", [P, KG * D + KG], F32R), ("w2l", [P, KG * D + KG], F32R),
                 ("prod", [P, 2, 8, D], F32), ("part", [P, 2, 4, D], F32), ("acc", [P, 2, 2, D], F32), ("x0f", [P, TB, D], F32), ("h_n", [P, TB, D], F32), ("nmr", [P, TB], F32),
                 ("hth", [P, 2, BW], F32R), ("htl", [P, 2, BW], F32R), ("node", [P, 2, TB, KG], F32),
                 ("w1t", [KG, P], F32), ("gb", [KG, P], F32), ("wbf", [P, P], F32),
                 ("wbh", [P, P], F32R), ("wbl", [P, P], F32R)],
                [("sw_t", [P, HB, N], F32)],
                [("m1h", [P, E, HID], F32R), ("m1l", [P, E, HID], F32R),
                 ("m2h", [P, E, HC, D], F32R), ("m2l", [P, E, HC, D], F32R)])
        overlay(32768,
                [("x0h", [P, NT, D], F32R), ("x0l", [P, NT, D], F32R)],
                [("x2raw", [P, NT, D], F32), ("hsc", [P, 4096], F32)],
                [("xnh", [P, NT, D], F32R), ("xnl", [P, NT, D], F32R)],
                [("mxh", [P, N], F32R), ("mxl", [P, N], F32R)])
        overlay(32768,
                [("term_t", [P, N], F32), ("lg", [P, 4, HG], F32), ("xn_n", [P, TB, TW], F32),
                 ("xn_t", [P, BW], F32)],
                [("x2h", [P, NT, D], F32R), ("x2l", [P, NT, D], F32R)],
                [("wb", [P, 2, E, BW], F32)])
        overlay(49152,
                [("raw", [P, RING, UW], F32), ("ah", [P, RING, UW], F32R), ("al", [P, RING, UW], F32R)],
                [("w2raw", [P, KG * D + KG], F32), ("wx", [P, HB, D], F32), ("wslt", [P, G], F32),
                 ("bxc", [P, HB], F32), ("bxb", [P, HB, P], F32), ("bsl", [P, G], F32),
                 ("tempb", [P, HEADS], F32)],
                [("hin", [P, 4, NIN], F32), ("hout", [P, 4, DI], F32), ("wfxt", [P, DI], F32),
                 ("outwt", [P, 4, D], F32), ("fcdt", [P, 4, HEADS], F32), ("convw", [P, 6, 4], F32),
                 ("normw", [P, 4], F32), ("bfx", [1, DI], F32), ("hvec", [P, 3, HEADS], F32),
                 ("hcst", [P, CW - P], F32), ("slices_t", [P, DI], F32), ("st_t", [P, 4, P], F32)],
                [("gel", [P, 4, BW], F32), ("geh", [P, 4, BW], F32R), ("gelo", [P, 4, BW], F32R),
                 ("xnr", [P, BW], F32), ("wy", [P, 2, BW], F32),
                 ("total", [P, BW], F32)])
        overlay(16384, [("res", [P, N], F32)])
        overlay(12544,
                [("wc", [P, HG], F32), ("cb", [P, HG], F32), ("sums", [P, HB, TW], F32),
                 ("pre", [P, BW], F32)],
                [("g1", [P, BW], F32), ("g2", [P, BW], F32), ("mlp", [P, 8, D], F32), ("gap", [P, 4], F32),
                 ("m1raw", [P, HID], F32), ("m2raw", [P, HID], F32)])
        for name, shape in [("ident", [P, P]), ("stat", [P, TB, 6]), ("mv", [P, TB, 2]), ("ve", [P, TB]),
                            ("lnv", [P, TB]), ("r0", [P, TB]), ("r1", [P, TB]), ("r2", [P, TB]),
                            ("rs", [P, TB]), ("itemp", [P, HEADS]), ("smx", [P, 4, HEADS]),
                            ("sden", [P, 4, HEADS]), ("pause", [P, 1])]:
            T[name] = ctx.enter_context(nc.sbuf_tensor("t_" + name, shape, F32))
        overlay(1792,
                [("outb", [P, 1], F32), ("bmc", [P, 1], F32), ("gbias", [P, 6], F32), ("epsb", [P, 2], F32),
                 ("lngb", [P, 2, E], F32), ("b1c", [P, STEPS], F32), ("wr", [P, E], F32),
                 ("brb", [P, E], F32), ("low", [P, 64], F32), ("b2c", [P, E], F32),
                 ("r3", [P, TB], F32), ("r4", [P, TB], F32), ("r5", [P, TB], F32), ("r6", [P, TB], F32),
                 ("r7", [P, TB], F32), ("r8", [P, TB], F32), ("rt", [P, TB, E], F32), ("rq", [P, TB], F32), ("rkg", [P, TB, E], F32), ("rke", [P, TB, E], F32)])
        (x_n, w2h, w2l, prod, part, acc, x0f, h_n, nmr, hth, htl, node, w1t, gb, wbf, wbh, wbl, sw_t, m1h, m1l, m2h, m2l,
         x0h, x0l, x2raw, hsc, xnh, xnl, mxh, mxl, term_t, lg, xn_n, xn_t, x2h, x2l, wb, raw, ah, al,
         w2raw, wx, wslt, bxc, bxb, bsl, tempb, hin, hout, wfxt, outwt, fcdt, convw, normw, bfx, hvec,
         hcst, slices_t, st_t, gel, geh, gelo, xnr, wy, total, res, wc, cb, sums, pre, g1, g2, mlp, _,
         m1raw, m2raw, ident, stat, mv, ve, lnv, r0, r1, r2, rs, itemp, smx, sden, pause, outb, bmc, gbias, epsb,
         lngb, b1c, wr, brb, low, b2c, r3, r4, r5, r6, r7, r8, rt, rq, rkg, rke) = T.values()
        ps = ctx.enter_context(nc.psum_tensor("ps", [P, 8, 512], F32))

        at = [0]

        def hs(n):
            at[0] += n
            return hsc[:, at[0] - n:at[0]]

        hden, hrden, hrr = hs(4), hs(4), hs(4)
        tn = hs(512).rearrange("p (b d) -> p b d", b=4)
        rrow = hs(512)
        xp = hs(6 * 66).rearrange("p (b t) -> p b t", b=6)
        xc = hs(384).rearrange("p (b t) -> p b t", b=6)
        xe = hs(384).rearrange("p (b t) -> p b t", b=6)
        xtd = hs(512).rearrange("p (b t) -> p b t", b=4)
        bt = hs(128)
        ct = hs(64)
        dtu, dtn, dtl, dtv, dta, hea = hs(8), hs(8), hs(8), hs(8), hs(8), hs(8)
        fcs = hs(8)
        hss, hms, hln, hr0, hr1, hr2, hrs = (hs(1) for _ in range(7))
        decay = slices_t[:].rearrange("p (h t) -> p h t", h=HEADS)
        scan = tn.rearrange("p b d -> p (b d)").rearrange("p (h t) -> p h t", h=HEADS)
        mix = hs(512).rearrange("p (h t) -> p h t", h=HEADS)
        assert at[0] <= 4096
        hfree = hin[:].rearrange("p a b -> p (a b)")
        xdt = hfree[:, 0:512].rearrange("p (h c) -> p h c", h=HEADS)
        xo = hfree[:, 512:1024]
        zs = hfree[:, 1024:1536]
        yy = hfree[:, 1536:2048]
        ze = hfree[:, 2048:2560]
        ygt = hfree[:, 2560:2816].rearrange("p (b t) -> p b t", b=4)
        ott = hfree[:, 2816:3072].rearrange("p (b t) -> p b t", b=4)
        msl = pre
        XB, XNB = (g1, m1raw), (g2, m2raw)
        rperm = hcst[:, 0:512]
        perm0 = hcst[:, 512:576]
        sameside = hcst[:, 576:576 + P]

        MIXER = ["den", "rden", "norm", "slices_ps", "slices", "st_ps", "st", "in_ps", "pad", "tap0", "tap1", "tap2",
                 "exp", "plus", "recip", "silu", "x_ps", "dt_neg", "dt_exp", "dt_plus", "dt_ln", "dt", "dt_a", "dt_a_min",
                 "keep", "spread", "keep_ps", "scan", "skip", "xdt", "y_ps", "y",
                 "gated_raw", "square", "ms", "ms_ln", "ms_guess", "ms_n1", "ms_n2", "ms_root", "gated", "gated_ps",
                 "ygt", "ot_ps", "ott", "msl_ps", "msl"]

        def mixer_after(eng, step):
            eng.wait_ge(sem("mixer"), MIXER.index(step) + 1)

        def mixer_done(ins):
            ins.then_inc(sem("mixer"), 1)

        block = ctx.enter_context(nc.Block())

        def lo_sem(u):
            return sem("rest_pool") if u % 4 == 3 else sem("rest_dve")

        def lo_val(blk, u):
            return 4 * blk + u // 4 + 1 if u % 4 == 3 else 12 * blk + 3 * (u // 4) + u % 4 + 1

        def before(blk, u, n):
            if u >= n:
                return blk, u - n
            if isinstance(blk, int) and blk == 0:
                return None
            return blk - 1, u - n + NU

        def after(blk, u, n):
            return (blk, u + n) if u + n < NU else (blk + 1, u + n - NU)

        def split_act(act, blk, u):
            s = u % RING
            act.wait_ge(sem(f"raw_in{s}"), 16 * (4 * blk + u // 4 + 1))
            prev = before(blk, u, RING)
            if prev:
                act.wait_ge(sem("unit_used"), NU * prev[0] + prev[1] + 1)
            nc.scalar.activation(ah[:, s, :], raw[:, s, :], ACT.Copy).then_inc(sem("rounded"), 1)

        def split_rest(eng, which, blk, u):
            if (u % 4 == 3) != (which is nc.gpsimd):
                return
            s = u % RING
            eng.wait_ge(sem("rounded"), NU * blk + u + 1)
            which.tensor_tensor(al[:, s, :], raw[:, s, :], ah[:, s, :].bitcast(F32), ALU.subtract).then_inc(lo_sem(u), 1)

        def load_unit(sp, blk, ib, u):
            s = u % RING
            prev = before(blk, u, RING)
            if prev:
                sp.wait_ge(lo_sem(prev[1]), lo_val(*prev))
            sp.dma_start(raw[:, s, :], A["adjt"][ib, u]).then_inc(sem(f"raw_in{s}"), 16)

        def mm3(o, wh, wl, mh, ml, start, stop):
            nc.tensor.matmul(o, wh, mh, start=start, stop=False)
            nc.tensor.matmul(o, wh, ml, start=False, stop=False)
            return nc.tensor.matmul(o, wl, mh, start=False, stop=stop)

        def transposes(src, bank, name):
            for q in range(TB):
                last = nc.tensor.transpose(ps[:, bank, q * P:(q + 1) * P], src[:, q * P:(q + 1) * P], ident[:])
            last.then_inc(sem(name), 1)

        def own(ins, tag):
            return ins.then_inc(sem(tag + "_own"), 1)

        def own_step(dve, k, tag, per, n):
            dve.wait_ge(sem(tag + "_own"), per * k + n)

        def ln_stats(dve, k, src, tag, per=5):
            for q in range(TB):
                last = nc.vector.bn_stats(stat[:, q, :], src(q))
            own(last, tag)
            own_step(dve, k, tag, per, 1)
            nc.vector.memset(pause[:], 0.0)
            for q in range(TB):
                last = nc.vector.bn_aggr(mv[:, q, :], stat[:, q, :])
            own(last, tag)
            own_step(dve, k, tag, per, 2)
            nc.vector.tensor_scalar(ve[:], mv[:, :, 1], EPS, None, ALU.add).then_inc(sem(tag + "_ve"), 1)

        def ln_guess(act, k, tag, v, first):
            act.wait_ge(sem(tag + "_ve"), k + 1)
            nc.scalar.activation(lnv[:], v, ACT.Ln).then_inc(sem(tag + "_ln"), 1)
            act.wait_ge(sem(tag + "_ln"), k + 1)
            nc.scalar.activation(first, lnv[:], ACT.Exp, scale=-0.5).then_inc(sem(tag + "_guess"), 1)

        def ln_newton(dve, k, tag, v, first, t1, t2, root, own_tag=None, per=5, n=3):
            o = own_tag or tag
            dve.wait_ge(sem(tag + "_guess"), k + 1)
            own(nc.vector.scalar_tensor_tensor(t1, first, -0.5, first, ALU.mult, ALU.mult), o)
            own_step(dve, k, o, per, n)
            own(nc.vector.tensor_tensor(t2, t1, v, ALU.mult), o)
            own_step(dve, k, o, per, n + 1)
            own(nc.vector.scalar_tensor_tensor(root, t2, 1.5, first, ALU.add, ALU.mult), o)
            own_step(dve, k, o, per, n + 2)

        def ln_apply(src, dst, root, name):
            for q in range(TB):
                last = nc.vector.tensor_scalar(dst(q), src(q), mv[:, q, 0:1], root[:, q:q + 1], ALU.subtract, ALU.mult)
            last.then_inc(sem(name), 1)

        @block.sync
        def _(sp):
            def load(dst, src, name):
                sp.dma_start(dst, src).then_inc(sem(name), 16)

            nodes = A["x"].rearrange("(t p) d -> p t d", p=P)
            load(x_n[:, 0:TB], nodes[:, 0:TB], "x_in0")
            load(ident[:], A["cst"][:, 0:P], "ident_in")
            load(w1t[:], A["w1t"], "prep_in")
            load(gb[:], A["gb"], "prep_in")
            load(wx[:], A["wx"].rearrange("(b p) d -> p b d", p=P), "prep_in")
            load(wslt[:], A["wslt"], "prep_in")
            load(bxc[:], A["bx"], "prep_in")
            load(bsl[:], A["bslice"].partition_broadcast(P), "prep_in")
            load(tempb[:], A["temp"].partition_broadcast(P), "prep_in")
            load(w2raw[:], A["w2"], "w2_in")
            load(x_n[:, TB:], nodes[:, TB:], "x_in")
            load(res[:], A["xt"], "xt_in")
            small = [(outb[:], A["outb"].rearrange("(p o) -> p o", o=1)), (bmc[:], A["bm"].rearrange("(p o) -> p o", o=1)),
                     (gbias[:, 0:3], A["gb1"]), (gbias[:, 3:6], A["gb2"]),
                     (epsb[:, 0:1], A["eps1"].partition_broadcast(P)), (epsb[:, 1:2], A["eps2"].partition_broadcast(P)),
                     (lngb[:, 0, :], A["lng"]), (lngb[:, 1, :], A["lnb"]),
                     (b1c[:], A["b1"]), (wr[:], A["wr"]), (brb[:], A["br"].partition_broadcast(P)),
                     (low[:], A["cst"][:, CW - 64:CW]), (b2c[:], A["b2"])]
            for dst, src in small:
                load(dst, src, "small_in")
            sp.wait_ge(sem("prep_done"), 1)
            sp.wait_ge(sem("w2_split"), 1)
            for u in range(NU):
                load_unit(sp, 0, 0, u)
            with sp.Fori(1, NB) as ib:
                for u in range(NU):
                    load_unit(sp, ib, ib, u)
            sp.wait_ge(sem("unit_used"), NU * NB)
            for dst, src in [(wfxt[:], A["wfxt"]), (bfx[:], A["bfx"].rearrange("(o n) -> o n", o=1)),
                             (hin[:], A["hin"].rearrange("(b p) n -> p b n", p=P)),
                             (convw[:], A["convw"]), (hcst[:], A["cst"][:, P:CW]),
                             (hvec[:, 0, :], A["dtb"].partition_broadcast(P)),
                             (hvec[:, 1, :], A["alog"].partition_broadcast(P)),
                             (hvec[:, 2, :], A["hd"].partition_broadcast(P)),
                             (fcdt[:], A["fcdt"].rearrange("(b p) h -> p b h", p=P)),
                             (hout[:], A["hout"].rearrange("(b p) n -> p b n", p=P)),
                             (outwt[:], A["outwt"].rearrange("(b p) d -> p b d", p=P)),
                             (normw[:], A["normw"]),
                             (x2raw[:], A["x2"].rearrange("(t p) d -> p t d", p=P))]:
                load(dst, src, "mixer_in")
            mixer_after(sp, "msl")

            def second(blk, ib, begin=0):
                for u in range(begin, NU):
                    load_unit(sp, blk, ib, u)
                    if u == 5:
                        if not isinstance(ib, int) or ib > 0:
                            sp.wait_ge(sem("m1_rest"), ib)
                            sp.wait_ge(sem("m2_rest"), ib)
                            sp.wait_ge(sem("b1_used"), ib)
                        load(m1raw[:], A["m1"][ib], "m_in")
                        load(m2raw[:], A["m2"][ib], "m_in")

            for u in range(RING):
                load_unit(sp, NB, 0, u)
            sp.wait_ge(sem("out_ps"), NB)
            load(mlp[:], A["mlpw"], "mlp_in")
            sp.wait_ge(sem("xn_rest"), NB)
            sp.wait_ge(sem("res2_ok"), NB)
            second(NB, 0, RING)
            with sp.Fori(1, NB) as ib:
                second(ib + NB, ib)

            def load_block(b):
                if not isinstance(b, int) or b > 0:
                    sp.wait_ge(sem("wb_in"), 16 * b)
                    sp.wait_ge(sem("mx_rest"), b)
                sp.wait_ge(sem("xn_stored"), 16 * (b + 1))
                sp.wait_ge(sem("w_stored"), 16 * (b + 1))
                if not isinstance(b, int) or b > 1:
                    sp.wait_ge(sem("weighted"), E * (b - 1))
                load(xnr[:], scratch_xn[:, bass.ts(b, BW)], "xnr_in")
                load(wb[:, b % 2, :, :], scratch_w[:, bass.ts(b, BW)].partition_broadcast(P), "wb_in")

            def store_block(b):
                sp.wait_ge(sem("added"), (E - 1) * (b + 1))
                sp.dma_start(out_t[:, bass.ts(b, BW)], total[:]).then_inc(sem("out_done"), 16)

            sp.wait_ge(sem("unit_used"), 2 * NU * NB)
            load_block(0)
            load_block(1)
            store_block(0)
            with sp.Fori(2, NB) as b:
                load_block(b)
                store_block(b - 1)
            store_block(NB - 1)
            sp.wait_ge(sem("out_done"), 16 * NB)

        @block.tensor
        def _(pe):
            def fold():
                pe.wait_ge(sem("prep_in"), 16 * 7)
                for h in range(HEADS):
                    o, b = HP * (h % 2), h // 2
                    nc.tensor.matmul(ps[:, VBANKS[0][h % 2], b * G:(b + 1) * G], wx[o:o + HP, b, :], wslt[o:o + HP, :],
                                     start=True, stop=True)
                pe.wait_ge(sem("ident_in"), 16)
                h_transposes(0)
                nc.tensor.matmul(ps[:, 5, 0:P], w1t[:], gb[:], start=True, stop=True).then_inc(sem("wb_ps"), 1)
                pe.wait_ge(sem("bias_cols"), 1)
                for h in range(HEADS):
                    o, b = HP * (h % 2), h // 2
                    last = nc.tensor.matmul(ps[:, VBANKS[1][h % 2], b * G:(b + 1) * G], bxb[o:o + HP, b, :],
                                            wslt[o:o + HP, :], start=True, stop=True)
                last.then_inc(sem("fold_ps"), 1)

            def h_transposes(b):
                pe.wait_ge(sem("la_xn"), b + 1)
                if not isinstance(b, int) or b > 0:
                    pe.wait_ge(sem("node_ok"), b)
                transposes(h_n[:].rearrange("p a d -> p (a d)"), 0, "h_ps")

            def h_products(b, par, has_next):
                pe.wait_ge(sem("ht_rest"), b + 1)
                if not isinstance(b, int) or b > 0:
                    pe.wait_ge(sem("term_ok"), b)
                for q in range(TB):
                    hh, hl = hth[:, par, q * P:(q + 1) * P], htl[:, par, q * P:(q + 1) * P]
                    c = KG * D
                    last = mm3(ps[:, 0, q * KG:(q + 1) * KG], hh, hl, w2h[:, c:c + KG], w2l[:, c:c + KG], True, True)
                last.then_inc(sem("node_ps"), 1)
                mm3(ps[:, 2, :], wbh[:], wbl[:], hth[:, par, :], htl[:, par, :], True, True).then_inc(sem("term_ps"), 1)
                if isinstance(b, int) and b == 0:
                    pe.wait_ge(sem("prep_done"), 1)
                for q in range(TB):
                    hh, hl = hth[:, par, q * P:(q + 1) * P], htl[:, par, q * P:(q + 1) * P]
                    def vector_pair():
                        if not isinstance(b, int) or b > 0 or q > 1:
                            pe.wait_ge(sem("acc_ok"), TB * b + q - 1)
                        for kc in (0, 1):
                            last = mm3(ps[:, VBANKS[q % 2][kc], :], hh, hl, w2h[:, kc * 512:(kc + 1) * 512],
                                       w2l[:, kc * 512:(kc + 1) * 512], True, True)
                        last.then_inc(sem("hw_dve"), 1)

                    def scalar_pair():
                        for kc in (2, 3):
                            if not isinstance(b, int) or b > 0 or q > 0:
                                pe.wait_ge(sem("prod_half" if kc == 2 else "prod_ok"), TB * b + q)
                            mm3(ps[:, 3 + kc, :], hh, hl, w2h[:, kc * 512:(kc + 1) * 512],
                                w2l[:, kc * 512:(kc + 1) * 512], True, True).then_inc(sem("hw_act"), 1)

                    if q == 0:
                        scalar_pair()
                    vector_pair()
                    if q == 2 and has_next:
                        h_transposes(b + 1)
                    if q > 0:
                        scalar_pair()

            fold()
            pe.wait_ge(sem("w2_split"), 1)
            pe.wait_ge(sem("wb_rest"), 1)
            h_products(0, 0, True)
            with pe.Fori(0, NB // 2 - 1) as i:
                h_products(2 * i + 1, 1, True)
                h_products(2 * i + 2, 0, True)
            h_products(NB - 1, 1, False)

            def post1(slot, b):
                if slot == 0:
                    pe.wait_ge(sem("x1_ok"), b + 1)
                    for q in range(TB):
                        last = nc.tensor.transpose(ps[:, 2, q * P:(q + 1) * P], xn_t[:, q * P:(q + 1) * P], ident[:])
                    last.then_inc(sem("x1n_ps"), 1)
                if slot == 3:
                    pe.wait_ge(sem("lb_xn"), b + 1)
                    for q in range(TB):
                        last = nc.tensor.transpose(ps[:, 2, q * P:(q + 1) * P], xn_n[:, q, 0:D], ident[:])
                    last.then_inc(sem("xnt_ps"), 1)
                if 4 <= slot < 8:
                    q = slot - 4
                    if q == 0:
                        pe.wait_ge(sem("xnt_ok"), b + 1)
                    if q >= 2:
                        pe.wait_ge(sem("lg_ok"), TB * b + q - 1)
                    nc.tensor.matmul(ps[:, 3 + q % 2, :], xn_t[:, q * P:(q + 1) * P], wc[:], start=True, stop=True)\
                        .then_inc(sem("lg_ps"), 1)
                if 11 <= slot < 15:
                    q = slot - 11
                    pe.wait_ge(sem("sw_ok"), TB * b + q + 1)
                    if q >= 1:
                        pe.wait_ge(sem("swt_ok"), TB * b + q)
                    for hb in range(HB):
                        last = nc.tensor.transpose(ps[:, 5, hb * P:(hb + 1) * P], lg[:, q, hb * P:(hb + 1) * P], ident[:])
                    last.then_inc(sem("swt_ps"), 1)
                    for hb in range(HB):
                        o = (hb % 2) * TW
                        last = nc.tensor.matmul(ps[:, 6 + hb // 2, o:o + TW], lg[:, q, hb * P:(hb + 1) * P], xn_n[:, q, :],
                                                start=(q == 0 and hb % 2 == 0), stop=(q == TB - 1), skip_group_check=True)
                    last.then_inc(sem("sums_ps"), 1)

            def pass1(ib, first):
                for u in range(NU):
                    s = u % RING
                    if first:
                        pe.wait_ge(sem("x0_rest"), UJ * (u + 1))
                    pe.wait_ge(lo_sem(u), lo_val(ib, u))
                    for j in range(UJ):
                        jt = u * UJ + j
                        last = mm3(ps[:, ib % 2, :], x0h[:, jt, :], x0l[:, jt, :], ah[:, s, j * BW:(j + 1) * BW],
                                   al[:, s, j * BW:(j + 1) * BW], jt == 0, jt == NT - 1)
                    last.then_inc(sem("unit_used"), 1)
                    if not first:
                        post1(u, ib - 1)

            pass1(0, True)
            with pe.Fori(1, NB) as ib:
                pass1(ib, False)
            for slot in range(NU):
                post1(slot, NB - 1)

            pe.wait_ge(sem("mixer_in"), 16 * 13)
            mixer_after(pe, "norm")
            for hb in range(HB):
                nc.tensor.transpose(ps[:, 2, hb * P:(hb + 1) * P], tn[:, hb, :], ident[:])
            for hb in range(HB):
                last = nc.tensor.matmul(ps[0:1, 3, hb * P:(hb + 1) * P], hrr[:, hb:hb + 1], ident[:], start=True, stop=True)
            mixer_done(last)
            mixer_after(pe, "slices")
            for h in range(HEADS):
                o = HP * (h % 2)
                dst = ps[o:o + HP, 0, (h // 2) * G:(h // 2 + 1) * G]
                nc.tensor.matmul(dst, wfxt[:, h * HP:(h + 1) * HP], slices_t[:, h * G:(h + 1) * G], start=True, stop=False)
                last = nc.tensor.matmul(dst, bfx[0:1, h * HP:(h + 1) * HP], rrow[0:1, h * G:(h + 1) * G],
                                        start=False, stop=True)
            mixer_done(last)
            mixer_after(pe, "st")
            for m in range(6):
                w, c = (P, DI + m * P) if m < 4 else (64, 2 * DI + (m - 4) * 64)
                for kb in range(4):
                    nc.tensor.matmul(ps[0:w, 2, m * 64:(m + 1) * 64], hin[:, kb, c:c + w], st_t[:, kb, 0:64],
                                     start=(kb == 0), stop=(kb == 3))
            for kb in range(4):
                last = nc.tensor.matmul(ps[:, 3, 0:16], st_t[:, kb, :], hin[:, kb, NIN - 16:NIN], start=(kb == 0), stop=(kb == 3))
            mixer_done(last)
            for kb in range(4):
                last = nc.tensor.matmul(ps[0:64, 4, :], st_t[:, kb, 0:64], hin[:, kb, 0:DI], start=(kb == 0), stop=(kb == 3))
            last.then_inc(sem("gate_ps"), 1)
            mixer_after(pe, "silu")
            for mb in range(4):
                nc.tensor.transpose(ps[:, 2, mb * P:(mb + 1) * P], xtd[:, mb, :], ident[:])
            nc.tensor.matmul(ps[:, 7, 0:64], bt[0:64, :], ct[0:64, :], start=True, stop=True)
            for mb in range(4):
                last = nc.tensor.matmul(ps[0:64, 0, 0:HEADS], xtd[:, mb, 0:64], fcdt[:, mb, :], start=(mb == 0), stop=(mb == 3))
            mixer_done(last)
            mixer_after(pe, "spread")
            mixer_done(nc.tensor.matmul(ps[:, 5, :], sameside, decay.rearrange("p h t -> p (h t)"), start=True, stop=True))
            mixer_after(pe, "xdt")
            for h in range(HEADS):
                last = nc.tensor.matmul(ps[0:64, 6, h * HP:(h + 1) * HP], mix[:, h, :], xdt[:, h, :], start=True, stop=True)
            mixer_done(last)
            mixer_after(pe, "gated")
            for b in range(4):
                last = nc.tensor.transpose(ps[:, 2, b * 64:(b + 1) * 64], yy[0:64, b * P:(b + 1) * P], ident[0:64, 0:64])
            mixer_done(last)
            mixer_after(pe, "ygt")
            for ob in range(4):
                for b in range(4):
                    last = nc.tensor.matmul(ps[:, 7, ob * 64:(ob + 1) * 64], hout[:, b, ob * P:(ob + 1) * P], ygt[:, b, :],
                                            start=(b == 0), stop=(b == 3))
            mixer_done(last)
            mixer_after(pe, "ott")
            for h in range(HEADS):
                o = HP * (h % 2)
                last = nc.tensor.matmul(ps[o:o + G, 3, (h // 2) * D:(h // 2 + 1) * D], ott[o:o + HP, h // 2, :],
                                        outwt[o:o + HP, h // 2, :], start=True, stop=True)
            mixer_done(last)
            mixer_after(pe, "msl")

            def deslice(b, par):
                if not isinstance(b, int) or b >= 2:
                    pe.wait_ge(sem("x2_ok"), b - 1)
                for hb in range(HB):
                    last = nc.tensor.matmul(ps[:, par, :], msl[:, hb * D:(hb + 1) * D], sw_t[:, hb, bass.ts(b, BW)],
                                            start=(hb == 0), stop=(hb == HB - 1))
                last.then_inc(sem("out_ps"), 1)

            def x2_transposes(b, par, has_next2):
                pe.wait_ge(sem("x2_ok"), b + 1)
                if not isinstance(b, int) or b >= 2:
                    pe.wait_ge(sem("lc_xn"), b - 1)
                for q in range(TB):
                    last = nc.tensor.transpose(ps[:, 2 + par, q * P:(q + 1) * P], XB[par][:, q * P:(q + 1) * P], ident[:])
                last.then_inc(sem("x2n_ps"), 1)
                if has_next2:
                    deslice(b + 2, par)

            deslice(0, 0)
            deslice(1, 1)
            x2_transposes(0, 0, True)
            x2_transposes(1, 1, True)
            with pe.Fori(1, NB // 2 - 1) as i:
                x2_transposes(2 * i, 0, True)
                x2_transposes(2 * i + 1, 1, True)
            x2_transposes(NB - 2, 0, False)
            x2_transposes(NB - 1, 1, False)

            def post2(slot, b):
                if 1 <= slot <= 3:
                    layer = slot - 1
                    pe.wait_ge(sem("g_ok"), 2 * (3 * b + layer) + 2)
                    nc.tensor.matmul(ps[:, 4, :], mlp[:, layer, :], g1[:], start=True, stop=True).then_inc(sem("mlp_ps"), 1)
                    nc.tensor.matmul(ps[:, 5, :], mlp[:, 3 + layer, :], g2[:], start=True, stop=True).then_inc(sem("mlp_ps"), 1)
                if slot == 4:
                    pe.wait_ge(sem("g_out"), 2 * b + 2)
                    pe.wait_ge(sem("b1_used"), b + 1)
                    nc.tensor.matmul(ps[:, 6, :], mlp[:, 6, :], g1[:], start=True, stop=False)
                    nc.tensor.matmul(ps[:, 6, :], mlp[:, 7, :], g2[:], start=False, stop=True).then_inc(sem("merge_ps"), 1)
                if slot == 5:
                    pe.wait_ge(sem("x3_ok"), b + 1)
                    for q in range(TB):
                        last = nc.tensor.transpose(ps[:, 7, q * P:(q + 1) * P], g2[:, q * P:(q + 1) * P], ident[:])
                    last.then_inc(sem("x3n_ps"), 1)
                if slot == 9:
                    pe.wait_ge(sem("ld_xn"), b + 1)
                    for q in range(TB):
                        last = nc.tensor.transpose(ps[:, 7, q * P:(q + 1) * P], g1[:, q * P:(q + 1) * P], ident[:])
                    last.then_inc(sem("x3t_ps"), 1)
                if slot == 11:
                    pe.wait_ge(sem("x3t_ok"), b + 1)
                    pe.wait_ge(sem("b1_used"), min(b + 2, NB) if isinstance(b, int) else b + 2)
                    for q in range(TB):
                        last = nc.tensor.matmul(ps[:, 6, q * E:(q + 1) * E], g2[:, q * P:(q + 1) * P], wr[:], start=True, stop=True)
                    last.then_inc(sem("router_ps"), 1)
                if slot == 14:
                    pe.wait_ge(sem("w_ok"), b + 1)
                    for q in range(TB):
                        last = nc.tensor.transpose(ps[0:E, 7, q * P:(q + 1) * P], rt[:, q, :], ident[:])
                    last.then_inc(sem("wt_ps"), 1)

            def expert_bias(e):
                pe.wait_ge(sem("m_in"), 32 * (e + 1))
                for hc in range(HC):
                    last = nc.tensor.matmul(ps[:, 6, 64 + hc:65 + hc], m1raw[:, hc * P:(hc + 1) * P],
                                            lngb[:, 1, bass.ts(e, 1)], start=True, stop=True)
                last.then_inc(sem("b1_ps"), 1)

            def pass2(blk, ib, first):
                for u in range(NU):
                    s = u % RING
                    if first:
                        pe.wait_ge(sem("xn_rest"), (UJ * u + UJ - 1) // TB + 1)
                    pe.wait_ge(lo_sem(u), lo_val(blk, u))
                    for j in range(UJ):
                        jt = u * UJ + j
                        mh, ml = ah[:, s, j * BW:(j + 1) * BW], al[:, s, j * BW:(j + 1) * BW]
                        mm3(ps[:, ib % 2, :], x2h[:, jt, :], x2l[:, jt, :], mh, ml, jt == 0, jt == NT - 1)
                        last = mm3(ps[:, 2 + ib % 2, :], xnh[:, jt, :], xnl[:, jt, :], mh, ml, jt == 0, jt == NT - 1)
                    last.then_inc(sem("unit_used"), 1)
                    if not first:
                        post2(u, ib - 1)
                    if u == 7:
                        expert_bias(ib)

            pe.wait_ge(sem("x2_rest"), 1)
            pe.wait_ge(sem("x2_ok"), NB - 1)
            pe.wait_ge(sem("lc_xn"), NB - 1)
            pass2(NB, 0, True)
            pe.wait_ge(sem("x2_ok"), NB)
            pe.wait_ge(sem("lc_xn"), NB)
            pe.wait_ge(sem("mlp_in"), 16)
            with pe.Fori(1, NB) as ib:
                pass2(ib + NB, ib, False)

            def tail(part):
                b, bank = NB - 1, ps[:, 7, :]
                if part.startswith("layer"):
                    i, second = int(part[6]), part.endswith("second")
                    if i == 2 and second:
                        pe.wait_ge(sem("g_out"), 2 * b + 1)
                    else:
                        pe.wait_ge(sem("g_ok"), 6 * b + 2 * i + 2 + second)
                    nc.tensor.matmul(bank, mlp[:, 3 * second + i, :], (g2 if second else g1)[:], start=True, stop=True)\
                        .then_inc(sem("mlp_ps"), 1)
                if part == "merge":
                    pe.wait_ge(sem("g_out"), 2 * b + 2)
                    nc.tensor.matmul(bank, mlp[:, 6, :], g1[:], start=True, stop=False)
                    nc.tensor.matmul(bank, mlp[:, 7, :], g2[:], start=False, stop=True).then_inc(sem("merge_ps"), 1)
                if part == "turn":
                    pe.wait_ge(sem("x3_ok"), b + 1)
                    transposes(g2, 7, "x3n_ps")
                if part == "turn back":
                    pe.wait_ge(sem("ld_xn"), b + 1)
                    transposes(g1, 7, "x3t_ps")
                if part == "route":
                    pe.wait_ge(sem("x3t_ok"), b + 1)
                    for q in range(TB):
                        last = nc.tensor.matmul(ps[:, 7, q * E:(q + 1) * E], g2[:, q * P:(q + 1) * P], wr[:], start=True, stop=True)
                    last.then_inc(sem("router_ps"), 1)
                if part == "turn weights":
                    pe.wait_ge(sem("w_ok"), b + 1)
                    for q in range(TB):
                        last = nc.tensor.transpose(ps[0:E, 7, q * P:(q + 1) * P], rt[:, q, :], ident[:])
                    last.then_inc(sem("wt_ps"), 1)

            def up(b, k):
                e, hc = divmod(k, HC)
                if k >= 4 or not isinstance(b, int) or b > 0:
                    pe.wait_ge(sem("gelu_ok"), STEPS * b + k - 3)
                if k == 0:
                    pe.wait_ge(sem("mx_rest"), b + 1)
                cols = bass.ts(b, BW)
                w = slice(hc * P, (hc + 1) * P)
                mm3(ps[:, k % 4, :], m1h[:, e, w], m1l[:, e, w], mxh[:, cols], mxl[:, cols], True, True)\
                    .then_inc(sem("up_ps"), 1)

            def down(b, k):
                e, hc = divmod(k, HC)
                pe.wait_ge(sem("gelu_rest"), STEPS * b + k + 1)
                if hc == 0 and (not isinstance(b, int) or b > 0 or e >= 2):
                    pe.wait_ge(sem("weighted"), E * b + e - 1)
                mm3(ps[:, 4 + e % 2, :], m2h[:, e, hc, :], m2l[:, e, hc, :], geh[:, k % 4, :], gelo[:, k % 4, :],
                    hc == 0, hc == HC - 1).then_inc(sem("down_used"), 1)

            def experts(b, last_block, parts=()):
                for k in range(STEPS):
                    if k + 3 < STEPS:
                        up(b, k + 3)
                    elif not last_block:
                        up(b + 1, k + 3 - STEPS)
                    if k in parts:
                        tail(parts[k])
                    down(b, k)

            pe.wait_ge(sem("m1_rest"), E)
            pe.wait_ge(sem("m2_rest"), E)
            pe.wait_ge(sem("b1_used"), E)
            pe.wait_ge(sem("wt_ok"), NB - 1)
            pe.wait_ge(sem("g_ok"), 6 * (NB - 1) + 2)
            for k in range(3):
                up(0, k)
            experts(0, False, PE_TAIL)
            with pe.Fori(1, NB - 1) as b:
                experts(b, False)
            experts(NB - 1, True)

        @block.scalar
        def _(act):
            nc.scalar.preload_act_table_set("natural_log_exp_and_others")
            ln_guess(act, 0, "la", ve[:], r0[:])
            act.wait_ge(sem("la_shift"), 1)
            for q in range(TB):
                last = nc.scalar.activation(h_n[:, q, :], x_n[:, q, :], ACT.Identity, bias=nmr[:, q:q + 1], scale=rs[:, q:q + 1])
            last.then_inc(sem("la_xn"), 1)
            act.wait_ge(sem("w2_in"), 16)
            nc.scalar.activation(w2h[:], w2raw[:], ACT.Copy).then_inc(sem("w2_round"), 1)
            act.wait_ge(sem("wb_ok"), 1)
            nc.scalar.activation(wbh[:], wbf[:], ACT.Copy).then_inc(sem("wb_round"), 1)

            def h_norm(b):
                act.wait_ge(sem("la_shift"), b + 1)
                if not isinstance(b, int) or b > 0:
                    act.wait_ge(sem("h_ps"), b)
                for q in range(TB):
                    last = nc.scalar.activation(h_n[:, q, :], x_n[:, TB * b + q, :], ACT.Identity, bias=nmr[:, q:q + 1],
                                                scale=rs[:, q:q + 1])
                last.then_inc(sem("la_xn"), 1)

            def h_round(b, par):
                act.wait_ge(sem("h_ps"), b + 1)
                nc.scalar.activation(hth[:, par, :], ps[:, 0, :], ACT.Copy).then_inc(sem("ht_round"), 1)

            def x0_round(t, s):
                act.wait_ge(sem("x0_full"), t + 1)
                nc.scalar.activation(x0h[:, t, :], x0f[:, s, :], ACT.Copy).then_inc(sem("x0_round"), 1)

            def basis(b, par, has_next, has_next2):
                act.wait_ge(sem("node_ps"), b + 1)
                nc.scalar.activation(node[:, par].rearrange("p q k -> p (q k)"), ps[:, 0, 0:TB * KG], ACT.Copy)\
                    .then_inc(sem("node_ok"), 1)
                act.wait_ge(sem("node_ok"), b + 1)
                for q in range(TB):
                    act.wait_ge(sem("hw_act"), 2 * (TB * b + q) + 1)
                    if not isinstance(b, int) or b > 0 or q >= 2:
                        act.wait_ge(sem("tree1"), TB * b + q - 1)
                    for i in range(8):
                        k = 8 + i
                        if i == 4:
                            act.wait_ge(sem("hw_act"), 2 * (TB * b + q) + 2)
                        last = nc.scalar.activation(prod[:, q % 2, i, :], ps[:, 5 + i // 4, (i % 4) * D:(i % 4 + 1) * D],
                                                    ACT.Copy, scale=node[:, par, q, k:k + 1])
                        if i % 4 == 3:
                            last.then_inc(sem("prod_ok" if i == 7 else "prod_half"), 1)
                    if not isinstance(b, int) or b > 0 or q >= 2:
                        x0_round(TB * b + q - 2, (q - 2) % TB)
                    if q == 0:
                        act.wait_ge(sem("term_ps"), b + 1)
                        nc.scalar.activation(term_t[:, bass.ts(b, BW)], ps[:, 2, :], ACT.Copy).then_inc(sem("term_ok"), 1)
                        if has_next:
                            h_norm(b + 1)
                    if q == 1 and has_next:
                        h_round(b + 1, 1 - par)
                    if q == 3 and has_next2:
                        ln_guess(act, b + 2, "la", ve[:], r0[:])

            h_round(0, 0)
            ln_guess(act, 1, "la", ve[:], r0[:])
            basis(0, 0, True, True)
            with act.Fori(0, NB // 2 - 2) as i:
                basis(2 * i + 1, 1, True, True)
                basis(2 * i + 2, 0, True, True)
            basis(NB - 3, 1, True, True)
            basis(NB - 2, 0, True, False)
            basis(NB - 1, 1, False, False)
            for u in range(LEAD - 1):
                split_act(act, 0, u)
            x0_round(NT - 2, 2)
            x0_round(NT - 1, 3)

            def post1(slot, b):
                if slot == 1:
                    act.wait_ge(sem("x1_ok"), b + 1)
                    nc.scalar.activation(res[:, bass.ts(b, BW)], xn_t[:], ACT.Copy).then_inc(sem("res1_ok"), 1)
                if slot == 1:
                    ln_guess(act, b, "lb", ve[:], r0[:])
                if slot == 4:
                    act.wait_ge(sem("xnt_ps"), b + 1)
                    act.wait_ge(sem("res1_ok"), b + 1)
                    nc.scalar.activation(xn_t[:], ps[:, 2, :], ACT.Copy).then_inc(sem("xnt_ok"), 1)
                if 7 <= slot < 11:
                    q = slot - 7
                    act.wait_ge(sem("lg_sub"), TB * b + q + 1)
                    nc.scalar.activation(lg[:, q, :], lg[:, q, :], ACT.Exp).then_inc(sem("lg_exp"), 1)
                if 12 <= slot < 16:
                    q = slot - 12
                    act.wait_ge(sem("swt_ps"), TB * b + q + 1)
                    nc.scalar.activation(sw_t[:, :, bass.ts(b * TB + q, P)],
                                         ps[:, 5, :].rearrange("p (h n) -> p h n", h=HB), ACT.Copy).then_inc(sem("swt_ok"), 1)

            def pass1(ib, first, last):
                for u in range(NU):
                    nxt = after(ib, u, LEAD)
                    if u + LEAD < NU or not last:
                        split_act(act, *nxt)
                    if not first:
                        post1(u, ib - 1)

            split_act(act, 0, LEAD - 1)
            pass1(0, True, False)
            with act.Fori(1, NB - 1) as ib:
                pass1(ib, False, False)
            pass1(NB - 1, False, True)
            for slot in range(NU):
                post1(slot, NB - 1)

            act.wait_ge(sem("alog_min"), 1)
            nc.scalar.activation(hea, hvec[:, 1, :], ACT.Exp).then_inc(sem("alog_exp"), 1)
            mixer_after(act, "tap2")
            nc.scalar.activation(xe[:, 0:4, :], xc[:, 0:4, :], ACT.Exp, scale=-1.0)
            mixer_done(nc.scalar.activation(xe[0:64, 4:6, :], xc[0:64, 4:6, :], ACT.Exp, scale=-1.0))
            act.wait_ge(sem("gate_ps"), 1)
            nc.scalar.activation(ze[0:64, :], ps[0:64, 4, :], ACT.Exp, scale=-1.0).then_inc(sem("gate_exp"), 1)
            mixer_after(act, "dt_neg")
            mixer_done(nc.scalar.activation(dtn, dtn, ACT.Exp, scale=-1.0))
            mixer_after(act, "dt_plus")
            mixer_done(nc.scalar.activation(dtl, dtn, ACT.Ln))
            mixer_after(act, "dt_a_min")
            mixer_done(nc.scalar.activation(dta, dta, ACT.Exp, scale=-1.0))
            mixer_after(act, "gated_raw")
            mixer_done(nc.scalar.activation(ze[0:64, :], yy[0:64, :], ACT.Square, accum_out=hss[0:64, :]))
            mixer_after(act, "ms")
            mixer_done(nc.scalar.activation(hln[0:64, :], hms[0:64, :], ACT.Ln))
            mixer_after(act, "ms_ln")
            mixer_done(nc.scalar.activation(hr0[0:64, :], hln[0:64, :], ACT.Exp, scale=-0.5))
            act.wait_ge(sem("sums_ok"), NB)
            nc.scalar.activation(x2h[:], x2raw[:], ACT.Copy).then_inc(sem("x2_round"), 1)

            def norm2(b, par):
                ln_guess(act, b, "lc", ve[:], r0[:])
                act.wait_ge(sem("lc_shift"), b + 1)
                if not isinstance(b, int) or b >= 2:
                    act.wait_ge(sem("xn_rest"), b - 1)
                for q in range(TB):
                    cols = slice(q * P, (q + 1) * P)
                    last = nc.scalar.activation(XNB[par][:, cols], ps[:, 2 + par, cols], ACT.Identity, bias=r3[:, q:q + 1],
                                                scale=rs[:, q:q + 1])
                last.then_inc(sem("lc_xn"), 1)
                act.wait_ge(sem("lc_xn"), b + 1)
                nc.scalar.activation(xnh[:, bass.ts(b, TB), :], XNB[par][:].rearrange("p (t d) -> p t d", t=TB), ACT.Copy)\
                    .then_inc(sem("xn_round"), 1)

            act.wait_ge(sem("x2_rest"), 1)
            for u in range(LEAD - 1):
                split_act(act, NB, u)
            norm2(0, 0)
            norm2(1, 1)
            with act.Fori(1, NB // 2) as i:
                norm2(2 * i, 0)
                norm2(2 * i + 1, 1)

            def post2(slot, b):
                if slot == 0:
                    act.wait_ge(sem("unit_used"), NU * NB + NU * (b + 1))
                    if not isinstance(b, int) or b > 0:
                        act.wait_ge(sem("xn_stored"), 16 * b)
                        act.wait_ge(sem("w_stored"), 16 * b)
                    nc.scalar.activation(g1[:], ps[:, 2 + b % 2, :], ACT.Copy, scale=epsb[:, 0:1]).then_inc(sem("g_ok"), 1)
                    nc.scalar.activation(g2[:], ps[:, b % 2, :], ACT.Copy, scale=epsb[:, 1:2]).then_inc(sem("g_ok"), 1)
                if 1 <= slot <= 3:
                    i = slot - 1
                    name = "g_out" if i == 2 else "g_ok"
                    act.wait_ge(sem("mlp_ps"), 6 * b + 2 * i + 1)
                    nc.scalar.activation(g1[:], ps[:, 4, :], ACT.Relu, bias=gbias[:, i:i + 1]).then_inc(sem(name), 1)
                    act.wait_ge(sem("mlp_ps"), 6 * b + 2 * i + 2)
                    nc.scalar.activation(g2[:], ps[:, 5, :], ACT.Relu, bias=gbias[:, 3 + i:4 + i]).then_inc(sem(name), 1)
                if slot == 6:
                    ln_guess(act, b, "ld", ve[:], r0[:])
                if slot == 7:
                    ln_guess(act, b, "le", r4[:], r5[:])
                if slot == 10:
                    act.wait_ge(sem("x3t_ps"), b + 1)
                    act.wait_ge(sem("res3_ok"), b + 1)
                    nc.scalar.activation(g2[:], ps[:, 7, :], ACT.Copy).then_inc(sem("x3t_ok"), 1)
                    act.wait_ge(sem("x3t_ok"), b + 1)
                    act.dma_start(scratch_xn[:, bass.ts(b, BW)], g2[:]).then_inc(sem("xn_stored"), 16)
                if slot == 12:
                    act.wait_ge(sem("router_sub"), b + 1)
                    nc.scalar.activation(rt[:], rt[:], ACT.Exp).then_inc(sem("router_exp"), 1)
                if slot == 15:
                    act.wait_ge(sem("wt_ok"), b + 1)
                    act.dma_start(scratch_w[:, bass.ts(b, BW)], g1[0:E, :]).then_inc(sem("w_stored"), 16)

            def pass2(blk, ib, first, last):
                for u in range(NU):
                    nxt = after(blk, u, LEAD)
                    if u + LEAD < NU or not last:
                        split_act(act, *nxt)
                    if not first:
                        post2(u, ib - 1)
                    if u == 8:
                        act.wait_ge(sem("m_in"), 32 * (ib + 1))
                        nc.scalar.activation(m2h[:, ib, :, :], m2raw[:].rearrange("p (c d) -> p c d", c=HC), ACT.Copy)\
                            .then_inc(sem("m2_round"), 1)

            act.wait_ge(sem("out_ps"), NB)
            act.wait_ge(sem("small_in"), 16 * 13)
            act.wait_ge(sem("eps_ok"), 1)
            split_act(act, NB, LEAD - 1)
            pass2(NB, 0, True, False)
            with act.Fori(1, NB - 1) as ib:
                pass2(ib + NB, ib, False, False)
            pass2(2 * NB - 1, NB - 1, False, True)
            post2(0, NB - 1)

            def tail(part):
                b, bank = NB - 1, ps[:, 7, :]
                if part.startswith("layer"):
                    i, second = int(part[6]), part.endswith("second")
                    act.wait_ge(sem("mlp_ps"), 6 * b + 2 * i + 1 + second)
                    nc.scalar.activation((g2 if second else g1)[:], bank, ACT.Relu, bias=gbias[:, 3 * second + i:3 * second + i + 1])\
                        .then_inc(sem("g_out" if i == 2 else "g_ok"), 1)
                if part == "keep normed":
                    post2(10, b)
                if part == "exponentials":
                    post2(12, b)
                if part == "store weights":
                    post2(15, b)

            def mx_round(b):
                act.wait_ge(sem("xnr_in"), 16 * (b + 1))
                nc.scalar.activation(mxh[:, bass.ts(b, BW)], xnr[:], ACT.Copy).then_inc(sem("mx_round"), 1)

            def gelu(b, k):
                act.wait_ge(sem("up_ps"), STEPS * b + k + 1)
                if k >= 4 or not isinstance(b, int) or b > 0:
                    act.wait_ge(sem("gelu_rest"), STEPS * b + k - 3)
                nc.scalar.activation(gel[:, k % 4, :], ps[:, k % 4, :], ACT.Gelu, bias=b1c[:, k:k + 1]).then_inc(sem("gelu_ok"), 1)

            def gelu_round(k):
                act.wait_ge(sem("gelu_ok"), k + 1)
                if k >= 4:
                    act.wait_ge(sem("down_used"), k - 3)
                nc.scalar.activation(geh[:, k % 4, :], gel[:, k % 4, :], ACT.Copy).then_inc(sem("gelu_round_act"), 1)

            def experts(b, last_block, parts=()):
                for k in range(STEPS):
                    if k + 2 < STEPS:
                        gelu(b, k + 2)
                        if parts and k % 2 == 1:
                            gelu_round(k + 2)
                    elif not last_block:
                        gelu(b + 1, k + 2 - STEPS)
                    if k in parts:
                        tail(parts[k])
                    if k == 16 and not last_block:
                        mx_round(b + 1)

            act.wait_ge(sem("unit_used"), 2 * NU * NB)
            act.wait_ge(sem("b1_used"), E)
            mx_round(0)
            gelu(0, 0)
            gelu(0, 1)
            gelu_round(1)
            experts(0, False, ACT_TAIL)
            with act.Fori(1, NB - 1) as b:
                experts(b, False)
            experts(NB - 1, True)

        @block.vector
        def _(dve):
            nc.vector.memset(sums[:], 0.0).then_inc(sem("sums_ok0"), 1)
            nc.vector.memset(xn_n[:, :, D:TW], 1.0).then_inc(sem("ones_ok"), 1)

            def la_norm(b, part):
                if part == 0:
                    ln_stats(dve, b, lambda q: x_n[:, b * TB + q, :], "la")
                else:
                    ln_newton(dve, b, "la", ve[:], r0[:], r1[:], r2[:], rs[:])
                    nc.vector.scalar_tensor_tensor(nmr[:], mv[:, :, 0], -1.0, rs[:], ALU.mult, ALU.mult).then_inc(sem("la_shift"), 1)

            dve.wait_ge(sem("x_in0"), 16)
            la_norm(0, 0)
            dve.wait_ge(sem("prep_in"), 16 * 7)
            nc.vector.tensor_copy(bxb[:], bxc[:].unsqueeze(2).to_broadcast([P, HB, P])).then_inc(sem("bias_cols"), 1)
            nc.vector.tensor_scalar(itemp[:], tempb[:], 1e-6, None, ALU.max).then_inc(sem("temp_max"), 1)
            dve.wait_ge(sem("temp_max"), 1)
            nc.vector.reciprocal(itemp[:], itemp[:]).then_inc(sem("itemp"), 1)
            dve.wait_ge(sem("itemp"), 1)
            la_norm(0, 1)
            def heads(ap):
                return ap.rearrange("p (h g) -> p h g", h=HEADS)

            def fold():
                dve.wait_ge(sem("fold_ps"), 1)
                for r in range(2):
                    def every2(ap):
                        return ap.rearrange("p (i r g) -> p i r g", r=2, g=G)[:, :, r, :]

                    def bank(pair):
                        return ps[:, pair[r], 0:4 * G].rearrange("p (i g) -> p i g", g=G)

                    nc.vector.tensor_tensor(every2(wc[:]), bank(VBANKS[0]), itemp[:, r::2].unsqueeze(2).to_broadcast([P, 4, G]), ALU.mult)
                    nc.vector.tensor_tensor(every2(cb[:]), bank(VBANKS[1]), bsl[:].unsqueeze(1).to_broadcast([P, 4, G]),
                                            ALU.add).then_inc(sem("cb_sum"), 1)
                dve.wait_ge(sem("cb_sum"), 2)
                nc.vector.tensor_tensor(heads(cb[:]), heads(cb[:]), itemp[:].unsqueeze(2).to_broadcast([P, HEADS, G]), ALU.mult)\
                    .then_inc(sem("prep_done"), 1)

            dve.wait_ge(sem("w2_round"), 1)
            nc.vector.tensor_tensor(w2l[:], w2raw[:], w2h[:].bitcast(F32), ALU.subtract).then_inc(sem("w2_split"), 1)
            dve.wait_ge(sem("wb_ps"), 1)
            nc.vector.tensor_copy(wbf[:], ps[:, 5, 0:P]).then_inc(sem("wb_ok"), 1)
            dve.wait_ge(sem("wb_round"), 1)
            nc.vector.tensor_tensor(wbl[:], wbf[:], wbh[:].bitcast(F32), ALU.subtract).then_inc(sem("wb_rest"), 1)

            def h_rest(b, par):
                dve.wait_ge(sem("ht_round"), b + 1)
                nc.vector.tensor_tensor(htl[:, par, :], ps[:, 0, :], hth[:, par, :].bitcast(F32), ALU.subtract)\
                    .then_inc(sem("ht_rest"), 1)

            def x0_full(t, s):
                dve.wait_ge(sem("acc_sum"), t + 1)
                dve.wait_ge(sem("tree3"), t + 1)
                if not isinstance(t, int) or t > 3:
                    dve.wait_ge(sem("x0_rest"), t - 3)
                nc.vector.tensor_tensor(x0f[:, s, :], acc[:, s % 2, 0, :], part[:, s % 2, 0, :], ALU.add).then_inc(sem("x0_full"), 1)

            def x0_rest(t, s):
                dve.wait_ge(sem("x0_round"), t + 1)
                nc.vector.tensor_tensor(x0l[:, t, :], x0f[:, s, :], x0h[:, t, :].bitcast(F32), ALU.subtract).then_inc(sem("x0_rest"), 1)

            def basis(b, par, has_next, has_next2):
                if has_next:
                    la_norm(b + 1, 1)
                dve.wait_ge(sem("node_ok"), b + 1)
                for q in range(TB):
                    t = TB * b + q
                    if q == 2 and has_next:
                        h_rest(b + 1, 1 - par)
                    if not isinstance(b, int) or b > 0 or q > 1:
                        dve.wait_ge(sem("x0_full"), t - 1)
                    dve.wait_ge(sem("hw_dve"), t + 1)
                    for i in range(4):
                        for c in range(2):
                            k, src, a = 4 * c + i, ps[:, VBANKS[q % 2][c], i * D:(i + 1) * D], acc[:, q % 2, c, :]
                            if i == 0:
                                ins = nc.vector.tensor_scalar(a, src, node[:, par, q, k:k + 1], None, ALU.mult)
                            else:
                                dve.wait_ge(sem(f"chain{c}"), 3 * t + i)
                                ins = nc.vector.scalar_tensor_tensor(a, src, node[:, par, q, k:k + 1], a, ALU.mult, ALU.add)
                            if i < 3:
                                ins.then_inc(sem(f"chain{c}"), 1)
                    ins.then_inc(sem("acc_ok"), 1)
                    if not isinstance(b, int) or b > 0 or q > 2:
                        x0_rest(t - 3, (q - 3) % TB)
                    if not isinstance(b, int) or b > 0 or q > 0:
                        x0_full(t - 1, (q - 1) % TB)
                    if q == 1 and has_next2:
                        la_norm(b + 2, 0)

            h_rest(0, 0)
            fold()
            dve.wait_ge(sem("x_in"), 16)
            la_norm(1, 0)
            basis(0, 0, True, True)
            with dve.Fori(0, NB // 2 - 2) as i:
                basis(2 * i + 1, 1, True, True)
                basis(2 * i + 2, 0, True, True)
            basis(NB - 3, 1, True, True)
            basis(NB - 2, 0, True, False)
            basis(NB - 1, 1, False, False)
            for u in range(LEAD - 1):
                split_rest(dve, nc.vector, 0, u)
            x0_full(NT - 1, 3)
            for t in range(NT - 3, NT):
                x0_rest(t, t % TB)

            def hg(ap):
                return ap.rearrange("p (h g) -> p h g", h=HEADS)

            def post1(slot, b):
                if slot == 0:
                    dve.wait_ge(sem("unit_used"), NU * (b + 1))
                    nc.vector.tensor_tensor(pre[:], ps[:, b % 2, :], term_t[:, bass.ts(b, BW)], ALU.add).then_inc(sem("pre_ok"), 1)
                    dve.wait_ge(sem("pre_ok"), b + 1)
                    nc.vector.scalar_tensor_tensor(xn_t[:], pre[:], 0.0, res[:, bass.ts(b, BW)], ALU.max, ALU.add)\
                        .then_inc(sem("x1_ok"), 1)
                if slot == 1:
                    dve.wait_ge(sem("x1n_ps"), b + 1)
                    ln_stats(dve, b, lambda q: ps[:, 2, q * P:(q + 1) * P], "lb")
                if slot == 2:
                    ln_newton(dve, b, "lb", ve[:], r0[:], r1[:], r2[:], rs[:])
                    ln_apply(lambda q: ps[:, 2, q * P:(q + 1) * P], lambda q: xn_n[:, q, 0:D], rs, "lb_xn")
                if 5 <= slot < 9:
                    q = slot - 5
                    dve.wait_ge(sem("lg_ps"), TB * b + q + 1)
                    nc.vector.tensor_tensor(lg[:, q, :], ps[:, 3 + q % 2, :], cb[:], ALU.add).then_inc(sem("lg_ok"), 1)
                    dve.wait_ge(sem("lg_ok"), TB * b + q + 1)
                    nc.vector.tensor_reduce(smx[:, q, :], hg(lg[:, q, :]), AX, ALU.max).then_inc(sem("lg_max"), 1)
                if 8 <= slot < 12:
                    q = slot - 8
                    dve.wait_ge(sem("lg_exp"), TB * b + q + 1)
                    nc.vector.tensor_reduce(sden[:, q, :], hg(lg[:, q, :]), AX, ALU.add).then_inc(sem("lg_sum"), 1)
                    dve.wait_ge(sem("lg_sum"), TB * b + q + 1)
                    nc.vector.reciprocal(sden[:, q, :], sden[:, q, :]).then_inc(sem("lg_rec"), 1)
                if slot == 15:
                    dve.wait_ge(sem("sums_ps"), TB * (b + 1))
                    for c in range(2):
                        part = sums[:, 2 * c:2 * c + 2, :].rearrange("p a d -> p (a d)")
                        last = nc.vector.tensor_tensor(part, ps[:, 6 + c, 0:2 * TW], part, ALU.add)
                    last.then_inc(sem("sums_ok"), 1)

            def pass1(ib, first, last):
                for u in range(NU):
                    nxt = after(ib, u, LEAD)
                    if u in (0, 2) and not first:
                        post1(u, ib - 1)
                    if u + LEAD < NU or not last:
                        split_rest(dve, nc.vector, *nxt)
                    if u not in (0, 2) and not first:
                        post1(u, ib - 1)

            dve.wait_ge(sem("xt_in"), 16)
            split_rest(dve, nc.vector, 0, LEAD - 1)
            pass1(0, True, False)
            with dve.Fori(1, NB - 1) as ib:
                pass1(ib, False, False)
            pass1(NB - 1, False, True)
            for slot in range(NU):
                post1(slot, NB - 1)

            dve.wait_ge(sem("sums_ok"), NB)
            dve.wait_ge(sem("unit_used"), NU * NB)
            mixer_done(nc.vector.tensor_scalar(hden, sums[:, :, D], EPS, None, ALU.add))
            mixer_after(dve, "den")
            mixer_done(nc.vector.reciprocal(hrden, hden))
            mixer_after(dve, "rden")
            for hb in range(HB):
                nc.vector.tensor_scalar(tn[:, hb, :], sums[:, hb, 0:D], hrden[:, hb:hb + 1], None, ALU.mult)
            mixer_done(nc.vector.tensor_tensor(hrr, sums[:, :, D], hrden, ALU.mult))
            dve.wait_ge(sem("mixer_in"), 16 * 13)
            nc.vector.tensor_scalar(hvec[:, 1, :], hvec[:, 1, :], 88.0, None, ALU.min).then_inc(sem("alog_min"), 1)
            mixer_after(dve, "slices_ps")
            nc.vector.tensor_copy(slices_t[:], ps[:, 2, :])
            mixer_done(nc.vector.tensor_copy(rrow[0:1, :], ps[0:1, 3, :]))
            mixer_after(dve, "st_ps")
            mixer_done(nc.vector.tensor_copy(st_t[:].rearrange("p b (r g) -> p b r g", r=2),
                                             ps[:, 0, 0:256].rearrange("p (b g) -> p b g", b=4).unsqueeze(2)
                                             .to_broadcast([P, 4, 2, G])))
            mixer_after(dve, "in_ps")
            nc.vector.memset(xp[:, :, 0:2], 0.0)
            nc.vector.tensor_copy(xp[:, 0:4, 2:66], ps[:, 2, 0:256].rearrange("p (b g) -> p b g", b=4))
            nc.vector.tensor_copy(xp[0:64, 4:6, 2:66], ps[0:64, 2, 256:384].rearrange("p (b g) -> p b g", b=2))
            nc.vector.tensor_tensor(dtu[0:64, :], ps[0:64, 3, 0:8], hvec[0:64, 0, :], ALU.add)
            mixer_done(nc.vector.tensor_tensor(dtu[64:P, :], ps[64:P, 3, 8:16], hvec[64:P, 0, :], ALU.add))
            for tap, before_step in ((2, "pad"), (1, "tap0"), (0, "tap1")):
                mixer_after(dve, before_step)
                for m in range(6):
                    w = P if m < 4 else 64
                    src, o = xp[0:w, m, tap:tap + 64], xc[0:w, m, :]
                    if tap == 2:
                        last = nc.vector.tensor_scalar(o, src, convw[0:w, m, 2:3], convw[0:w, m, 3:4], ALU.mult, ALU.add)
                    else:
                        last = nc.vector.scalar_tensor_tensor(o, src, convw[0:w, m, tap:tap + 1], o, ALU.mult, ALU.add)
                mixer_done(last)
            mixer_after(dve, "exp")
            nc.vector.tensor_scalar(xe[:, 0:4, :], xe[:, 0:4, :], 1.0, None, ALU.add)
            mixer_done(nc.vector.tensor_scalar(xe[0:64, 4:6, :], xe[0:64, 4:6, :], 1.0, None, ALU.add))
            mixer_after(dve, "plus")
            nc.vector.reciprocal(xe[:, 0:4, :], xe[:, 0:4, :])
            mixer_done(nc.vector.reciprocal(xe[0:64, 4:6, :], xe[0:64, 4:6, :]))
            mixer_after(dve, "recip")
            for r in range(2):
                nc.vector.tensor_tensor(xtd[:, :, r * 64:(r + 1) * 64], xc[:, 0:4, :], xe[:, 0:4, :], ALU.mult)
                nc.vector.tensor_tensor(bt[0:64, r * 64:(r + 1) * 64], xc[0:64, 4, :], xe[0:64, 4, :], ALU.mult)
            mixer_done(nc.vector.tensor_tensor(ct[0:64, :], xc[0:64, 5, :], xe[0:64, 5, :], ALU.mult))
            dve.wait_ge(sem("gate_exp"), 1)
            nc.vector.tensor_scalar(ze[0:64, :], ze[0:64, :], 1.0, None, ALU.add).then_inc(sem("gate_own"), 1)
            dve.wait_ge(sem("gate_own"), 1)
            nc.vector.reciprocal(zs[0:64, :], ze[0:64, :]).then_inc(sem("gate_own"), 1)
            dve.wait_ge(sem("gate_own"), 2)
            nc.vector.tensor_tensor(zs[0:64, :], ps[0:64, 4, :], zs[0:64, :], ALU.mult).then_inc(sem("gate_own"), 1)
            mixer_after(dve, "x_ps")
            mixer_done(nc.vector.scalar_tensor_tensor(dtn, dtu, -1.0, dtu, ALU.mult, ALU.max))
            mixer_after(dve, "dt_exp")
            mixer_done(nc.vector.tensor_scalar(dtn, dtn, 1.0, None, ALU.add))
            mixer_after(dve, "dt_ln")
            mixer_done(nc.vector.scalar_tensor_tensor(dtv, dtu, 0.0, dtl, ALU.max, ALU.add))
            mixer_after(dve, "dt")
            dve.wait_ge(sem("alog_exp"), 1)
            mixer_done(nc.vector.tensor_tensor(dta, hea, dtv, ALU.mult))
            mixer_after(dve, "dt_a")
            mixer_done(nc.vector.tensor_scalar(dta, dta, 200.0, None, ALU.min))
            mixer_after(dve, "keep")
            nc.vector.memset(mix, 0.0)
            mixer_done(nc.vector.tensor_tensor(decay, perm0.unsqueeze(1).to_broadcast([P, HEADS, 64]),
                                               dta.unsqueeze(2).to_broadcast([P, HEADS, 64]), ALU.mult))
            mixer_after(dve, "keep_ps")
            mixer_done(nc.vector.tensor_tensor_scan(scan.rearrange("p h t -> p (h t)"), ps[:, 5, :], rperm, 0.0,
                                                    ALU.mult, ALU.add))
            mixer_after(dve, "scan")
            nc.vector.tensor_tensor(mix[0:64, :, 1:64], scan[0:64, :, 0:63],
                                    ps[0:64, 7, 0:63].unsqueeze(1).to_broadcast([64, HEADS, 63]), ALU.mult)
            nc.vector.tensor_tensor(mix[64:P, :, 0:63], scan[64:P, :, 62::-1],
                                    ps[64:P, 7, 1:64].unsqueeze(1).to_broadcast([64, HEADS, 63]), ALU.mult)
            mixer_done(nc.vector.tensor_tensor(fcs[0:64, :], ps[0:64, 0, 0:8], hvec[0:64, 2, :], ALU.add))
            mixer_after(dve, "skip")
            nc.vector.tensor_tensor(xdt, heads(ps[:, 2, :]), dtv.unsqueeze(2).to_broadcast([P, HEADS, HP]), ALU.mult)
            mixer_done(nc.vector.tensor_tensor(heads(xo[0:64, :]), heads(ps[0:64, 2, :]),
                                               fcs[0:64, :].unsqueeze(2).to_broadcast([64, HEADS, HP]), ALU.mult))
            mixer_after(dve, "y_ps")
            mixer_done(nc.vector.tensor_tensor(yy[0:64, :], ps[0:64, 6, :], xo[0:64, :], ALU.add))
            mixer_after(dve, "y")
            dve.wait_ge(sem("gate_own"), 3)
            mixer_done(nc.vector.tensor_tensor(yy[0:64, :], yy[0:64, :], zs[0:64, :], ALU.mult))
            mixer_after(dve, "square")
            mixer_done(nc.vector.tensor_scalar(hms[0:64, :], hss[0:64, :], 1.0 / DI, EPS, ALU.mult, ALU.add))
            mixer_after(dve, "ms_guess")
            mixer_done(nc.vector.scalar_tensor_tensor(hr1[0:64, :], hr0[0:64, :], -0.5, hr0[0:64, :], ALU.mult, ALU.mult))
            mixer_after(dve, "ms_n1")
            mixer_done(nc.vector.tensor_tensor(hr2[0:64, :], hr1[0:64, :], hms[0:64, :], ALU.mult))
            mixer_after(dve, "ms_n2")
            mixer_done(nc.vector.scalar_tensor_tensor(hrs[0:64, :], hr2[0:64, :], 1.5, hr0[0:64, :], ALU.add, ALU.mult))
            mixer_after(dve, "ms_root")
            mixer_done(nc.vector.tensor_scalar(yy[0:64, :], yy[0:64, :], hrs[0:64, :], None, ALU.mult))
            mixer_after(dve, "gated_ps")
            for b in range(4):
                last = nc.vector.tensor_scalar(ygt[:, b, :], ps[:, 2, b * 64:(b + 1) * 64], normw[:, b:b + 1], None, ALU.mult)
            mixer_done(last)
            mixer_after(dve, "ot_ps")
            mixer_done(nc.vector.tensor_copy(ott.rearrange("p b t -> p (b t)"), ps[:, 7, 0:256]))
            mixer_after(dve, "msl_ps")
            mixer_done(nc.vector.tensor_copy(msl[:], ps[:, 3, :]))
            dve.wait_ge(sem("small_in"), 16 * 13)
            nc.vector.tensor_scalar(epsb[:], epsb[:], 2.0, None, ALU.add).then_inc(sem("eps_ok"), 1)

            def x2_block(b, par):
                dve.wait_ge(sem("out_ps"), b + 1)
                if not isinstance(b, int) or b >= 2:
                    dve.wait_ge(sem("x2n_ps"), b - 1)
                    dve.wait_ge(sem("res2_ok"), b - 1)
                nc.vector.scalar_tensor_tensor(XB[par][:], ps[:, par, :], outb[:], res[:, bass.ts(b, BW)], ALU.add, ALU.add)\
                    .then_inc(sem("x2_ok"), 1)

            def xn_rest(b, par):
                dve.wait_ge(sem("xn_round"), b + 1)
                nc.vector.tensor_tensor(xnl[:, bass.ts(b, TB), :], XNB[par][:].rearrange("p (t d) -> p t d", t=TB),
                                        xnh[:, bass.ts(b, TB), :].bitcast(F32), ALU.subtract).then_inc(sem("xn_rest"), 1)

            def x2_norm(b, par, has_next):
                if has_next:
                    x2_block(b + 1, 1 - par)
                dve.wait_ge(sem("x2n_ps"), b + 1)
                ln_stats(dve, b, lambda q: ps[:, 2 + par, q * P:(q + 1) * P], "lc")
                if not isinstance(b, int) or b > 0:
                    xn_rest(b - 1, 1 - par)
                ln_newton(dve, b, "lc", ve[:], r0[:], r1[:], r2[:], rs[:])
                nc.vector.scalar_tensor_tensor(r3[:], mv[:, :, 0], -1.0, rs[:], ALU.mult, ALU.mult).then_inc(sem("lc_shift"), 1)

            dve.wait_ge(sem("res1_ok"), NB)
            for u in range(LEAD - 1):
                split_rest(dve, nc.vector, NB, u)
            x2_block(0, 0)
            x2_norm(0, 0, True)
            x2_norm(1, 1, True)
            with dve.Fori(1, NB // 2 - 1) as i:
                x2_norm(2 * i, 0, True)
                x2_norm(2 * i + 1, 1, True)
            x2_norm(NB - 2, 0, True)
            x2_norm(NB - 1, 1, False)
            xn_rest(NB - 1, 1)

            def e4(ap):
                return ap.rearrange("p q e -> p (q e)")

            def post2(slot, b, router_bank=6):
                if slot == 5:
                    dve.wait_ge(sem("merge_ps"), b + 1)
                    nc.vector.scalar_tensor_tensor(g2[:], ps[:, 6, :], bmc[:], res[:, bass.ts(b, BW)], ALU.add, ALU.add)\
                        .then_inc(sem("x3_ok"), 1)
                if slot == 6:
                    dve.wait_ge(sem("x3n_ps"), b + 1)
                    ln_stats(dve, b, lambda q: ps[:, 7, q * P:(q + 1) * P], "ld", 12)
                if slot == 7:
                    ln_newton(dve, b, "ld", ve[:], r0[:], r1[:], r2[:], rs[:], per=12)
                    nc.vector.tensor_tensor(r3[:], rs[:], rs[:], ALU.mult).then_inc(sem("ld_own"), 1)
                    own_step(dve, b, "ld", 12, 6)
                    nc.vector.tensor_tensor(r3[:], r3[:], mv[:, :, 1], ALU.mult).then_inc(sem("ld_own"), 1)
                    own_step(dve, b, "ld", 12, 7)
                    nc.vector.tensor_scalar(r4[:], r3[:], EPS, None, ALU.add).then_inc(sem("le_ve"), 1)
                if slot == 8:
                    ln_newton(dve, b, "le", r4[:], r5[:], r6[:], r7[:], r8[:], "ld", 12, 8)
                    nc.vector.tensor_tensor(r6[:], rs[:], r8[:], ALU.mult).then_inc(sem("ld_own"), 1)
                    nc.vector.tensor_tensor(r7[:], r4[:], r8[:], ALU.mult).then_inc(sem("ld_own"), 1)
                    own_step(dve, b, "ld", 12, 12)
                    ln_apply(lambda q: ps[:, 7, q * P:(q + 1) * P], lambda q: g1[:, q * P:(q + 1) * P], r6, "ld_xn")
                if slot == 12:
                    dve.wait_ge(sem("router_ps"), b + 1)
                    pr = ps[:, router_bank, 0:TB * E].rearrange("p (q e) -> p q e", q=TB)
                    nc.vector.tensor_tensor(rt[:], pr, r7[:].unsqueeze(2).to_broadcast([P, TB, E]), ALU.mult).then_inc(sem("router_own"), 1)
                    own_step(dve, b, "router", 12, 1)
                    nc.vector.tensor_tensor(rt[:], rt[:], brb[:].unsqueeze(1).to_broadcast([P, TB, E]), ALU.add).then_inc(sem("router_own"), 1)
                    own_step(dve, b, "router", 12, 2)
                    nc.vector.tensor_reduce(rq[:], rt[:], AX, ALU.max).then_inc(sem("router_own"), 1)
                    own_step(dve, b, "router", 12, 3)
                    nc.vector.tensor_tensor(rt[:], rt[:], rq[:].unsqueeze(2).to_broadcast([P, TB, E]), ALU.subtract)\
                        .then_inc(sem("router_sub"), 1)
                if slot == 13:
                    dve.wait_ge(sem("router_exp"), b + 1)
                    dve.wait_ge(sem("x3t_ok"), b + 1)
                    other = rt[:].unsqueeze(2).to_broadcast([P, TB, E, E])
                    own = rt[:].unsqueeze(3).to_broadcast([P, TB, E, E])
                    gt = ps[:, 7, 0:256].rearrange("p (q e f) -> p q e f", q=TB, e=E)
                    eq = ps[:, 7, 256:512].rearrange("p (q e f) -> p q e f", q=TB, e=E)
                    lowb = low[:].rearrange("p (e f) -> p e f", e=E).unsqueeze(1).to_broadcast([P, TB, E, E])
                    nc.vector.tensor_tensor(gt, other, own, ALU.is_gt).then_inc(sem("router_own"), 1)
                    nc.vector.tensor_tensor(eq, other, own, ALU.is_equal).then_inc(sem("router_own"), 1)
                    own_step(dve, b, "router", 12, 4)
                    nc.vector.tensor_reduce(rkg[:], gt, AX, ALU.add).then_inc(sem("router_own"), 1)
                    own_step(dve, b, "router", 12, 5)
                    nc.vector.tensor_tensor(eq, eq, lowb, ALU.mult).then_inc(sem("router_own"), 1)
                    own_step(dve, b, "router", 12, 7)
                    nc.vector.tensor_reduce(rke[:], eq, AX, ALU.add).then_inc(sem("router_own"), 1)
                    own_step(dve, b, "router", 12, 8)
                    own_step(dve, b, "router", 12, 6)
                    nc.vector.tensor_tensor(rkg[:], rkg[:], rke[:], ALU.add).then_inc(sem("router_own"), 1)
                    own_step(dve, b, "router", 12, 9)
                    nc.vector.scalar_tensor_tensor(e4(rt[:]), e4(rkg[:]), 2.0, e4(rt[:]), ALU.is_lt, ALU.mult).then_inc(sem("router_own"), 1)
                    own_step(dve, b, "router", 12, 10)
                    nc.vector.tensor_reduce(rq[:], rt[:], AX, ALU.add).then_inc(sem("router_own"), 1)
                    own_step(dve, b, "router", 12, 11)
                    nc.vector.reciprocal(rq[:], rq[:]).then_inc(sem("router_own"), 1)
                    own_step(dve, b, "router", 12, 12)
                    nc.vector.tensor_tensor(rt[:], rt[:], rq[:].unsqueeze(2).to_broadcast([P, TB, E]), ALU.mult).then_inc(sem("w_ok"), 1)
                if slot == 15:
                    dve.wait_ge(sem("wt_ps"), b + 1)
                    nc.vector.tensor_copy(g1[0:E, :], ps[0:E, 7, :]).then_inc(sem("wt_ok"), 1)

            def expert_weights(e):
                dve.wait_ge(sem("m_in"), 32 * (e + 1))
                g = lngb[:, 0, bass.ts(e, 1)]
                nc.vector.tensor_scalar(m1h[:, e, :], m1raw[:], g, None, ALU.mult).then_inc(sem("m1_round"), 1)
                dve.wait_ge(sem("m1_round"), e + 1)
                nc.vector.scalar_tensor_tensor(m1l[:, e, :], m1raw[:], g, m1h[:, e, :].bitcast(F32), ALU.mult, ALU.subtract)\
                    .then_inc(sem("m1_rest"), 1)
                dve.wait_ge(sem("m2_round"), e + 1)
                nc.vector.tensor_tensor(m2l[:, e, :, :], m2raw[:].rearrange("p (c d) -> p c d", c=HC),
                                        m2h[:, e, :, :].bitcast(F32), ALU.subtract).then_inc(sem("m2_rest"), 1)
                dve.wait_ge(sem("b1_ps"), e + 1)
                nc.vector.tensor_tensor(b1c[:, bass.ts(e, HC)], ps[:, 6, 64:64 + HC], b1c[:, bass.ts(e, HC)], ALU.add)\
                    .then_inc(sem("b1_used"), 1)

            def pass2(blk, ib, first, last):
                for u in range(NU):
                    nxt = after(blk, u, LEAD)
                    early = u in (5, 7, 8)
                    if early and not first:
                        post2(u, ib - 1)
                    if u + LEAD < NU or not last:
                        split_rest(dve, nc.vector, *nxt)
                    if not early and not first:
                        post2(u, ib - 1)
                    if u == 10:
                        expert_weights(ib)

            dve.wait_ge(sem("res2_ok"), NB)
            split_rest(dve, nc.vector, NB, LEAD - 1)
            pass2(NB, 0, True, False)
            with dve.Fori(1, NB - 1) as ib:
                pass2(ib + NB, ib, False, False)
            pass2(2 * NB - 1, NB - 1, False, True)

            def step(ins, count):
                ins.then_inc(sem("tail_own"), 1)
                dve.wait_ge(sem("tail_own"), count)

            def root_newton(v, out, t1, t2, count):
                step(nc.vector.tensor_scalar(out.bitcast(I32), v.bitcast(I32), 1, None, ALU.logical_shift_right), count + 1)
                step(nc.vector.tensor_scalar(out.bitcast(I32), out.bitcast(I32), -1, 0x5f3759df, ALU.mult, ALU.add), count + 2)
                for i in range(3):
                    c = count + 3 + 3 * i
                    step(nc.vector.scalar_tensor_tensor(t1, out, -0.5, out, ALU.mult, ALU.mult), c)
                    step(nc.vector.tensor_tensor(t2, t1, v, ALU.mult), c + 1)
                    step(nc.vector.scalar_tensor_tensor(out, t2, 1.5, out, ALU.add, ALU.mult), c + 2)

            def tail(part):
                b, bank = NB - 1, ps[:, 7, :]
                if part == "merge":
                    dve.wait_ge(sem("merge_ps"), b + 1)
                    nc.vector.scalar_tensor_tensor(g2[:], bank, bmc[:], res[:, b * BW:N], ALU.add, ALU.add).then_inc(sem("x3_ok"), 1)
                if part == "statistics":
                    dve.wait_ge(sem("x3n_ps"), b + 1)
                    ln_stats(dve, b, lambda q: ps[:, 7, q * P:(q + 1) * P], "ld", 12)
                if part == "root":
                    dve.wait_ge(sem("ld_ve"), b + 1)
                    root_newton(ve[:], rs[:], r1[:], r2[:], 0)
                if part == "second variance":
                    step(nc.vector.tensor_tensor(r3[:], rs[:], rs[:], ALU.mult), 12)
                    step(nc.vector.tensor_tensor(r3[:], r3[:], mv[:, :, 1], ALU.mult), 13)
                    step(nc.vector.tensor_scalar(r4[:], r3[:], EPS, None, ALU.add), 14)
                if part == "second root":
                    root_newton(r4[:], r8[:], r6[:], r7[:], 14)
                if part == "norm":
                    step(nc.vector.tensor_tensor(r6[:], rs[:], r8[:], ALU.mult), 26)
                    step(nc.vector.tensor_tensor(r7[:], r4[:], r8[:], ALU.mult), 27)
                    ln_apply(lambda q: ps[:, 7, q * P:(q + 1) * P], lambda q: g1[:, q * P:(q + 1) * P], r6, "ld_xn")
                if part == "route":
                    post2(12, b, 7)
                if part == "choose":
                    post2(13, b)
                if part == "keep weights":
                    post2(15, b)

            def split(b, k):
                dve.wait_ge(sem("gelu_ok"), STEPS * b + k + 1)
                if k >= 4 or not isinstance(b, int) or b > 0:
                    dve.wait_ge(sem("down_used"), STEPS * b + k - 3)
                if isinstance(b, int) and b == 0 and k % 2 == 1:
                    dve.wait_ge(sem("gelu_round_act"), k // 2 + 1)
                else:
                    nc.vector.tensor_copy(geh[:, k % 4, :], gel[:, k % 4, :]).then_inc(sem("gelu_round"), 1)
                    dve.wait_ge(sem("gelu_round"), STEPS * b + k + 1 - STEPS // 2 if not (isinstance(b, int) and b == 0) else k // 2 + 1)
                nc.vector.tensor_tensor(gelo[:, k % 4, :], gel[:, k % 4, :], geh[:, k % 4, :].bitcast(F32), ALU.subtract)\
                    .then_inc(sem("gelu_rest"), 1)

            def weigh(b, e):
                dve.wait_ge(sem("down_used"), STEPS * b + HC * (e + 1))
                if e == 0:
                    dve.wait_ge(sem("wb_in"), 16 * (b + 1))
                if e >= 2:
                    dve.wait_ge(sem("added"), (E - 1) * b + max(1, e - 2))
                elif not isinstance(b, int) or b > 0:
                    dve.wait_ge(sem("added"), (E - 1) * b)
                ins = nc.vector.scalar_tensor_tensor(wy[:, e % 2, :], ps[:, 4 + e % 2, :], b2c[:, e:e + 1], wb[:, b % 2, e, :],
                                                     ALU.add, ALU.mult)
                if e == 0:
                    ins.then_inc(sem("first_own"), 1)
                    dve.wait_ge(sem("first_own"), b + 1)
                    ins = nc.vector.tensor_tensor(wy[:, 0, :], res[:, bass.ts(b, BW)], wy[:, 0, :], ALU.add)
                ins.then_inc(sem("weighted"), 1)

            def mx_rest(b):
                dve.wait_ge(sem("mx_round"), b + 1)
                nc.vector.tensor_tensor(mxl[:, bass.ts(b, BW)], xnr[:], mxh[:, bass.ts(b, BW)].bitcast(F32), ALU.subtract)\
                    .then_inc(sem("mx_rest"), 1)

            def experts(b, last_block, parts=()):
                for k in range(STEPS):
                    if k + 2 < STEPS:
                        split(b, k + 2)
                    elif not last_block:
                        split(b + 1, k + 2 - STEPS)
                    if k in parts:
                        tail(parts[k])
                    if k % HC == HC - 1:
                        weigh(b, k // HC)
                    if k == 17 and not last_block:
                        mx_rest(b + 1)

            dve.wait_ge(sem("res3_ok"), NB - 1)
            mx_rest(0)
            split(0, 0)
            split(0, 1)
            experts(0, False, DVE_TAIL)
            dve.wait_ge(sem("res3_ok"), NB)
            with dve.Fori(1, NB - 1) as b:
                experts(b, False)
            experts(NB - 1, True)

        @block.gpsimd
        def _(pool):
            def tree(b):
                for q in range(TB):
                    t, s = TB * b + q, q % 2
                    pool.wait_ge(sem("prod_ok"), t + 1)
                    if not isinstance(b, int) or b > 0 or q > 1:
                        pool.wait_ge(sem("x0_full"), t - 1)
                    nc.gpsimd.tensor_tensor(part[:, s], prod[:, s, 0:4, :], prod[:, s, 4:8, :], ALU.add).then_inc(sem("tree1"), 1)
                    pool.wait_ge(sem("tree1"), t + 1)
                    nc.gpsimd.tensor_tensor(part[:, s, 0:2, :], part[:, s, 0:2, :], part[:, s, 2:4, :], ALU.add).then_inc(sem("tree2"), 1)
                    pool.wait_ge(sem("acc_ok"), t + 1)
                    nc.gpsimd.tensor_tensor(acc[:, s, 0, :], acc[:, s, 0, :], acc[:, s, 1, :], ALU.add).then_inc(sem("acc_sum"), 1)
                    pool.wait_ge(sem("tree2"), t + 1)
                    nc.gpsimd.tensor_tensor(part[:, s, 0, :], part[:, s, 0, :], part[:, s, 1, :], ALU.add).then_inc(sem("tree3"), 1)

            tree(0)
            with pool.Fori(1, NB) as b:
                tree(b)

            def post1(slot, b):
                if 6 <= slot < 10:
                    q = slot - 6
                    pool.wait_ge(sem("lg_max"), TB * b + q + 1)
                    nc.gpsimd.tensor_tensor(hg(lg[:, q, :]), hg(lg[:, q, :]), smx[:, q, :].unsqueeze(2).to_broadcast([P, HEADS, G]),
                                            ALU.subtract).then_inc(sem("lg_sub"), 1)
                if 9 <= slot < 13:
                    q = slot - 9
                    pool.wait_ge(sem("lg_rec"), TB * b + q + 1)
                    nc.gpsimd.tensor_tensor(hg(lg[:, q, :]), hg(lg[:, q, :]), sden[:, q, :].unsqueeze(2).to_broadcast([P, HEADS, G]),
                                            ALU.mult).then_inc(sem("sw_ok"), 1)

            def hg(ap):
                return ap.rearrange("p (h g) -> p h g", h=HEADS)

            def pass1(ib, first, last):
                for u in range(NU):
                    nxt = after(ib, u, LEAD)
                    if u + LEAD < NU or not last:
                        split_rest(pool, nc.gpsimd, *nxt)
                    if not first:
                        post1(u, ib - 1)

            pass1(0, True, False)
            with pool.Fori(1, NB - 1) as ib:
                pass1(ib, False, False)
            pass1(NB - 1, False, True)
            for slot in range(NU):
                post1(slot, NB - 1)

            pool.wait_ge(sem("x2_round"), 1)
            nc.gpsimd.tensor_tensor(x2l[:], x2raw[:], x2h[:].bitcast(F32), ALU.subtract).then_inc(sem("x2_rest"), 1)

            def keep(b, par):
                pool.wait_ge(sem("x2_ok"), b + 1)
                nc.gpsimd.tensor_copy(res[:, bass.ts(b, BW)], XB[par][:]).then_inc(sem("res2_ok"), 1)

            with pool.Fori(0, NB // 2) as i:
                keep(2 * i, 0)
                keep(2 * i + 1, 1)

            def post2(slot, b):
                if slot == 6:
                    pool.wait_ge(sem("x3_ok"), b + 1)
                    nc.gpsimd.tensor_copy(res[:, bass.ts(b, BW)], g2[:]).then_inc(sem("res3_ok"), 1)

            def pass2(blk, ib, first, last):
                for u in range(NU):
                    nxt = after(blk, u, LEAD)
                    if u + LEAD < NU or not last:
                        split_rest(pool, nc.gpsimd, *nxt)
                    if not first:
                        post2(u, ib - 1)

            pass2(NB, 0, True, False)
            with pool.Fori(1, NB - 1) as ib:
                pass2(ib + NB, ib, False, False)
            pass2(2 * NB - 1, NB - 1, False, True)

            def add(b):
                for e in range(1, E):
                    if isinstance(b, int) and b == 0 and e == 2:
                        post2(6, NB - 1)
                    pool.wait_ge(sem("weighted"), E * b + e + 1)
                    if e > 1:
                        pool.wait_ge(sem("added"), (E - 1) * b + e - 1)
                    elif not isinstance(b, int) or b > 0:
                        pool.wait_ge(sem("out_done"), 16 * b)
                    nc.gpsimd.tensor_tensor(total[:], wy[:, 0, :] if e == 1 else total[:], wy[:, e % 2, :], ALU.add)\
                        .then_inc(sem("added"), 1)

            add(0)
            with pool.Fori(1, NB) as b:
                add(b)


def kernel(**inputs):
    import numpy as np
    import concourse.bacc as bacc
    from concourse.bass_utils import run_bass_kernel_spmd

    v = {k: np.asarray(a) for k, a in inputs.items()}
    same = lambda a: np.ascontiguousarray(a)
    f = "L0_ffn_"
    conv = np.zeros((P, 6, 4), np.float32)
    for m in range(6):
        w, c = (P, m * P) if m < 4 else (64, DI + (m - 4) * 64)
        conv[:w, m, 0:3] = v[f + "hy_conv_w"][c:c + w]
        conv[:w, m, 3] = v[f + "hy_conv_b"][c:c + w]
    r = np.arange(P)
    step = np.where(r < 64, r, P - 1 - r)
    own = (step[:, None] == np.arange(64)[None, :]).astype(np.float32)
    first_off = own.copy()
    first_off[:, 0] = 0
    side = (r[:, None] // 64 == r[None, :] // 64).astype(np.float32)
    low = np.tile(np.tril(np.ones((E, E), np.float32), -1).reshape(1, 64), (P, 1))
    cst = np.concatenate([np.eye(P, dtype=np.float32), np.tile(own, (1, HEADS)), first_off, side, low], 1)
    arrays = {
        "x": same(v["x"]), "xt": same(v["x"].T),
        "adjt": same(v["adj"].reshape(NB, BW, NU, UJ, P).transpose(0, 2, 4, 3, 1)).reshape(NB, NU, P, UW),
        "cst": cst,
        "w2": same(np.concatenate([v["L0_gnn_W2"].transpose(1, 0, 2).reshape(D, KG * D), v["L0_gnn_W1"]], 1)),
        "w1t": same(v["L0_gnn_W1"].T), "gb": same(v["L0_gnn_b"]),
        "wx": same(v[f + "W_x"]), "wslt": same(np.concatenate([v[f + "W_slice"].T] * 2, 0)), "bx": same(v[f + "b_x"].reshape(HB, P).T),
        "bslice": same(v[f + "b_slice"]), "temp": same(v[f + "temperature"].reshape(HEADS)),
        "outb": same(v[f + "out_b"]), "bm": same(v["L1_gnn_bm"]), "gb1": same(v["L1_gnn_b1"].T), "gb2": same(v["L1_gnn_b2"].T),
        "eps1": same(v["L1_gnn_eps1"]), "eps2": same(v["L1_gnn_eps2"]),
        "lng": same(v["L1_ffn_ln_g"].T), "lnb": same(v["L1_ffn_ln_b"].T),
        "b1": same(v["L1_ffn_b1"].reshape(STEPS, P).T), "wr": same(v["L1_ffn_Wr"]), "br": same(v["L1_ffn_br"]),
        "b2": same(v["L1_ffn_b2"].T),
        "wfxt": same(v[f + "W_fx"].T), "bfx": same(v[f + "b_fx"]), "hin": same(v[f + "hy_in_w"].T), "convw": conv,
        "dtb": same(v[f + "hy_dt_bias"]), "alog": same(v[f + "hy_A_log"]), "hd": same(v[f + "hy_D"]),
        "fcdt": same(v[f + "hy_fcD_w"].T), "hout": same(v[f + "hy_out_w"].T), "outwt": same(v[f + "out_w"].T),
        "normw": same(v[f + "hy_norm_w"].reshape(4, P).T), "x2": same(v["L1_gnn_x2"]),
        "mlpw": same(np.concatenate([v["L1_gnn_W1"].transpose(2, 0, 1), v["L1_gnn_W2"].transpose(2, 0, 1),
                                     v["L1_gnn_Wm"].reshape(D, 2, D).transpose(2, 1, 0)], 1)),
        "m1": same(v["L1_ffn_W1"]),
        "m2": same(v["L1_ffn_W2"].reshape(E, HC, P, D).transpose(0, 2, 1, 3)).reshape(E, P, HC * D),
    }
    nc = bacc.Bacc("TRN2", target_bir_lowering=False, num_devices=1)
    ins = {k: nc.dram_tensor("in_" + k, a.shape, F32, kind="ExternalInput").ap() for k, a in arrays.items()}
    out_t = nc.dram_tensor("out_t", (D, N), F32, kind="ExternalOutput").ap()
    scratch_xn = nc.dram_tensor("scratch_xn", (D, N), F32).ap()
    scratch_w = nc.dram_tensor("scratch_w", (E, N), F32).ap()
    build_network(nc, ins, out_t, scratch_xn, scratch_w)
    result = run_bass_kernel_spmd(nc, [{"in_" + k: a for k, a in arrays.items()}], core_ids=[0])
    return np.ascontiguousarray(result.results[0]["out_t"].T)
```
